# Optimizing a Trainium2 kernel written in Bass

```python
import numpy as np
import jax
import jax.numpy as jnp

def _softmax(x, axis=-1):
    return jax.nn.softmax(x, axis=axis)

def _gelu(x):
    return jax.nn.gelu(x, approximate=True)

def _silu(x):
    return jax.nn.silu(x)

def _sigmoid(x):
    return jax.nn.sigmoid(x)

def _layernorm(x, axis=-1, eps=1e-05):
    m = jnp.mean(x, axis=axis, keepdims=True)
    v = jnp.var(x, axis=axis, keepdims=True)
    return (x - m) / jnp.sqrt(v + eps)

def _scatter_add(tgt, idx, src, axis=0):
    return tgt.at[idx].add(src)

def _segment_sum(src, seg, n):
    return jax.ops.segment_sum(src, seg, n)
kernel_name = 'mk_decoder_postln_d1_seqx_r8_524810'

def setup_inputs(seed: int=0):
    np.random.seed(seed)
    _w = jnp.asarray

    def _rec_inputs():
        import jax
        import jax.numpy as jnp
        _rk = jax.random.key(seed)
        x = -0.0003929 + 0.9999 * jax.random.normal(jax.random.fold_in(_rk, 1), (8, 128, 512), jnp.float32)
        _lenS = 128 - jax.random.randint(jax.random.fold_in(_rk, 7), (8,), 0, max(1, 128 // 4) + 1, jnp.int32)
        _lenS2 = 128 - jax.random.randint(jax.random.fold_in(_rk, 8), (8,), 0, max(1, 128 // 4) + 1, jnp.int32)
        _ctx_4096P = jax.random.normal(jax.random.fold_in(_rk, 11), (8, 16, 512), jnp.float32)
        _ctx_4096c = jax.random.dirichlet(jax.random.fold_in(_rk, 511), 0.3 * jnp.ones((16,), jnp.float32), (8, 128))
        _ctx_4096t = jnp.einsum('bsk,bkd->bsd', _ctx_4096c, _ctx_4096P)
        _ctx_4096t = _ctx_4096t * jax.lax.rsqrt(jnp.mean(jnp.square(_ctx_4096t)) + 1e-12) * 0.953939
        ctx_4096 = 2.81802e-05 + 1.00001 * (_ctx_4096t + 0.3 * jax.random.normal(jax.random.fold_in(_rk, 611), (8, 128, 512), jnp.float32))
        pos_BxS2 = jnp.broadcast_to(jnp.arange(128, dtype=jnp.int32), (8, 128))
        _validS = jnp.arange(128)[None, :] < _lenS[:, None]
        _validS2 = jnp.arange(128)[None, :] < _lenS2[:, None]
        _causal = jnp.tril(jnp.ones((128, 128), dtype=bool))
        mask_BxSxS2_ik0 = jnp.where(jnp.broadcast_to(_validS2[:, None, :], (8, 128, 128)), 0, 1).astype(jnp.int32)
        return (x, ctx_4096, pos_BxS2, mask_BxSxS2_ik0)
    x, ctx_4096, pos_BxS2, mask_BxSxS2_ik0 = _rec_inputs()

    def _L0_attn_setup():
        import jax, jax.numpy as jnp
        import numpy as np
        BATCH, SEQ, HIDDEN = (2, 512, 512)
        HEADS, HEAD_DIM, BLOCK = (32, 128, 32)
        LAYER_IDX, N_LAYERS = (1, 32)
        EPS = 1e-05

        def _decays():
            base = 1.0 / 2.0 ** (8.0 / HEADS)
            exponent = jnp.arange(HEADS, dtype=jnp.float32) + 1.0
            factor = 1.0 - LAYER_IDX / (N_LAYERS - 1 + 1e-05) + 1e-05
            slope = (base ** exponent * factor)[:, None, None]
            r = jnp.arange(BLOCK, dtype=jnp.float32) + 1.0
            q_decay = jnp.exp(-slope * r[:, None])
            k_decay = jnp.exp(-slope * (BLOCK - r)[:, None])
            diff = r[:, None] - r[None, :]
            diag = slope[None] * diff[None, None]
            diag = jnp.where(diag >= 0, -diag, -jnp.inf)
            diag_decay = jnp.exp(diag)
            block_decay = jnp.exp(-slope * BLOCK)
            return (q_decay, k_decay, diag_decay, block_decay)
        key = jax.random.key(seed)
        ks = jax.random.split(key, 5)
        s = 0.02
        return {'hidden_states': jax.random.normal(ks[0], (BATCH, SEQ, HIDDEN), jnp.float32), 'qkv_w': jax.random.normal(ks[1], (3 * HEADS * HEAD_DIM, HIDDEN), jnp.float32) * s, 'out_w': jax.random.normal(ks[2], (HIDDEN, HEADS * HEAD_DIM), jnp.float32) * s, 'gate_w': jax.random.normal(ks[3], (HEADS * HEAD_DIM, HIDDEN), jnp.float32) * s, 'norm_w': jnp.ones((HEADS * HEAD_DIM,), jnp.float32)}
    _L0_attn_all = _L0_attn_setup()
    _L0_attn_in = {k: v for k, v in _L0_attn_all.items() if k in ('qkv_w', 'out_w', 'gate_w', 'norm_w')}
    del _L0_attn_all

    def _L0_xattn_setup():
        import jax, jax.numpy as jnp
        import numpy as np
        B, S, E = (2, 256, 512)
        H, KVH, D = (32, 8, 128)
        GROUPS = H // KVH
        MAX_POS = 512
        ROPE_THETA = 10000.0

        def _rope_tables(max_pos, dim, theta):
            inv_freq = 1.0 / theta ** (jnp.arange(0, dim, 2, dtype=jnp.float32) / dim)
            t = jnp.arange(max_pos, dtype=jnp.float32)
            freqs = jnp.einsum('i,j->ij', t, inv_freq)
            emb = jnp.concatenate([freqs, freqs], axis=-1)
            return (jnp.cos(emb), jnp.sin(emb))

        def _rotate_half(x):
            x1, x2 = (x[..., :x.shape[-1] // 2], x[..., x.shape[-1] // 2:])
            return jnp.concatenate([-x2, x1], axis=-1)
        key = jax.random.key(seed)
        ks = jax.random.split(key, 8)
        scale_w = 1.0 / np.sqrt(E)
        query = jax.random.normal(ks[0], (B, S, E), dtype=jnp.float32)
        k_in = jax.random.normal(ks[1], (B, S, E), dtype=jnp.float32)
        v_in = jax.random.normal(ks[2], (B, S, E), dtype=jnp.float32)
        position_ids = jnp.broadcast_to(jnp.arange(S, dtype=jnp.int64), (B, S))
        src_mask = jnp.tril(jnp.ones((S, S), dtype=jnp.int32))
        src_mask = jnp.broadcast_to(src_mask, (B, S, S))
        Wq = jax.random.normal(ks[3], (E, H * D), dtype=jnp.float32) * scale_w
        Wk = jax.random.normal(ks[4], (E, KVH * D), dtype=jnp.float32) * scale_w
        Wv = jax.random.normal(ks[5], (E, KVH * D), dtype=jnp.float32) * scale_w
        Wo = jax.random.normal(ks[6], (H * D, E), dtype=jnp.float32) * scale_w
        return {'query': query, 'key': k_in, 'value': v_in, 'position_ids': position_ids, 'src_mask': src_mask, 'Wq': Wq, 'Wk': Wk, 'Wv': Wv, 'Wo': Wo}
    _L0_xattn_all = _L0_xattn_setup()
    _L0_xattn_in = {k: v for k, v in _L0_xattn_all.items() if k in ('Wq', 'Wk', 'Wv', 'Wo')}
    del _L0_xattn_all

    def _L0_ffn_setup():
        import jax, jax.numpy as jnp
        import numpy as np
        DIM = 512
        HIDDEN = 1376
        B, S = (4, 256)

        def _qlinear(x, w_int, scale):
            w = w_int.astype(x.dtype) * scale
            return jnp.einsum('bsd,hd->bsh', x, w)
        key = jax.random.key(seed)
        k_x, k_g, k_u, k_d = jax.random.split(key, 4)
        x = jax.random.normal(k_x, (B, S, DIM), dtype=jnp.float32)
        w_gate = jax.random.randint(k_g, (HIDDEN, DIM), -127, 128, dtype=jnp.int32)
        w_up = jax.random.randint(k_u, (HIDDEN, DIM), -127, 128, dtype=jnp.int32)
        w_down = jax.random.randint(k_d, (DIM, HIDDEN), -127, 128, dtype=jnp.int32)
        scale_gate = jnp.float32(0.01)
        scale_up = jnp.float32(0.01)
        scale_down = jnp.float32(0.01)
        return {'x': x, 'w_gate': w_gate, 'w_up': w_up, 'w_down': w_down, 'scale_gate': scale_gate, 'scale_up': scale_up, 'scale_down': scale_down}
    _L0_ffn_all = _L0_ffn_setup()
    _L0_ffn_in = {k: v for k, v in _L0_ffn_all.items() if k in ('w_gate', 'w_up', 'w_down', 'scale_gate', 'scale_up', 'scale_down')}
    del _L0_ffn_all
    return {'x': x, 'ctx_4096': ctx_4096, 'pos_BxS2': pos_BxS2, 'mask_BxSxS2_ik0': mask_BxSxS2_ik0, 'L0_attn_qkv_w': _L0_attn_in['qkv_w'], 'L0_attn_out_w': _L0_attn_in['out_w'], 'L0_attn_gate_w': _L0_attn_in['gate_w'], 'L0_attn_norm_w': _L0_attn_in['norm_w'], 'L0_xattn_Wq': _L0_xattn_in['Wq'], 'L0_xattn_Wk': _L0_xattn_in['Wk'], 'L0_xattn_Wv': _L0_xattn_in['Wv'], 'L0_xattn_Wo': _L0_xattn_in['Wo'], 'L0_ffn_w_gate': _L0_ffn_in['w_gate'], 'L0_ffn_w_up': _L0_ffn_in['w_up'], 'L0_ffn_w_down': _L0_ffn_in['w_down'], 'L0_ffn_scale_gate': _L0_ffn_in['scale_gate'], 'L0_ffn_scale_up': _L0_ffn_in['scale_up'], 'L0_ffn_scale_down': _L0_ffn_in['scale_down']}

def reference(x, ctx_4096, pos_BxS2, mask_BxSxS2_ik0, L0_attn_qkv_w, L0_attn_out_w, L0_attn_gate_w, L0_attn_norm_w, L0_xattn_Wq, L0_xattn_Wk, L0_xattn_Wv, L0_xattn_Wo, L0_ffn_w_gate, L0_ffn_w_up, L0_ffn_w_down, L0_ffn_scale_gate, L0_ffn_scale_up, L0_ffn_scale_down):
    import jax
    import jax.numpy as jnp

    def _L0_attn_ref(hidden_states, qkv_w, out_w, gate_w, norm_w):
        import jax, jax.numpy as jnp
        import numpy as np
        BATCH, SEQ, HIDDEN = (2, 512, 512)
        HEADS, HEAD_DIM, BLOCK = (32, 128, 32)
        LAYER_IDX, N_LAYERS = (1, 32)
        EPS = 1e-05

        def _decays():
            base = 1.0 / 2.0 ** (8.0 / HEADS)
            exponent = jnp.arange(HEADS, dtype=jnp.float32) + 1.0
            factor = 1.0 - LAYER_IDX / (N_LAYERS - 1 + 1e-05) + 1e-05
            slope = (base ** exponent * factor)[:, None, None]
            r = jnp.arange(BLOCK, dtype=jnp.float32) + 1.0
            q_decay = jnp.exp(-slope * r[:, None])
            k_decay = jnp.exp(-slope * (BLOCK - r)[:, None])
            diff = r[:, None] - r[None, :]
            diag = slope[None] * diff[None, None]
            diag = jnp.where(diag >= 0, -diag, -jnp.inf)
            diag_decay = jnp.exp(diag)
            block_decay = jnp.exp(-slope * BLOCK)
            return (q_decay, k_decay, diag_decay, block_decay)
        b, s, _ = hidden_states.shape
        h, d, bs = (HEADS, HEAD_DIM, BLOCK)
        nb = s // bs
        q_decay, k_decay, diag_decay, block_decay = _decays()
        qkv = jax.nn.silu(hidden_states @ qkv_w.T)
        qkv = qkv.reshape(b, s, h, 3, d)
        q = jnp.moveaxis(qkv[:, :, :, 0], 2, 1)
        k = jnp.moveaxis(qkv[:, :, :, 1], 2, 1)
        v = jnp.moveaxis(qkv[:, :, :, 2], 2, 1)

        def to_blocks(x):
            return jnp.moveaxis(x.reshape(b, h, nb, bs, d), 2, 0)
        qb, kb, vb = (to_blocks(q), to_blocks(k), to_blocks(v))

        def step(kv, blk):
            cq, ck, cv = blk
            scores = jnp.einsum('bhnd,bhmd->bhnm', cq, ck) * diag_decay
            intra = jnp.einsum('bhnm,bhmd->bhnd', scores, cv)
            inter = jnp.einsum('bhnd,bhde->bhne', cq * q_decay, kv)
            kv_next = kv * block_decay + jnp.einsum('bhnd,bhne->bhde', ck * k_decay, cv)
            return (kv_next, intra + inter)
        kv0 = jnp.zeros((b, h, d, d), hidden_states.dtype)
        _, out_blocks = jax.lax.scan(step, kv0, (qb, kb, vb))
        attn = jnp.moveaxis(out_blocks, 0, 2)
        attn = attn.reshape(b, h, s, d).transpose(0, 2, 1, 3).reshape(b, s, h * d)
        xf = attn.astype(jnp.float32)
        xf = xf * jax.lax.rsqrt(jnp.mean(xf * xf, axis=-1, keepdims=True) + EPS)
        normed = norm_w * xf.astype(attn.dtype)
        gate = jax.nn.sigmoid(hidden_states @ gate_w.T)
        return gate * normed @ out_w.T

    def _L0_xattn_ref(query, key, value, position_ids, src_mask, Wq, Wk, Wv, Wo):
        import jax, jax.numpy as jnp
        import numpy as np
        B, S, E = (2, 256, 512)
        H, KVH, D = (32, 8, 128)
        GROUPS = H // KVH
        MAX_POS = 512
        ROPE_THETA = 10000.0

        def _rope_tables(max_pos, dim, theta):
            inv_freq = 1.0 / theta ** (jnp.arange(0, dim, 2, dtype=jnp.float32) / dim)
            t = jnp.arange(max_pos, dtype=jnp.float32)
            freqs = jnp.einsum('i,j->ij', t, inv_freq)
            emb = jnp.concatenate([freqs, freqs], axis=-1)
            return (jnp.cos(emb), jnp.sin(emb))

        def _rotate_half(x):
            x1, x2 = (x[..., :x.shape[-1] // 2], x[..., x.shape[-1] // 2:])
            return jnp.concatenate([-x2, x1], axis=-1)
        nb, q_len, _ = query.shape
        q = (query @ Wq).reshape(nb, q_len, H, D).transpose(0, 2, 1, 3)
        k = (key @ Wk).reshape(nb, q_len, KVH, D).transpose(0, 2, 1, 3)
        v = (value @ Wv).reshape(nb, q_len, KVH, D).transpose(0, 2, 1, 3)
        cos_t, sin_t = _rope_tables(MAX_POS, D, ROPE_THETA)
        cos = cos_t[position_ids][:, None]
        sin = sin_t[position_ids][:, None]
        q = q * cos + _rotate_half(q) * sin
        k = k * cos + _rotate_half(k) * sin
        k = jnp.repeat(k, GROUPS, axis=1)
        v = jnp.repeat(v, GROUPS, axis=1)
        scores = jnp.einsum('bhqd,bhkd->bhqk', q, k) / jnp.sqrt(jnp.float32(D))
        mask = src_mask[:, None]
        scores = jnp.where(mask == 0, jnp.float32(-1000000000.0), scores)
        attn = jax.nn.softmax(scores, axis=-1)
        x = jnp.einsum('bhqk,bhkd->bhqd', attn, v)
        x = x.transpose(0, 2, 1, 3).reshape(nb, q_len, H * D)
        return x @ Wo

    def _L0_ffn_ref(x, w_gate, w_up, w_down, scale_gate, scale_up, scale_down):
        import jax, jax.numpy as jnp
        import numpy as np
        DIM = 512
        HIDDEN = 1376
        B, S = (4, 256)

        def _qlinear(x, w_int, scale):
            w = w_int.astype(x.dtype) * scale
            return jnp.einsum('bsd,hd->bsh', x, w)
        x_gate = _qlinear(x, w_gate, scale_gate)
        x_up = _qlinear(x, w_up, scale_up)
        x_mid = jax.nn.silu(x_gate) * x_up
        x_out = _qlinear(x_mid, w_down, scale_down)
        return x_out
    x = _layernorm(x + _L0_attn_ref(x, L0_attn_qkv_w, L0_attn_out_w, L0_attn_gate_w, L0_attn_norm_w), axis=-1)
    x = _layernorm(x + _L0_xattn_ref(x, ctx_4096, ctx_4096, pos_BxS2, mask_BxSxS2_ik0, L0_xattn_Wq, L0_xattn_Wk, L0_xattn_Wv, L0_xattn_Wo), axis=-1)
    x = _layernorm(x + _L0_ffn_ref(x, L0_ffn_w_gate, L0_ffn_w_up, L0_ffn_w_down, L0_ffn_scale_gate, L0_ffn_scale_up, L0_ffn_scale_down), axis=-1)
    return x

_drawn_inputs = setup_inputs


def setup_inputs(seed=0):
    import zlib

    import numpy as np

    out = dict(_drawn_inputs(seed))
    spreads = {'L0_attn_norm_w': (1.0, 0.2)}
    factors = {}
    for name, (base, spread) in spreads.items():
        noise = np.random.default_rng([zlib.crc32(name.encode()), seed]).standard_normal(out[name].shape)
        drawn = base * np.exp(spread * noise) if base else spread * noise
        out[name] = jnp.asarray(drawn.astype(out[name].dtype))
    for name, factor in factors.items():
        out[name] = (out[name] * factor).astype(out[name].dtype)
    return out
```

```python
import numpy as np

import concourse.bass as bass
from concourse import mybir

FP32 = mybir.dt.float32
FP32R = mybir.dt.float32r
INT32 = mybir.dt.int32
ALU = mybir.AluOpType
ACT = mybir.ActivationFunctionType
AX = mybir.AxisListType

P = 128
BATCH, SEQ, DIM = 8, 128, 512
TOK = BATCH * SEQ
KC = DIM // P
HEADS = 32
PAIRS = HEADS // 2
KV_HEADS = 8
GROUP = HEADS // KV_HEADS
HIDDEN = 1376
HCHUNKS = -(-HIDDEN // P)
POSITIONS = 512
ROPE_THETA = 10000.0
LN_EPS = 1e-5
RMS_EPS = 1e-5
SM_SCALE = float(1.0 / np.sqrt(np.float32(P)))
MASKED = float(-1e9 * np.sqrt(np.float32(P)))
UNMASKED = 3.0e38
HALF = TOK // 2
RING = 5
RING_F = 3


UNITS_PAIR, JOBS_PAIR = 10, 12
U_FRONT0, U_LOOP_A = 0, 4
J_ROPE = 0
J_FRONT0 = 2
J_LOOP_A = J_FRONT0 + 4
J_END_A = J_LOOP_A + JOBS_PAIR * (PAIRS - 1) + 8
U_B = U_LOOP_A + UNITS_PAIR * (PAIRS - 1) + 6
J_K0, J_V0, J_LN1, J_Q0 = J_END_A, J_END_A + 1, J_END_A + 2, J_END_A + 6
J_Q1, J_T0, J_Q2, J_T1 = J_Q0 + 1, J_Q0 + 2, J_Q0 + 3, J_Q0 + 4
J_LOOP_B = J_T1 + 1
UNITS_KV, JOBS_KV = 10, 18
U_LOOP_B = U_B + 5
ROPES_KV, R_LOOP_B = 5, 4
J_LAST_B = J_LOOP_B + JOBS_KV * (KV_HEADS - 1)
J_TAIL_B = J_LAST_B + 7
J_LN2 = J_TAIL_B + 4
U_F = U_LOOP_B + UNITS_KV * (KV_HEADS - 1) + 5
J_F0 = J_LN2 + 4
J_LOOP_F = J_F0 + 2
UNITS_F, JOBS_F = 3, 6
J_TAIL_F = J_LOOP_F + JOBS_F * (HCHUNKS - 1)
UF_LOOP = 2
UF_TOTAL = UF_LOOP + UNITS_F * (HCHUNKS - 1) + 1


def at(base, per, i, j):
    return i * per + (base + j)


def job(base, per, i, j):
    return (base + j) % 2, i * (per // 2) + (base + j) // 2, at(base, per, i, j)


def build(nc, x_t, x_rows, ctx_t, pos, mask, weights, ffn_weights, ffn_scales, norm_w, decay, rope_table,
          consts, out):
    place_at = [(nc.sbuf_base + 31) // 32 * 32]

    def sb(name, shape, dtype=FP32, offset=None):
        size = 4 * int(np.prod(shape[1:]))
        if offset is None:
            offset = place_at[0]
            place_at[0] += (size + 31) // 32 * 32
            offsets[name] = offset
        return nc.alloc_sbuf_tensor_at(name, shape, dtype, offset=offset)

    offsets = {}
    xt_hi = sb("xt_hi", [P, KC, TOK], FP32R)
    xt_lo = sb("xt_lo", [P, KC, TOK], FP32R)
    ctx_hi = sb("ctx_hi", [P, KC, TOK], FP32R)
    ctx_lo = sb("ctx_lo", [P, KC, TOK], FP32R)
    acc = sb("acc", [P, BATCH, DIM])
    raw = sb("raw", [P, RING, DIM])
    w_hi = sb("w_hi", [P, RING, DIM], FP32R)
    w_lo = sb("w_lo", [P, RING, DIM], FP32R)
    q_sb = sb("q_sb", [P, TOK])
    k_sb = sb("k_sb", [P, TOK])
    v_sb = sb("v_sb", [P, BATCH, 2 * P])
    gate = sb("gate", [P, TOK])
    probs = sb("probs", [P, BATCH, P])
    y_raw = sb("y_raw", [P, TOK])
    squares = sb("squares", [P, TOK])
    sq_sum = sb("sq_sum", [P, TOK])
    y_hi = sb("y_hi", [P, 2, TOK], FP32R)
    y_lo = sb("y_lo", [P, 2, TOK], FP32R)
    decay_sb = sb("decay_sb", [P, HEADS, P])
    cos_t = sb("cos_t", [P, TOK])
    sin_t = sb("sin_t", [P, TOK])
    cap = sb("cap", [P, BATCH, P])
    nw = sb("nw", [P, HEADS])
    scales = sb("scales", [P, 3])
    cst = sb("cst", [P, P + 5])
    stats = sb("stats", [P, BATCH, 6])
    mean_var = sb("mean_var", [P, BATCH, 2])
    var_e = sb("var_e", [P, BATCH])
    std = sb("std", [P, BATCH])
    rstd = sb("rstd", [P, BATCH])
    newton = sb("newton", [P, BATCH])
    cosed = sb("cosed", [P, TOK])
    row_max = sb("row_max", [P, BATCH])
    neg_max = sb("neg_max", [P, BATCH])
    row_sum = sb("row_sum", [P, BATCH])
    row_inv = sb("row_inv", [P, BATCH])
    assert place_at[0] <= nc.sbuf_usable_end
    ident, iota, ones = cst[:, 0:P], cst[:, P:P + 4], cst[:, P + 4:P + 5]
    x_raw = sb("x_raw", [P, KC, TOK], offset=offsets["q_sb"])
    ctx_raw = sb("ctx_raw", [P, KC, TOK], offset=offsets["acc"])
    onehot = sb("onehot", [P, 4, TOK], offset=offsets["decay_sb"])
    pos_i = sb("pos_i", [P, TOK], INT32, offset=offsets["gate"])
    pos_wrap = sb("pos_wrap", [P, TOK], offset=offsets["probs"])
    pos_f = sb("pos_f", [P, TOK], offset=offsets["y_raw"])
    table = sb("table", [P, 4, 2 * P], offset=offsets["squares"])
    mask_i = sb("mask_i", [P, BATCH, P], INT32, offset=offsets["y_hi"])
    mask_tmp = sb("mask_tmp", [P, BATCH, P], offset=offsets["y_lo"])
    x_res = sb("x_res", [P, BATCH, DIM], offset=offsets["xt_lo"])
    qr = sb("qr", [P, TOK], offset=offsets["q_sb"])
    pb = sb("pb", [P, BATCH, P], offset=offsets["k_sb"])
    rot = sb("rot", [P, TOK], offset=offsets["v_sb"])
    pt = sb("pt", [P, BATCH, P], offset=offsets["v_sb"] + 4 * TOK)
    kr = sb("kr", [P, TOK], offset=offsets["gate"])
    vx = sb("vx", [P, BATCH, P], offset=offsets["probs"])
    swapped = sb("swapped", [P, TOK], offset=offsets["y_raw"])
    vt = sb("vt", [P, TOK], offset=offsets["squares"])
    g_act = sb("g_act", [P, TOK], offset=offsets["q_sb"])
    mid = sb("mid", [P, TOK], offset=offsets["k_sb"])

    proj = [nc.alloc_psum_tensor(f"proj{s}", [P, TOK], FP32) for s in range(2)]
    ps_s = nc.alloc_psum_tensor("ps_s", [P, TOK], FP32)
    ps_o = nc.alloc_psum_tensor("ps_o", [P, TOK], FP32)

    sem = nc.alloc_semaphore
    tables_in = sem("tables_in")
    pos_in = sem("pos_in")
    mask_in = sem("mask_in")
    x_in = [sem(f"x_in{k}") for k in range(KC)]
    ctx_in = [sem(f"ctx_in{k}") for k in range(KC)]
    small_in = sem("small_in")
    decay_in = sem("decay_in")
    res_in = sem("res_in")
    raw_in = [sem(f"raw_in{s}") for s in range(RING)]
    rawf_in = [sem(f"rawf_in{s}") for s in range(RING_F)]
    stored = sem("stored")
    w_hi_done = sem("w_hi_done")
    w_lo_done = sem("w_lo_done")
    w_ffn_done = sem("w_ffn_done")
    onehot_done = sem("onehot_done")
    in_hi_done = sem("in_hi_done")
    in_lo_done = sem("in_lo_done")
    acc_zeroed = sem("acc_zeroed")
    jobs_done = sem("jobs_done")
    evacuated = [sem(f"evacuated{s}") for s in range(2)]
    scores_done = sem("scores_done")
    probs_done = sem("probs_done")
    pv_done = sem("pv_done")
    gate_done = sem("gate_done")
    squares_done = sem("squares_done")
    sq_sum_done = sem("sq_sum_done")
    y_done = sem("y_done")
    y_hi_done = sem("y_hi_done")
    y_lo_done = sem("y_lo_done")
    ms_done = sem("ms_done")
    var_done = sem("var_done")
    std_done = sem("std_done")
    rms_done = sem("rms_done")
    normed = sem("normed")
    xt_hi_done = sem("xt_hi_done")
    swap_done = sem("swap_done")
    sin_done = sem("sin_done")
    rope_done = sem("rope_done")
    masked = sem("masked")
    max_done = sem("max_done")
    neg_max_done = sem("neg_max_done")
    exp_done = sem("exp_done")
    inv_done = sem("inv_done")
    soft_done = sem("soft_done")
    vt_turned = sem("vt_turned")
    v_ready = sem("v_ready")
    dve_step = sem("dve_step")

    def bank_view(tensor, n):
        return tensor[:, :].rearrange("p (b n) -> p b n", n=n)

    def wait_job(eng, n):
        eng.wait_ge(jobs_done, n + 1)

    def wait_out_of_slot(eng, j):
        eng.wait_ge(evacuated[j[0]], j[1] + 1)

    def wait_all_out(eng, n):
        for s in range(2):
            eng.wait_ge(evacuated[s], (n + 1 - s) // 2)

    def one_job(n):
        return n % 2, n // 2, n

    def turned_view(s, c):
        return proj[s][:, c * DIM:(c + 1) * DIM].rearrange("p (k t) -> p k t", k=KC)

    with nc.Block() as block:

        @block.sync
        def _(sp):
            sp.dma_start(cst[:, :], consts).then_inc(tables_in, 16)
            sp.dma_start(pos_i[:, :], pos.partition_broadcast(P)).then_inc(pos_in, 16)
            sp.dma_start(table[:, :, :], rope_table).then_inc(tables_in, 16)

            def load_unit(unit, slot, lo_before):
                if lo_before is not None:
                    sp.wait_ge(w_lo_done, lo_before)
                sp.dma_start(raw[:, slot, :], weights[unit, :, :].squeeze(0)).then_inc(raw_in[slot], 16)

            for k in range(KC):
                sp.dma_start(x_raw[:, k, :], x_t[:, k, :]).then_inc(x_in[k], 16)
            for n in range(RING):
                load_unit(slice(n, n + 1), n, None)
            sp.dma_start(nw[:, :], norm_w).then_inc(small_in, 16)
            sp.dma_start(scales[:, :], ffn_scales).then_inc(small_in, 16)
            wait_job(sp, J_ROPE + 1)
            sp.dma_start(decay_sb[:, :, :], decay).then_inc(decay_in, 16)
            for k in range(KC):
                sp.dma_start(ctx_raw[:, k, :], ctx_t[:, k, :]).then_inc(ctx_in[k], 16)
            sp.dma_start(mask_i[:, :, :], mask).then_inc(mask_in, 16)
            with sp.Fori(1, U_F // RING) as r:
                for s in range(RING):
                    load_unit(bass.ds(r * RING + s, 1), s, r * RING + (s + 1 - RING))
            ffn_i = raw[:, :, :].bitcast(INT32)
            sp.wait_ge(w_lo_done, U_F)
            for m in range(RING_F):
                sp.dma_start(ffn_i[:, m, :], ffn_weights[m, :, :]).then_inc(rawf_in[m], 16)
            with sp.Fori(1, UF_TOTAL // RING_F) as r:
                for s in range(RING_F):
                    sp.wait_ge(w_lo_done, r * RING_F + (U_F - RING_F + s + 1))
                    sp.dma_start(ffn_i[:, s, :], ffn_weights[bass.ds(r * RING_F + s, 1), :, :].squeeze(0))\
                        .then_inc(rawf_in[s], 16)
            for c in range(BATCH):
                sp.wait_ge(normed, 2 * BATCH + c + 1)
                sp.dma_start(out[c, :, :], acc[:, c, :]).then_inc(stored, 16)
            sp.wait_ge(stored, 16 * BATCH)

        @block.gpsimd
        def _(pool):
            def lo_of_unit(n, s):
                pool.wait_ge(w_hi_done, n + 1)
                nc.gpsimd.tensor_tensor(w_lo[:, s, :], raw[:, s, :], w_hi[:, s, :].bitcast(FP32),
                                        ALU.subtract).then_inc(w_lo_done, 1)

            def add_squares(h):
                pool.wait_ge(squares_done, h + 1)
                pool.wait_ge(sq_sum_done, h + 1)
                nc.gpsimd.tensor_tensor(sq_sum[:, :], sq_sum[:, :], squares[:, :], ALU.add)\
                    .then_inc(sq_sum_done, 1)

            nc.gpsimd.memset(sq_sum[:, :], 0.0).then_inc(sq_sum_done, 1)
            for n in range(U_LOOP_A + RING):
                lo_of_unit(n, n % RING)

            def pair(i, last):
                def lo(j):
                    lo_of_unit(at(U_LOOP_A + RING + j, UNITS_PAIR, i, 0), (U_LOOP_A + RING + j) % RING)
                lo(0)
                add_squares(i * 2)
                for j in range(1, 4):
                    lo(j)
                add_squares(i * 2 + 1)
                for j in range(4, 6 if last else UNITS_PAIR):
                    lo(j)

            with pool.Fori(0, PAIRS - 1) as i:
                pair(i, False)
            pair(PAIRS - 1, True)
            with pool.Fori(U_LOOP_B // RING, U_F // RING) as r:
                for s in range(RING):
                    lo_of_unit(r * RING + s, s)

            with pool.Fori(0, UF_TOTAL // RING_F) as r:
                for s in range(RING_F):
                    lo_of_unit(r * RING_F + (U_F + s), s)

        @block.scalar
        def _(act):
            def hi_of_unit(n, loads):
                s = n[0]
                act.wait_ge(raw_in[s], loads * 16)
                nc.scalar.activation(w_hi[:, s, :], raw[:, s, :], ACT.Copy).then_inc(w_hi_done, 1)

            def pair_unit(i, j):
                n = U_LOOP_A + j
                hi_of_unit((n % RING,), i * (UNITS_PAIR // RING) + (n // RING + 1))

            def kv_unit(i, j):
                n = U_LOOP_B + j
                hi_of_unit((n % RING,), i * (UNITS_KV // RING) + (n // RING + 1))

            for k in range(KC):
                act.wait_ge(x_in[k], 16)
                nc.scalar.activation(xt_hi[:, k, :], x_raw[:, k, :], ACT.Copy).then_inc(in_hi_done, 1)
            for n in range(RING):
                hi_of_unit((n,), 1)
            for n, dst in enumerate((cos_t, sin_t)):
                wait_job(act, J_ROPE + n)
                nc.scalar.activation(dst[:, :], proj[n][:, :], ACT.Copy).then_inc(evacuated[n], 1)
            for k in range(KC):
                act.wait_ge(ctx_in[k], 16)
                nc.scalar.activation(ctx_hi[:, k, :], ctx_raw[:, k, :], ACT.Copy).then_inc(in_hi_done, 1)

            def silu_v(jb, half, free):
                wait_job(act, jb[2])
                if free is not None:
                    act.wait_ge(pv_done, free)
                nc.scalar.activation(v_sb[:, 4 * half:4 * half + 4, :], bank_view(proj[jb[0]], 2 * P), ACT.Silu)\
                    .then_inc(evacuated[jb[0]], 1)

            def silu_head(dst, jb, free):
                wait_job(act, jb[2])
                if free is not None:
                    act.wait_ge(scores_done, free)
                nc.scalar.activation(dst[:, :], proj[jb[0]][:, :], ACT.Silu).then_inc(evacuated[jb[0]], 1)

            def tanh_gate(jb, free):
                wait_job(act, jb[2])
                if free is not None:
                    act.wait_ge(y_done, free)
                nc.scalar.activation(gate[:, :], proj[jb[0]][:, :], ACT.Tanh, scale=0.5)\
                    .then_inc(evacuated[jb[0]], 1)

            def square(h):
                act.wait_ge(pv_done, h + 1)
                act.wait_ge(sq_sum_done, h + 1)
                nc.scalar.activation(squares[:, :], ps_o[:, :], ACT.Square).then_inc(squares_done, 1)

            def y_hi_of(h, hd, before):
                act.wait_ge(y_done, h + 1)
                if before is not None:
                    wait_job(act, before)
                nc.scalar.activation(y_hi[:, hd, :], y_raw[:, :], ACT.Copy).then_inc(y_hi_done, 1)

            def back(i):
                jb = [job(J_LOOP_A, JOBS_PAIR, i, j) for j in range(4)]
                silu_head(q_sb, jb[0], i * 2 + 1)
                pair_unit(i, 5)
                square(i * 2)
                silu_head(k_sb, jb[1], i * 2 + 1)
                pair_unit(i, 6)
                tanh_gate(jb[2], at(0, 2, i, 0) if not isinstance(i, int) or i else None)
                pair_unit(i, 7)
                y_hi_of(i * 2, 0, at(J_LOOP_A, JOBS_PAIR, i, -1))
                tanh_gate(jb[3], i * 2 + 1)
                pair_unit(i, 8)
                square(i * 2 + 1)
                y_hi_of(i * 2 + 1, 1, None)

            silu_v(one_job(J_FRONT0), 0, None)
            silu_v(one_job(J_FRONT0 + 1), 1, None)
            pair_unit(0, 1)
            pair_unit(0, 2)
            silu_head(q_sb, one_job(J_FRONT0 + 2), None)
            pair_unit(0, 3)
            silu_head(k_sb, one_job(J_FRONT0 + 3), None)
            pair_unit(0, 4)
            with act.Fori(0, PAIRS - 1) as i:
                back(i)
                jb = [job(J_LOOP_A, JOBS_PAIR, i, j) for j in range(JOBS_PAIR)]
                silu_v(jb[4], 0, i * 2 + 2)
                silu_v(jb[5], 1, None)
                pair_unit(i, 9)
                pair_unit(i, 10)
                silu_head(q_sb, jb[6], i * 2 + 2)
                pair_unit(i, 11)
                silu_head(k_sb, jb[7], None)
                pair_unit(i, 12)
                wait_job(act, jb[11][2])
                pair_unit(i, 13)
                pair_unit(i, 14)
            back(PAIRS - 1)
            act.dma_start(x_res[:, :, :], x_rows).then_inc(res_in, 16)
            wait_job(act, J_END_A - 1)
            pair_unit(PAIRS - 1, 9)
            pair_unit(PAIRS - 1, 10)

            def sqrt_var(n):
                act.wait_ge(var_done, n + 1)
                nc.scalar.activation(std[:, :], var_e[:, :], ACT.Sqrt).then_inc(std_done, 1)

            def turned_hi(jobs):
                for c2 in range(BATCH // 2):
                    s, _, n = one_job(jobs + c2)
                    wait_job(act, n)
                    for c in range(2):
                        tok = slice((2 * c2 + c) * P, (2 * c2 + c + 1) * P)
                        last = nc.scalar.activation(xt_hi[:, :, tok], turned_view(s, c), ACT.Copy)
                    last.then_inc(xt_hi_done, 1)

            def copy_vt(jb, free):
                wait_job(act, jb[2])
                if free is not None:
                    act.wait_ge(vt_turned, free)
                nc.scalar.activation(vt[:, :], proj[jb[0]][:, :], ACT.Copy).then_inc(evacuated[jb[0]], 1)

            def copy_v(i):
                act.wait_ge(vt_turned, i + 1)
                nc.scalar.activation(vx[:, :, :], bank_view(ps_o, P), ACT.Copy).then_inc(v_ready, 1)

            def swap_halves(jb, free):
                wait_job(act, jb[2])
                if free is not None:
                    act.wait_ge(sin_done, free)
                nc.scalar.activation(swapped[0:64, :], proj[jb[0]][64:128, :], ACT.Copy)
                nc.scalar.activation(swapped[64:128, :], proj[jb[0]][0:64, :], ACT.Copy).then_inc(swap_done, 1)

            def exps(h):
                act.wait_ge(neg_max_done, h + 1)
                for b in range(BATCH):
                    last = nc.scalar.activation(pb[:, b, :], pb[:, b, :], ACT.Exp, bias=neg_max[:, b:b + 1],
                                                scale=SM_SCALE, accum_out=row_sum[:, b:b + 1])
                last.then_inc(exp_done, 1)

            def y_hi_cross(h, hd, before):
                act.wait_ge(pv_done, h + (HEADS + 1))
                if before is not None:
                    wait_job(act, before)
                nc.scalar.activation(y_hi[:, hd, :], ps_o[:, :], ACT.Copy).then_inc(y_hi_done, 1)

            def copy_pt(h, jb):
                wait_job(act, jb[2])
                act.wait_ge(pv_done, h + HEADS)
                nc.scalar.activation(pt[:, :, :], bank_view(proj[jb[0]], P), ACT.Copy)\
                    .then_inc(evacuated[jb[0]], 1)

            sqrt_var(0)
            act.wait_ge(y_lo_done, HEADS)
            act.wait_ge(sq_sum_done, HEADS + 1)
            swap_halves(one_job(J_K0), None)
            kv_unit(0, 0)
            copy_vt(one_job(J_V0), None)
            kv_unit(0, 1)
            sqrt_var(1)
            copy_v(0)
            turned_hi(J_LN1)
            swap_halves(one_job(J_Q0), 1)
            kv_unit(0, 2)
            exps(0)
            swap_halves(one_job(J_Q1), 2)
            kv_unit(0, 3)
            copy_pt(0, one_job(J_T0))
            exps(1)
            swap_halves(one_job(J_Q2), 3)
            kv_unit(0, 4)
            y_hi_cross(0, 0, None)
            copy_pt(1, one_job(J_T1))

            def heads_2_3(i, last):
                g = i * GROUP
                r = at(R_LOOP_B, ROPES_KV, i, 0)
                jb = [job(J_LOOP_B, JOBS_KV, i, j) for j in range(9)]
                q3, kn, t2, q0, o3, t3 = (jb[0], None, jb[1], None, jb[5], jb[6]) if last else \
                    (jb[0], jb[1], jb[2], jb[3], jb[7], jb[8])
                exps(g + 2)
                swap_halves(q3, r)
                if not last:
                    kv_unit(i, 5)
                y_hi_cross(g + 1, 1, None)
                if not last:
                    swap_halves(kn, r + 1)
                    kv_unit(i, 6)
                copy_pt(g + 2, t2)
                exps(g + 3)
                if not last:
                    swap_halves(q0, r + 2)
                    kv_unit(i, 7)
                y_hi_cross(g + 2, 0, o3[2])
                if not last:
                    kv_unit(i, 8)
                    kv_unit(i, 9)
                copy_pt(g + 3, t3)

            with act.Fori(0, KV_HEADS - 1) as i:
                heads_2_3(i, False)
                g = i * GROUP
                r = at(R_LOOP_B, ROPES_KV, i, 3)
                jb = [job(J_LOOP_B, JOBS_KV, i, j) for j in range(JOBS_KV)]
                exps(g + 4)
                swap_halves(jb[9], r)
                kv_unit(i, 10)
                y_hi_cross(g + 3, 1, None)
                copy_vt(jb[10], i + 1)
                kv_unit(i, 11)
                copy_pt(g + 4, jb[11])
                copy_v(i + 1)
                exps(g + 5)
                swap_halves(jb[12], r + 1)
                kv_unit(i, 12)
                y_hi_cross(g + 4, 0, jb[16][2])
                kv_unit(i, 13)
                kv_unit(i, 14)
                copy_pt(g + 5, jb[17])
            heads_2_3(KV_HEADS - 1, True)
            y_hi_cross(HEADS - 1, 1, None)

            def ffn_unit(i, j, which):
                n = UF_LOOP + j
                s = n % RING_F
                act.wait_ge(rawf_in[s], i * 16 + 16 * (n // RING_F + 1))
                nc.scalar.activation(raw[:, s, :], raw[:, s, :].bitcast(INT32), ACT.Copy,
                                     scale=scales[:, which:which + 1]).then_inc(w_ffn_done, 1)
                act.wait_ge(w_ffn_done, i * UNITS_F + (n + 1))
                nc.scalar.activation(w_hi[:, s, :], raw[:, s, :], ACT.Copy).then_inc(w_hi_done, 1)

            def silu_gate(jb, free):
                wait_job(act, jb[2])
                if free is not None:
                    wait_out_of_slot(act, free)
                nc.scalar.activation(g_act[:, :], proj[jb[0]][:, :], ACT.Silu).then_inc(evacuated[jb[0]], 1)

            def mid_hi(jb, before):
                wait_out_of_slot(act, jb)
                wait_job(act, before)
                nc.scalar.activation(y_hi[:, 0, :], mid[:, :], ACT.Copy).then_inc(y_hi_done, 1)

            act.wait_ge(small_in, 32)
            wait_job(act, J_LN2 - 1)
            for j, which in ((-2, 0), (-1, 1), (0, 0)):
                ffn_unit(0, j, which)
            sqrt_var(2)
            turned_hi(J_LN2)
            silu_gate(one_job(J_F0), None)
            ffn_unit(0, 1, 1)
            mid_hi(one_job(J_F0 + 1), J_LN2 - 1)
            ffn_unit(0, 2, 2)

            def chunk(i, last):
                jb = [job(J_LOOP_F, JOBS_F, i, j) for j in range(-3, JOBS_F)]
                up_before, gate_job, up_job, down_last = job(J_LOOP_F, JOBS_F, i, -1 - 2), jb[3], jb[6], jb[8]
                if isinstance(i, int) and i == 0:
                    up_before = one_job(J_F0 + 1)
                silu_gate(gate_job, up_before)
                ffn_unit(i, 3, 2 if last else 0)
                wait_job(act, up_job[2])
                if not last:
                    ffn_unit(i, 4, 1)
                mid_hi(up_job, down_last[2])
                if not last:
                    ffn_unit(i, 5, 2)

            chunk(0, False)
            with act.Fori(1, HCHUNKS - 2) as i:
                chunk(i, False)
            chunk(HCHUNKS - 2, True)
            sqrt_var(3)

        @block.vector
        def _(dve):
            steps = [0]

            def link(ins):
                steps[0] += 1
                ins.then_inc(dve_step, 1)
                dve.wait_ge(dve_step, steps[0])

            dve.wait_ge(pos_in, 16)
            link(nc.vector.tensor_scalar(pos_wrap[:, :], pos_i[:, :], 0.0, float(POSITIONS), ALU.is_lt, ALU.mult))
            link(nc.vector.tensor_tensor(pos_f[:, :], pos_i[:, :], pos_wrap[:, :], ALU.add))
            link(nc.vector.tensor_scalar(pos_f[:, :], pos_f[:, :], 0.0, float(POSITIONS - 1), ALU.max, ALU.min))
            dve.wait_ge(tables_in, 32)
            for c in range(4):
                nc.vector.tensor_scalar(onehot[:, c, :], pos_f[:, :], iota[:, c:c + 1], None, ALU.is_equal)\
                    .then_inc(onehot_done, 1)
            for k in range(KC):
                dve.wait_ge(in_hi_done, k + 1)
                nc.vector.tensor_tensor(xt_lo[:, k, :], x_raw[:, k, :], xt_hi[:, k, :].bitcast(FP32), ALU.subtract)\
                    .then_inc(in_lo_done, 1)
            for k in range(KC):
                dve.wait_ge(in_hi_done, KC + k + 1)
                nc.vector.tensor_tensor(ctx_lo[:, k, :], ctx_raw[:, k, :], ctx_hi[:, k, :].bitcast(FP32), ALU.subtract)\
                    .then_inc(in_lo_done, 1)
            dve.wait_ge(in_lo_done, 2 * KC)
            nc.vector.memset(acc[:, :, :], 0.0).then_inc(acc_zeroed, 1)
            dve.wait_ge(mask_in, 16)
            link(nc.vector.tensor_scalar(mask_tmp[:, :, :], mask_i[:, :, :], 0.0, MASKED, ALU.is_equal, ALU.mult))
            link(nc.vector.tensor_scalar(cap[:, :, :], mask_i[:, :, :], 0.0, UNMASKED, ALU.not_equal, ALU.mult))
            link(nc.vector.tensor_tensor(cap[:, :, :], cap[:, :, :], mask_tmp[:, :, :], ALU.add))
            dve.wait_ge(acc_zeroed, 1)
            dve.wait_ge(decay_in, 16)
            dve.wait_ge(small_in, 32)

            def decayed(h, free):
                dve.wait_ge(scores_done, h + 1)
                if free is not None:
                    dve.wait_ge(pv_done, free)
                nc.vector.tensor_tensor(probs[:, :, :], bank_view(ps_s, P),
                                        decay_sb[:, bass.ds(h, 1), :].broadcast_to([P, BATCH, P]),
                                        ALU.mult).then_inc(probs_done, 1)

            def finish_gate(jb):
                wait_out_of_slot(dve, jb)
                nc.vector.tensor_scalar(gate[:, :], gate[:, :], 0.5, 0.5, ALU.mult, ALU.add).then_inc(gate_done, 1)

            def gated(h, free):
                dve.wait_ge(squares_done, h + 1)
                dve.wait_ge(gate_done, h + 1)
                if free is not None:
                    dve.wait_ge(y_lo_done, free)
                nc.vector.scalar_tensor_tensor(out=y_raw[:, :], in0=ps_o[:, :], scalar=nw[:, bass.ds(h, 1)],
                                               in1=gate[:, :], op0=ALU.mult, op1=ALU.mult).then_inc(y_done, 1)

            def y_lo_of(h, hd):
                dve.wait_ge(y_hi_done, h + 1)
                nc.vector.tensor_tensor(y_lo[:, hd, :], y_raw[:, :], y_hi[:, hd, :].bitcast(FP32), ALU.subtract)\
                    .then_inc(y_lo_done, 1)

            def add_out(c, jb):
                wait_job(dve, jb[2])
                nc.vector.tensor_tensor(acc[:, 2 * c:2 * c + 2, :], acc[:, 2 * c:2 * c + 2, :],
                                        bank_view(proj[jb[0]], DIM), ALU.add).then_inc(evacuated[jb[0]], 1)

            def back(i):
                free = None if isinstance(i, int) and i == 0 else i * 2
                decayed(i * 2, free)
                finish_gate(job(J_LOOP_A, JOBS_PAIR, i, 2))
                decayed(i * 2 + 1, i * 2 + 1)
                gated(i * 2, free)
                y_lo_of(i * 2, 0)
                finish_gate(job(J_LOOP_A, JOBS_PAIR, i, 3))
                gated(i * 2 + 1, i * 2 + 1)
                y_lo_of(i * 2 + 1, 1)

            back(0)
            for c in range(4):
                add_out(c, one_job(J_LOOP_A + 8 + c))
            with dve.Fori(1, PAIRS - 1) as i:
                back(i)
                for c in range(4):
                    add_out(c, job(J_LOOP_A, JOBS_PAIR, i, 8 + c))
            back(PAIRS - 1)
            for c in range(4):
                add_out(c, one_job(J_END_A - 4 + c))

            def rsqrt(n):
                dve.wait_ge(std_done, n + 1)
                link(nc.vector.reciprocal(rstd[:, :], std[:, :]))
                link(nc.vector.tensor_tensor(newton[:, :], rstd[:, :], rstd[:, :], ALU.mult))
                link(nc.vector.tensor_tensor(newton[:, :], newton[:, :], var_e[:, :], ALU.mult))
                link(nc.vector.tensor_scalar(newton[:, :], newton[:, :], -0.5, 1.5, ALU.mult, ALU.add))
                link(nc.vector.tensor_tensor(rstd[:, :], rstd[:, :], newton[:, :], ALU.mult))

            def ln_statistics():
                for c in range(BATCH):
                    last = nc.vector.bn_stats(stats[:, c, :], acc[:, c, :])
                link(last)
                for c in range(BATCH):
                    last = nc.vector.bn_aggr(mean_var[:, c, :], stats[:, c, :])
                link(last)
                nc.vector.tensor_scalar(var_e[:, :], mean_var[:, :, 1], LN_EPS, None, ALU.add).then_inc(var_done, 1)

            def ln_apply(n):
                rsqrt(n)
                for c in range(BATCH):
                    nc.vector.tensor_scalar(acc[:, c, :], acc[:, c, :], mean_var[:, c, 0:1], rstd[:, c:c + 1],
                                            ALU.subtract, ALU.mult).then_inc(normed, 1)

            def turned_lo(jobs, before):
                for c2 in range(BATCH // 2):
                    s = one_job(jobs + c2)[0]
                    dve.wait_ge(xt_hi_done, before + c2 + 1)
                    for c in range(2):
                        tok = slice((2 * c2 + c) * P, (2 * c2 + c + 1) * P)
                        last = nc.vector.tensor_tensor(xt_lo[:, :, tok], turned_view(s, c),
                                                       xt_hi[:, :, tok].bitcast(FP32), ALU.subtract)
                    last.then_inc(evacuated[s], 1)

            dve.wait_ge(ms_done, 1)
            nc.vector.tensor_scalar(var_e[:, :], ps_o[:, 0:BATCH], 1.0 / (HEADS * P), RMS_EPS, ALU.mult, ALU.add)\
                .then_inc(var_done, 1)
            rsqrt(0)
            dve.wait_ge(res_in, 16)
            wait_all_out(dve, J_END_A)
            for c in range(BATCH):
                last = nc.vector.scalar_tensor_tensor(out=acc[:, c, :], in0=acc[:, c, :], scalar=rstd[:, c:c + 1],
                                                      in1=x_res[:, c, :], op0=ALU.mult, op1=ALU.add)
            link(last)
            ln_statistics()

            def rope_parts(r, jb):
                dve.wait_ge(swap_done, r + 1)
                if not (isinstance(r, int) and r == 0):
                    dve.wait_ge(rope_done, r)
                nc.vector.tensor_tensor(cosed[:, :], proj[jb[0]][:, :], cos_t[:, :], ALU.mult)\
                    .then_inc(evacuated[jb[0]], 1)
                nc.vector.tensor_tensor(rot[:, :], swapped[:, :], sin_t[:, :], ALU.mult).then_inc(sin_done, 1)

            def rope_sum(r, dst, free):
                dve.wait_ge(sin_done, r + 1)
                dve.wait_ge(scores_done, free)
                nc.vector.tensor_tensor(dst[:, :], cosed[:, :], rot[:, :], ALU.add).then_inc(rope_done, 1)

            def cap_and_max(h, t_before):
                dve.wait_ge(scores_done, h + (HEADS + 1))
                if t_before is not None:
                    wait_job(dve, t_before)
                nc.vector.tensor_tensor(pb[:, :, :], bank_view(ps_s, P), cap[:, :, :], ALU.min).then_inc(masked, 1)
                dve.wait_ge(masked, h + 1)
                nc.vector.tensor_reduce(row_max[:, :], pb[:, :, :], AX.X, ALU.max).then_inc(max_done, 1)
                dve.wait_ge(max_done, h + 1)
                nc.vector.tensor_scalar(neg_max[:, :], row_max[:, :], -SM_SCALE, None, ALU.mult)\
                    .then_inc(neg_max_done, 1)

            def normalise(h):
                dve.wait_ge(exp_done, h + 1)
                nc.vector.reciprocal(row_inv[:, :], row_sum[:, :]).then_inc(inv_done, 1)
                dve.wait_ge(inv_done, h + 1)
                nc.vector.tensor_tensor(pb[:, :, :], pb[:, :, :],
                                        row_inv[:, :].unsqueeze(2).broadcast_to([P, BATCH, P]),
                                        ALU.mult).then_inc(soft_done, 1)

            def y_lo_cross(h, hd):
                dve.wait_ge(y_hi_done, h + (HEADS + 1))
                nc.vector.tensor_tensor(y_lo[:, hd, :], ps_o[:, :], y_hi[:, hd, :].bitcast(FP32), ALU.subtract)\
                    .then_inc(y_lo_done, 1)

            dve.wait_ge(pv_done, HEADS)
            dve.wait_ge(y_done, HEADS)
            rope_parts(0, one_job(J_K0))
            rope_sum(0, kr, HEADS)
            ln_apply(1)
            turned_lo(J_LN1, 0)
            rope_parts(1, one_job(J_Q0))
            rope_sum(1, qr, HEADS)
            dve.wait_ge(normed, BATCH)
            cap_and_max(0, None)
            normalise(0)
            rope_parts(2, one_job(J_Q1))
            rope_sum(2, qr, HEADS + 1)
            cap_and_max(1, J_T0)
            normalise(1)
            rope_parts(3, one_job(J_Q2))
            rope_sum(3, qr, HEADS + 2)
            y_lo_cross(0, 0)

            def heads_2_3(i, last):
                g = i * GROUP
                r = at(R_LOOP_B, ROPES_KV, i, 0)
                jb = [job(J_LOOP_B, JOBS_KV, i, j) for j in range(-1, 9)]
                t1, q3, kn, t2, q0, outs = (jb[0], jb[1], None, jb[2], None, jb[3:7]) if last else \
                    (jb[0], jb[1], jb[2], jb[3], jb[4], jb[5:9])
                cap_and_max(g + 2, t1[2])
                normalise(g + 2)
                rope_parts(r, q3)
                rope_sum(r, qr, g + (HEADS + 3))
                y_lo_cross(g + 1, 1)
                if not last:
                    rope_parts(r + 1, kn)
                cap_and_max(g + 3, t2[2])
                if not last:
                    rope_sum(r + 1, kr, g + (HEADS + 4))
                normalise(g + 3)
                if not last:
                    rope_parts(r + 2, q0)
                    rope_sum(r + 2, qr, g + (HEADS + 4))
                for c in range(4):
                    add_out(c, outs[c])
                y_lo_cross(g + 2, 0)

            with dve.Fori(0, KV_HEADS - 1) as i:
                heads_2_3(i, False)
                g = i * GROUP
                r = at(R_LOOP_B, ROPES_KV, i, 3)
                jb = [job(J_LOOP_B, JOBS_KV, i, j) for j in range(JOBS_KV)]
                cap_and_max(g + 4, jb[8][2])
                normalise(g + 4)
                rope_parts(r, jb[9])
                rope_sum(r, qr, g + (HEADS + 5))
                y_lo_cross(g + 3, 1)
                cap_and_max(g + 5, jb[11][2])
                normalise(g + 5)
                rope_parts(r + 1, jb[12])
                rope_sum(r + 1, qr, g + (HEADS + 6))
                for c in range(4):
                    add_out(c, jb[13 + c])
                y_lo_cross(g + 4, 0)
            heads_2_3(KV_HEADS - 1, True)
            y_lo_cross(HEADS - 1, 1)
            for c in range(4):
                add_out(c, one_job(J_TAIL_B + c))
            wait_all_out(dve, J_LN2)
            ln_statistics()
            ln_apply(2)
            turned_lo(J_LN2, 4)
            dve.wait_ge(normed, 2 * BATCH)

            def gate_up(c, gate_job, up_job):
                wait_out_of_slot(dve, gate_job)
                wait_job(dve, up_job[2])
                dve.wait_ge(y_lo_done, c + 2 * HEADS)
                nc.vector.tensor_tensor(mid[:, :], proj[up_job[0]][:, :], g_act[:, :], ALU.mult)\
                    .then_inc(evacuated[up_job[0]], 1)

            def mid_lo(c):
                dve.wait_ge(y_hi_done, c + (2 * HEADS + 1))
                nc.vector.tensor_tensor(y_lo[:, 0, :], mid[:, :], y_hi[:, 0, :].bitcast(FP32), ALU.subtract)\
                    .then_inc(y_lo_done, 1)

            gate_up(0, one_job(J_F0), one_job(J_F0 + 1))
            mid_lo(0)
            with dve.Fori(0, HCHUNKS - 1) as i:
                jb = [job(J_LOOP_F, JOBS_F, i, j) for j in range(JOBS_F)]
                add_out(0, jb[1])
                add_out(1, jb[2])
                gate_up(i + 1, jb[0], jb[3])
                add_out(2, jb[4])
                add_out(3, jb[5])
                mid_lo(i + 1)
            for c in range(4):
                add_out(c, one_job(J_TAIL_F + c))
            wait_all_out(dve, J_TAIL_F + 4)
            ln_statistics()
            ln_apply(3)

        @block.tensor
        def _(pe):
            def split_product(ps, stationary, moving, k, count):
                (s_hi, s_lo), (m_hi, m_lo) = stationary, moving
                nc.tensor.matmul(ps, s_hi, m_hi, start=(k == 0), stop=False)
                nc.tensor.matmul(ps, s_hi, m_lo, start=False, stop=False)
                return nc.tensor.matmul(ps, s_lo, m_hi, start=False, stop=(k == count - 1))

            def begin(jb, unit):
                if not (isinstance(jb[1], int) and jb[1] == 0):
                    pe.wait_ge(evacuated[jb[0]], jb[1])
                if unit is not None:
                    pe.wait_ge(w_lo_done, unit + 1)

            def channels(jb, unit, slot, x_hi, x_lo):
                begin(jb, unit)
                for half in range(2):
                    tok = slice(half * HALF, (half + 1) * HALF)
                    for k in range(KC):
                        cols = slice(k * P, (k + 1) * P)
                        last = split_product(proj[jb[0]][:, tok], (w_hi[:, slot, cols], w_lo[:, slot, cols]),
                                             (x_hi[:, k, tok], x_lo[:, k, tok]), k, KC)
                last.then_inc(jobs_done, 1)

            def values(jb, unit, slots, half):
                begin(jb, unit)
                for b in range(4):
                    tok = slice((4 * half + b) * P, (4 * half + b + 1) * P)
                    for k in range(KC):
                        cols = slice(k % 2 * 2 * P, (k % 2 + 1) * 2 * P)
                        s = slots[k // 2]
                        last = split_product(proj[jb[0]][:, b * 2 * P:(b + 1) * 2 * P],
                                             (xt_hi[:, k, tok], xt_lo[:, k, tok]),
                                             (w_hi[:, s, cols], w_lo[:, s, cols]), k, KC)
                last.then_inc(jobs_done, 1)

            def output(jb, c, unit, slots, heads_ready):
                begin(jb, unit)
                if heads_ready is not None:
                    pe.wait_ge(y_lo_done, heads_ready)
                for b in range(2):
                    tok = slice((2 * c + b) * P, (2 * c + b + 1) * P)
                    for hd, s in enumerate(slots):
                        last = split_product(proj[jb[0]][:, b * DIM:(b + 1) * DIM],
                                             (y_hi[:, hd, tok], y_lo[:, hd, tok]),
                                             (w_hi[:, s, :], w_lo[:, s, :]), hd, len(slots))
                last.then_inc(jobs_done, 1)

            pe.wait_ge(tables_in, 32)
            pe.wait_ge(onehot_done, 4)
            for t in range(2):
                for half in range(2):
                    tok = slice(half * HALF, (half + 1) * HALF)
                    for c in range(4):
                        last = nc.tensor.matmul(proj[t][:, tok], table[:, c, t * P:(t + 1) * P], onehot[:, c, tok],
                                                start=(c == 0), stop=(c == 3))
                last.then_inc(jobs_done, 1)

            def slot_a(j):
                return (U_LOOP_A + j) % RING

            def front(unit, jobs, slots):
                values(jobs[0], unit + 1, slots[0:2], 0)
                values(jobs[1], None, slots[0:2], 1)
                channels(jobs[2], unit + 2, slots[2], xt_hi, xt_lo)
                channels(jobs[3], unit + 3, slots[3], xt_hi, xt_lo)

            def scores(h, q_job, k_job, free):
                wait_out_of_slot(pe, q_job)
                wait_out_of_slot(pe, k_job)
                if free is not None:
                    pe.wait_ge(probs_done, free)
                for b in range(BATCH):
                    tok = slice(b * P, (b + 1) * P)
                    last = nc.tensor.matmul(ps_s[:, tok], k_sb[:, tok], q_sb[:, tok], start=True, stop=True)
                last.then_inc(scores_done, 1)

            def times_v(h, hd, free):
                pe.wait_ge(probs_done, h + 1)
                if free is not None:
                    pe.wait_ge(y_done, free)
                for b in range(BATCH):
                    last = nc.tensor.matmul(ps_o[:, b * P:(b + 1) * P], v_sb[:, b, hd * P:(hd + 1) * P],
                                            probs[:, b, :], start=True, stop=True)
                last.then_inc(pv_done, 1)

            def back(i, first):
                jb = [job(J_LOOP_A, JOBS_PAIR, i, j) for j in range(4)]
                u = at(U_LOOP_A, UNITS_PAIR, i, 0)
                v_a, v_b, q_a, k_a = [one_job(J_FRONT0 + j) for j in range(4)] if first else \
                    [job(J_LOOP_A, JOBS_PAIR, i, j) for j in (-8, -7, -6, -5)]
                scores(i * 2, q_a, k_a, None if first else i * 2)
                channels(jb[0], u, slot_a(0), xt_hi, xt_lo)
                wait_out_of_slot(pe, v_a)
                wait_out_of_slot(pe, v_b)
                times_v(i * 2, 0, None if first else i * 2)
                channels(jb[1], u + 1, slot_a(1), xt_hi, xt_lo)
                channels(jb[2], u + 2, slot_a(2), xt_hi, xt_lo)
                scores(i * 2 + 1, jb[0], jb[1], i * 2 + 1)
                channels(jb[3], u + 3, slot_a(3), xt_hi, xt_lo)
                times_v(i * 2 + 1, 1, i * 2 + 1)

            def next_front_and_out(i):
                jb = [job(J_LOOP_A, JOBS_PAIR, i, j) for j in range(JOBS_PAIR)]
                u = at(U_LOOP_A, UNITS_PAIR, i, 0)
                front(u + 4, jb[4:8], [slot_a(j) for j in range(4, 8)])
                for c in range(4):
                    output(jb[8 + c], c, u + 9, [slot_a(8), slot_a(9)], i * 2 + 2)

            pe.wait_ge(in_lo_done, KC)
            front(U_FRONT0, [one_job(J_FRONT0 + j) for j in range(4)], [0, 1, 2, 3])
            back(0, True)
            next_front_and_out(0)
            with pe.Fori(1, PAIRS - 1) as i:
                back(i, False)
                next_front_and_out(i)
            back(PAIRS - 1, False)
            for c in range(4):
                output(one_job(J_END_A - 4 + c), c, U_B - 1, [slot_a(4), slot_a(5)], HEADS)
            pe.wait_ge(sq_sum_done, HEADS + 1)
            pe.wait_ge(y_done, HEADS)
            for b in range(BATCH):
                last = nc.tensor.matmul(ps_o[:, b:b + 1], sq_sum[:, b * P:(b + 1) * P], ones, start=True, stop=True)
            last.then_inc(ms_done, 1)

            def turn_residual(jobs, normed_before):
                for c2 in range(BATCH // 2):
                    jb = one_job(jobs + c2)
                    begin(jb, None)
                    pe.wait_ge(normed, normed_before + 2 * c2 + 2)
                    for c in range(2):
                        for k in range(KC):
                            last = nc.tensor.transpose(turned_view(jb[0], c)[:, k, :],
                                                       acc[:, 2 * c2 + c, k * P:(k + 1) * P], ident)
                    last.then_inc(jobs_done, 1)

            def cross_scores(h, r_q):
                pe.wait_ge(rope_done, r_q + 1)
                if not (isinstance(h, int) and h == 0):
                    pe.wait_ge(masked, h)
                for b in range(BATCH):
                    tok = slice(b * P, (b + 1) * P)
                    last = nc.tensor.matmul(ps_s[:, tok], qr[:, tok], kr[:, tok], start=True, stop=True)
                last.then_inc(scores_done, 1)

            def turn_probs(h, jb):
                begin(jb, None)
                pe.wait_ge(soft_done, h + 1)
                for b in range(BATCH):
                    last = nc.tensor.transpose(proj[jb[0]][:, b * P:(b + 1) * P], pb[:, b, :], ident)
                last.then_inc(jobs_done, 1)

            def times_vx(h, t_job, free):
                wait_out_of_slot(pe, t_job)
                pe.wait_ge(y_lo_done, free)
                for b in range(BATCH):
                    last = nc.tensor.matmul(ps_o[:, b * P:(b + 1) * P], vx[:, b, :], pt[:, b, :],
                                            start=True, stop=True)
                last.then_inc(pv_done, 1)

            def turn_v(i, jb):
                wait_out_of_slot(pe, jb)
                pe.wait_ge(y_lo_done, i * GROUP + HEADS)
                for b in range(BATCH):
                    last = nc.tensor.transpose(ps_o[:, b * P:(b + 1) * P], vt[:, b * P:(b + 1) * P], ident)
                last.then_inc(vt_turned, 1)

            pe.wait_ge(in_lo_done, 2 * KC)
            channels(one_job(J_K0), U_B, U_B % RING, ctx_hi, ctx_lo)
            channels(one_job(J_V0), U_B + 1, (U_B + 1) % RING, ctx_hi, ctx_lo)
            pe.wait_ge(var_done, 1)
            turn_v(0, one_job(J_V0))
            turn_residual(J_LN1, 0)
            wait_all_out(pe, J_Q0)
            channels(one_job(J_Q0), U_B + 2, (U_B + 2) % RING, xt_hi, xt_lo)
            cross_scores(0, 1)
            channels(one_job(J_Q1), U_B + 3, (U_B + 3) % RING, xt_hi, xt_lo)
            turn_probs(0, one_job(J_T0))
            cross_scores(1, 2)
            channels(one_job(J_Q2), U_B + 4, (U_B + 4) % RING, xt_hi, xt_lo)
            pe.wait_ge(v_ready, 1)
            times_vx(0, one_job(J_T0), HEADS)
            turn_probs(1, one_job(J_T1))

            def slot_b(j):
                return (U_LOOP_B + j) % RING

            def heads_2_3(i, last):
                g = i * GROUP
                r = at(R_LOOP_B, ROPES_KV, i, 0)
                u = at(U_LOOP_B, UNITS_KV, i, 0)
                jb = [job(J_LOOP_B, JOBS_KV, i, j) for j in range(-1, 9)]
                t1, q3, kn, t2, q0, outs, t3 = (jb[0], jb[1], None, jb[2], None, jb[3:7], jb[7]) if last else \
                    (jb[0], jb[1], jb[2], jb[3], jb[4], jb[5:9], jb[9])
                o = 1 if last else 3
                cross_scores(g + 2, r - 1)
                channels(q3, u, slot_b(0), xt_hi, xt_lo)
                times_vx(g + 1, t1, g + (HEADS + 1))
                if not last:
                    channels(kn, u + 1, slot_b(1), ctx_hi, ctx_lo)
                turn_probs(g + 2, t2)
                cross_scores(g + 3, r)
                if not last:
                    channels(q0, u + 2, slot_b(2), xt_hi, xt_lo)
                for c in range(4):
                    output(outs[c], c, u + (o + 1), [slot_b(o), slot_b(o + 1)], g + (HEADS + 2))
                times_vx(g + 2, t2, g + (HEADS + 2))
                turn_probs(g + 3, t3)

            with pe.Fori(0, KV_HEADS - 1) as i:
                heads_2_3(i, False)
                g = i * GROUP
                r = at(R_LOOP_B, ROPES_KV, i, 0)
                u = at(U_LOOP_B, UNITS_KV, i, 0)
                jb = [job(J_LOOP_B, JOBS_KV, i, j) for j in range(JOBS_KV)]
                cross_scores(g + 4, r + 2)
                channels(jb[9], u + 5, slot_b(5), xt_hi, xt_lo)
                times_vx(g + 3, jb[8], g + (HEADS + 3))
                channels(jb[10], u + 6, slot_b(6), ctx_hi, ctx_lo)
                turn_probs(g + 4, jb[11])
                turn_v(i + 1, jb[10])
                cross_scores(g + 5, r + 3)
                channels(jb[12], u + 7, slot_b(7), xt_hi, xt_lo)
                for c in range(4):
                    output(jb[13 + c], c, u + 9, [slot_b(8), slot_b(9)], g + (HEADS + 4))
                pe.wait_ge(v_ready, i + 2)
                times_vx(g + 4, jb[11], g + (HEADS + 4))
                turn_probs(g + 5, jb[17])
            heads_2_3(KV_HEADS - 1, True)
            times_vx(HEADS - 1, one_job(J_TAIL_B - 1), 2 * HEADS - 1)
            for c in range(4):
                output(one_job(J_TAIL_B + c), c, U_F - 1, [slot_b(3), slot_b(4)], 2 * HEADS)

            turn_residual(J_LN2, BATCH)
            wait_all_out(pe, J_F0)
            channels(one_job(J_F0), U_F, 0, xt_hi, xt_lo)
            channels(one_job(J_F0 + 1), U_F + 1, 1, xt_hi, xt_lo)

            def slot_f(j):
                return (UF_LOOP + j) % RING_F

            with pe.Fori(0, HCHUNKS - 1) as i:
                jb = [job(J_LOOP_F, JOBS_F, i, j) for j in range(JOBS_F)]
                u = at(U_F + UF_LOOP, UNITS_F, i, 0)
                channels(jb[0], u, slot_f(0), xt_hi, xt_lo)
                output(jb[1], 0, u + 2, [slot_f(2)], i + (2 * HEADS + 1))
                output(jb[2], 1, None, [slot_f(2)], None)
                channels(jb[3], None, slot_f(1), xt_hi, xt_lo)
                output(jb[4], 2, None, [slot_f(2)], None)
                output(jb[5], 3, None, [slot_f(2)], None)
            for c in range(4):
                output(one_job(J_TAIL_F + c), c, U_F + UF_TOTAL - 1, [(UF_TOTAL - 1) % RING_F],
                       2 * HEADS + HCHUNKS)


def _decay_table():
    layer, layers = 1, 32
    base = 1.0 / 2.0 ** (8.0 / HEADS)
    slope = base ** (np.arange(HEADS, dtype=np.float32) + 1.0) * (1.0 - layer / (layers - 1 + 1e-05) + 1e-05)
    diff = np.arange(P)[None, :] - np.arange(P)[:, None]
    table = np.exp(-slope.astype(np.float64)[None, :, None] * np.maximum(diff, 0)[:, None, :])
    return (table * (diff >= 0)[:, None, :]).astype(np.float32)


def _rope_table():
    inv = (1.0 / ROPE_THETA ** (np.arange(0, P, 2, dtype=np.float32) / np.float32(P))).astype(np.float32)
    freqs = np.arange(POSITIONS, dtype=np.float32)[:, None] * inv[None, :]
    cos, sin = np.cos(freqs), np.sin(freqs)
    table = np.concatenate([cos, cos, -sin, sin], axis=1).astype(np.float32)
    return np.ascontiguousarray(table.reshape(4, P, 2 * P).transpose(1, 0, 2))


def _consts():
    iota = np.arange(POSITIONS, dtype=np.float32).reshape(4, P).T
    return np.concatenate([np.eye(P, dtype=np.float32), iota, np.ones((P, 1), np.float32)], axis=1)


def _in_rows(w):
    return w.reshape(KC, P, -1).transpose(1, 0, 2)


def _weight_stream(qkv_w, gate_w, out_w, wq, wk, wv, wo):
    qkv = qkv_w.reshape(HEADS, 3, P, DIM)

    def head(w):
        return _in_rows(w).reshape(P, DIM)

    units = []

    def front(i):
        v = _in_rows(qkv[2 * i:2 * i + 2, 2].reshape(2 * P, DIM).T)
        units.extend([v[:, 0:2].reshape(P, DIM), v[:, 2:4].reshape(P, DIM), head(qkv[2 * i, 0].T), head(qkv[2 * i, 1].T)])

    def back(i):
        units.extend([head(qkv[2 * i + 1, 0].T), head(qkv[2 * i + 1, 1].T)])
        units.extend(head(gate_w[h * P:(h + 1) * P].T) for h in (2 * i, 2 * i + 1))

    def out(i):
        units.extend(out_w[:, h * P:(h + 1) * P].T for h in (2 * i, 2 * i + 1))

    front(0)
    for i in range(PAIRS):
        back(i)
        if i + 1 < PAIRS:
            front(i + 1)
        out(i)

    def of(w, h):
        return head(w[:, h * P:(h + 1) * P])

    def rows(h):
        return [wo[n * P:(n + 1) * P] for n in (h, h + 1)]

    units += [of(wk, 0), of(wv, 0), of(wq, 0), of(wq, 1), of(wq, 2)]
    for i in range(KV_HEADS):
        g, more = GROUP * i, i + 1 < KV_HEADS
        units += [of(wq, g + 3)] + ([of(wk, i + 1), of(wq, g + 4)] if more else []) + rows(g)
        units += [of(wq, g + 5), of(wv, i + 1), of(wq, g + 6)] if more else []
        units += rows(g + 2)
    return np.stack(units)


def _ffn_stream(w_gate, w_up, w_down):
    pad = HCHUNKS * P - HIDDEN
    gate, up = (np.pad(w, ((0, pad), (0, 0))) for w in (w_gate, w_up))
    down = np.pad(w_down, ((0, 0), (0, pad)))
    units = []

    def cols(w, c):
        return _in_rows(w[c * P:(c + 1) * P].T).reshape(P, DIM)

    for c in range(HCHUNKS):
        units += [cols(gate, c), cols(up, c)]
        if c:
            units.append(down[:, (c - 1) * P:c * P].T)
    units.append(down[:, -P:].T)
    return np.stack(units)


def kernel(**inputs):
    import concourse.bacc as bacc
    from concourse.bass_utils import run_bass_kernel_spmd

    a = {k: np.asarray(v) for k, v in inputs.items()}
    x, ctx = a["x"], a["ctx_4096"]
    arrays = {
        "x_t": _in_rows(x.reshape(TOK, DIM).T),
        "x_rows": x.transpose(1, 0, 2),
        "ctx_t": _in_rows(ctx.reshape(TOK, DIM).T),
        "pos": a["pos_BxS2"].reshape(TOK),
        "mask": a["mask_BxSxS2_ik0"].transpose(1, 0, 2),
        "weights": _weight_stream(a["L0_attn_qkv_w"], a["L0_attn_gate_w"], a["L0_attn_out_w"], a["L0_xattn_Wq"],
                                  a["L0_xattn_Wk"], a["L0_xattn_Wv"], a["L0_xattn_Wo"]),
        "ffn_weights": _ffn_stream(a["L0_ffn_w_gate"], a["L0_ffn_w_up"], a["L0_ffn_w_down"]),
        "ffn_scales": np.tile(np.stack([a["L0_ffn_scale_gate"], a["L0_ffn_scale_up"], a["L0_ffn_scale_down"]])
                              .reshape(1, 3), (P, 1)),
        "norm_w": a["L0_attn_norm_w"].reshape(HEADS, P).T,
        "decay": _decay_table(),
        "rope_table": _rope_table(),
        "consts": _consts(),
    }
    arrays = {k: np.ascontiguousarray(v) for k, v in arrays.items()}
    nc = bacc.Bacc("TRN2", target_bir_lowering=False, num_devices=1)
    args = [nc.dram_tensor(k, v.shape, mybir.dt.from_np(v.dtype), kind="ExternalInput").ap()
            for k, v in arrays.items()]
    out = nc.dram_tensor("out", [BATCH, SEQ, DIM], FP32, kind="ExternalOutput").ap()
    build(nc, *args, out)
    r = run_bass_kernel_spmd(nc, [arrays], core_ids=[0])
    return r.results[0]["out"]
```

```python
import numpy as np

import concourse.bass as bass
from concourse import mybir

FP32 = mybir.dt.float32
FP32R = mybir.dt.float32r
INT32 = mybir.dt.int32
ALU = mybir.AluOpType
ACT = mybir.ActivationFunctionType
AX = mybir.AxisListType

P = 128
BATCH, SEQ, DIM = 8, 128, 512
TOK = BATCH * SEQ
KC = DIM // P
HEADS = 32
PAIRS = HEADS // 2
KV_HEADS = 8
GROUP = HEADS // KV_HEADS
HIDDEN = 1376
HCHUNKS = -(-HIDDEN // P)
POSITIONS = 512
ROPE_THETA = 10000.0
LN_EPS = 1e-5
RMS_EPS = 1e-5
SM_SCALE = float(1.0 / np.sqrt(np.float32(P)))
MASKED = float(-1e9 * np.sqrt(np.float32(P)))
UNMASKED = 3.0e38
HALF = TOK // 2
RING = 5
RING_F = 3


UNITS_PAIR, JOBS_PAIR = 10, 12
U_FRONT0, U_LOOP_A = 0, 4
J_FRONT0 = 0
J_TABLES = J_FRONT0 + 4
J_LOOP_A = J_TABLES + 2
J_END_A = J_LOOP_A + JOBS_PAIR * (PAIRS - 1) + 8
U_B = U_LOOP_A + UNITS_PAIR * (PAIRS - 1) + 6
J_K0, J_LN1, J_Q0, J_V0 = J_END_A, J_END_A + 1, J_END_A + 3, J_END_A + 4
J_Q1, J_T0, J_Q2, J_T1 = (J_V0 + n for n in (1, 2, 3, 4))
J_LOOP_B = J_T1 + 1
UNITS_KV, JOBS_KV = 10, 18
U_LOOP_B = U_B + 5
ROPES_KV, R_LOOP_B = 5, 4
HALVED_KV, H_LOOP_B = 6, 5
J_LAST_B = J_LOOP_B + JOBS_KV * (KV_HEADS - 1)
J_TAIL_B = J_LAST_B + 7
J_LN2 = J_TAIL_B + 4
U_F = U_LOOP_B + UNITS_KV * (KV_HEADS - 1) + 5
J_F0 = J_LN2 + 2
J_LOOP_F = J_F0 + 2
UNITS_F, JOBS_F = 3, 6
J_TAIL_F = J_LOOP_F + JOBS_F * (HCHUNKS - 1)
UF_LOOP = 2
UF_TOTAL = UF_LOOP + UNITS_F * (HCHUNKS - 1) + 1


def at(base, per, i, j):
    return i * per + (base + j)


def job(base, per, i, j):
    return (base + j) % 2, i * (per // 2) + (base + j) // 2, at(base, per, i, j)


def build(nc, x_t, x_rows, ctx_t, pos, mask, weights, ffn_weights, ffn_scales, norm_w, decay, rope_table,
          consts, out):
    place_at = [(nc.sbuf_base + 31) // 32 * 32]

    def sb(name, shape, dtype=FP32, offset=None):
        size = 4 * int(np.prod(shape[1:]))
        if offset is None:
            offset = place_at[0]
            place_at[0] += (size + 31) // 32 * 32
            offsets[name] = offset
        return nc.alloc_sbuf_tensor_at(name, shape, dtype, offset=offset)

    offsets = {}
    xt_hi = sb("xt_hi", [P, KC, TOK], FP32R)
    xt_lo = sb("xt_lo", [P, KC, TOK], FP32R)
    ctx_hi = sb("ctx_hi", [P, KC, TOK], FP32R)
    ctx_lo = sb("ctx_lo", [P, KC, TOK], FP32R)
    acc = sb("acc", [P, BATCH, DIM])
    raw = sb("raw", [P, RING, DIM])
    w_hi = sb("w_hi", [P, RING, DIM], FP32R)
    w_lo = sb("w_lo", [P, RING, DIM], FP32R)
    q_sb = sb("q_sb", [P, TOK])
    k_sb = sb("k_sb", [P, TOK])
    v_sb = sb("v_sb", [P, BATCH, 2 * P])
    gate = sb("gate", [P, TOK])
    probs = sb("probs", [P, BATCH, P])
    y_raw = sb("y_raw", [P, TOK])
    squares = sb("squares", [P, TOK])
    sq_sum = sb("sq_sum", [P, TOK])
    y_hi = sb("y_hi", [P, 2, TOK], FP32R)
    y_lo = sb("y_lo", [P, 2, TOK], FP32R)
    decay_sb = sb("decay_sb", [P, HEADS, P])
    cos_t = sb("cos_t", [P, TOK])
    sin_t = sb("sin_t", [P, TOK])
    cap = sb("cap", [P, BATCH, P])
    nw = sb("nw", [P, HEADS])
    scales = sb("scales", [P, 3])
    cst = sb("cst", [P, P + 5])
    stats = sb("stats", [P, BATCH, 6])
    mean_var = sb("mean_var", [P, BATCH, 2])
    var_e = sb("var_e", [P, BATCH])
    std = sb("std", [P, BATCH])
    shift = sb("shift", [P, BATCH])
    table_lo = sb("table_lo", [P, 4, 2 * P], FP32R)
    rstd = sb("rstd", [P, BATCH])
    newton = sb("newton", [P, BATCH])
    cosed = sb("cosed", [P, TOK])
    row_max = sb("row_max", [P, BATCH])
    neg_max = sb("neg_max", [P, BATCH])
    row_sum = sb("row_sum", [P, BATCH])
    row_inv = sb("row_inv", [P, BATCH])
    assert place_at[0] <= nc.sbuf_usable_end
    ident, iota, ones = cst[:, 0:P], cst[:, P:P + 4], cst[:, P + 4:P + 5]
    x_raw = sb("x_raw", [P, KC, TOK], offset=offsets["q_sb"])
    ctx_raw = sb("ctx_raw", [P, KC, TOK], offset=offsets["acc"])
    onehot = sb("onehot", [P, 4, TOK], FP32R, offset=offsets["y_hi"])
    pos_i = sb("pos_i", [P, TOK], INT32, offset=offsets["gate"])
    pos_wrap = sb("pos_wrap", [P, TOK], offset=offsets["y_raw"])
    pos_f = sb("pos_f", [P, TOK], offset=offsets["squares"])
    table = sb("table", [P, 4, 2 * P], offset=offsets["cosed"])
    table_hi = sb("table_hi", [P, 4, 2 * P], FP32R, offset=offsets["probs"])
    mask_i = sb("mask_i", [P, BATCH, P], INT32, offset=offsets["cap"])
    mask_tmp = sb("mask_tmp", [P, BATCH, P], offset=offsets["gate"])
    x_res = sb("x_res", [P, BATCH, DIM], offset=offsets["xt_lo"])
    qr = sb("qr", [P, TOK], offset=offsets["q_sb"])
    pb = sb("pb", [P, BATCH, P], offset=offsets["k_sb"])
    rot = sb("rot", [P, TOK], offset=offsets["v_sb"])
    pt = sb("pt", [P, BATCH, P], offset=offsets["v_sb"] + 4 * TOK)
    kr = sb("kr", [P, TOK], offset=offsets["gate"])
    vx = sb("vx", [P, BATCH, P], offset=offsets["probs"])
    swapped = sb("swapped", [P, TOK], offset=offsets["y_raw"])
    vt = sb("vt", [P, TOK], offset=offsets["squares"])
    g_act = sb("g_act", [P, TOK], offset=offsets["q_sb"])
    mid = sb("mid", [P, TOK], offset=offsets["k_sb"])

    proj = [nc.alloc_psum_tensor(f"proj{s}", [P, TOK], FP32) for s in range(2)]
    ps_s = nc.alloc_psum_tensor("ps_s", [P, TOK], FP32)
    ps_o = nc.alloc_psum_tensor("ps_o", [P, TOK], FP32)

    sem = nc.alloc_semaphore
    tables_in = sem("tables_in")
    pos_in = sem("pos_in")
    table_hi_done = sem("table_hi_done")
    table_lo_done = sem("table_lo_done")
    mask_in = sem("mask_in")
    x_in = [sem(f"x_in{n}") for n in range(2 * KC)]
    ctx_in = [sem(f"ctx_in{k}") for k in range(KC)]
    small_in = sem("small_in")
    decay_in = sem("decay_in")
    res_in = sem("res_in")
    raw_in = [sem(f"raw_in{s}") for s in range(RING)]
    rawf_in = [sem(f"rawf_in{s}") for s in range(RING_F)]
    stored = sem("stored")
    w_hi_done = sem("w_hi_done")
    w_lo_done = sem("w_lo_done")
    w_ffn_done = sem("w_ffn_done")
    onehot_done = sem("onehot_done")
    in_hi_done = sem("in_hi_done")
    in_lo_done = sem("in_lo_done")
    acc_zeroed = sem("acc_zeroed")
    jobs_done = sem("jobs_done")
    evacuated = [sem(f"evacuated{s}") for s in range(2)]
    scores_done = sem("scores_done")
    probs_done = sem("probs_done")
    pv_done = sem("pv_done")
    gate_done = sem("gate_done")
    squares_done = sem("squares_done")
    sq_sum_done = sem("sq_sum_done")
    y_done = sem("y_done")
    y_hi_done = sem("y_hi_done")
    y_lo_done = sem("y_lo_done")
    ms_done = sem("ms_done")
    var_done = sem("var_done")
    std_done = sem("std_done")
    shift_done = sem("shift_done")
    normed = sem("normed")
    first_half = sem("first_half")
    late_turned = sem("late_turned")
    late_hi_done = sem("late_hi_done")
    late_taken = sem("late_taken")
    xt_hi_done = sem("xt_hi_done")
    swap_done = sem("swap_done")
    sin_done = sem("sin_done")
    rope_done = sem("rope_done")
    masked = sem("masked")
    max_done = sem("max_done")
    neg_max_done = sem("neg_max_done")
    exp_done = sem("exp_done")
    inv_done = sem("inv_done")
    soft_done = sem("soft_done")
    vt_turned = sem("vt_turned")
    v_ready = sem("v_ready")
    dve_step = sem("dve_step")

    def bank_view(tensor, n):
        return tensor[:, :].rearrange("p (b n) -> p b n", n=n)

    def wait_job(eng, n):
        eng.wait_ge(jobs_done, n + 1)

    def wait_out_of_slot(eng, j):
        eng.wait_ge(evacuated[j[0]], j[1] + 1)

    def wait_all_out(eng, n):
        for s in range(2):
            eng.wait_ge(evacuated[s], (n + 1 - s) // 2)

    def one_job(n):
        return n % 2, n // 2, n

    def turned_view(tensor, c):
        return tensor[:, c * DIM:(c + 1) * DIM].rearrange("p (k t) -> p k t", k=KC)

    def half(h):
        return slice(h * HALF, (h + 1) * HALF)

    with nc.Block() as block:

        @block.sync
        def _(sp):
            def load_unit(unit, slot, lo_before):
                if lo_before is not None:
                    sp.wait_ge(w_lo_done, lo_before)
                sp.dma_start(raw[:, slot, :], weights[unit, :, :].squeeze(0)).then_inc(raw_in[slot], 16)

            def load_x(h):
                for k in range(KC):
                    sp.dma_start(x_raw[:, k, half(h)], x_t[:, k, half(h)]).then_inc(x_in[h * KC + k], 16)

            load_x(0)
            for n in range(2):
                load_unit(slice(n, n + 1), n, None)
            load_x(1)
            for n in range(2, RING):
                load_unit(slice(n, n + 1), n, None)
            sp.dma_start(pos_i[:, :], pos.partition_broadcast(P)).then_inc(pos_in, 16)
            sp.dma_start(cst[:, :], consts).then_inc(tables_in, 16)
            sp.dma_start(table[:, :, :], rope_table).then_inc(tables_in, 16)
            sp.dma_start(decay_sb[:, :, :], decay).then_inc(decay_in, 16)
            sp.dma_start(nw[:, :], norm_w).then_inc(small_in, 16)
            sp.dma_start(scales[:, :], ffn_scales).then_inc(small_in, 16)
            for k in range(KC):
                sp.dma_start(ctx_raw[:, k, :], ctx_t[:, k, :]).then_inc(ctx_in[k], 16)
            sp.dma_start(mask_i[:, :, :], mask).then_inc(mask_in, 16)
            with sp.Fori(1, U_F // RING) as r:
                for s in range(RING):
                    load_unit(bass.ds(r * RING + s, 1), s, r * RING + (s + 1 - RING))
            ffn_i = raw[:, :, :].bitcast(INT32)
            sp.wait_ge(w_lo_done, U_F)
            for m in range(RING_F):
                sp.dma_start(ffn_i[:, m, :], ffn_weights[m, :, :]).then_inc(rawf_in[m], 16)
            with sp.Fori(1, UF_TOTAL // RING_F) as r:
                for s in range(RING_F):
                    sp.wait_ge(w_lo_done, r * RING_F + (U_F - RING_F + s + 1))
                    sp.dma_start(ffn_i[:, s, :], ffn_weights[bass.ds(r * RING_F + s, 1), :, :].squeeze(0))\
                        .then_inc(rawf_in[s], 16)
            for c in range(BATCH):
                sp.wait_ge(normed, 2 * BATCH + c + 1)
                sp.dma_start(out[c, :, :], acc[:, c, :]).then_inc(stored, 16)
            sp.wait_ge(stored, 16 * BATCH)

        @block.gpsimd
        def _(pool):
            def lo_of_unit(n, s):
                pool.wait_ge(w_hi_done, n + 1)
                nc.gpsimd.tensor_tensor(w_lo[:, s, :], raw[:, s, :], w_hi[:, s, :].bitcast(FP32),
                                        ALU.subtract).then_inc(w_lo_done, 1)

            def add_squares(h):
                pool.wait_ge(squares_done, h + 1)
                pool.wait_ge(sq_sum_done, h + 1)
                nc.gpsimd.tensor_tensor(sq_sum[:, :], sq_sum[:, :], squares[:, :], ALU.add)\
                    .then_inc(sq_sum_done, 1)

            nc.gpsimd.memset(sq_sum[:, :], 0.0).then_inc(sq_sum_done, 1)
            for n in range(U_LOOP_A + RING):
                lo_of_unit(n, n % RING)

            def pair(i, last):
                def lo(j):
                    lo_of_unit(at(U_LOOP_A + RING + j, UNITS_PAIR, i, 0), (U_LOOP_A + RING + j) % RING)
                lo(0)
                add_squares(i * 2)
                for j in range(1, 4):
                    lo(j)
                add_squares(i * 2 + 1)
                for j in range(4, 6 if last else UNITS_PAIR):
                    lo(j)

            with pool.Fori(0, PAIRS - 1) as i:
                pair(i, False)
            pair(PAIRS - 1, True)
            with pool.Fori(U_LOOP_B // RING, U_F // RING) as r:
                for s in range(RING):
                    lo_of_unit(r * RING + s, s)

            with pool.Fori(0, UF_TOTAL // RING_F) as r:
                for s in range(RING_F):
                    lo_of_unit(r * RING_F + (U_F + s), s)

        @block.scalar
        def _(act):
            def hi_of_unit(n, loads):
                s = n[0]
                act.wait_ge(raw_in[s], loads * 16)
                nc.scalar.activation(w_hi[:, s, :], raw[:, s, :], ACT.Copy).then_inc(w_hi_done, 1)

            def pair_unit(i, j):
                n = U_LOOP_A + j
                hi_of_unit((n % RING,), i * (UNITS_PAIR // RING) + (n // RING + 1))

            def kv_unit(i, j):
                n = U_LOOP_B + j
                hi_of_unit((n % RING,), i * (UNITS_KV // RING) + (n // RING + 1))

            def hi_of_x(h):
                for k in range(KC):
                    act.wait_ge(x_in[h * KC + k], 16)
                    nc.scalar.activation(xt_hi[:, k, half(h)], x_raw[:, k, half(h)], ACT.Copy)\
                        .then_inc(in_hi_done, 1)

            hi_of_x(0)
            for n in range(2):
                hi_of_unit((n,), 1)
            hi_of_x(1)
            for n in range(2, RING):
                hi_of_unit((n,), 1)

            def silu_v(jb, half, free):
                wait_job(act, jb[2])
                if free is not None:
                    act.wait_ge(pv_done, free)
                nc.scalar.activation(v_sb[:, 4 * half:4 * half + 4, :], bank_view(proj[jb[0]], 2 * P), ACT.Silu)\
                    .then_inc(evacuated[jb[0]], 1)

            def silu_head(dst, jb, free):
                wait_job(act, jb[2])
                if free is not None:
                    act.wait_ge(scores_done, free)
                nc.scalar.activation(dst[:, :], proj[jb[0]][:, :], ACT.Silu).then_inc(evacuated[jb[0]], 1)

            def tanh_gate(jb, free):
                wait_job(act, jb[2])
                if free is not None:
                    act.wait_ge(y_done, free)
                nc.scalar.activation(gate[:, :], proj[jb[0]][:, :], ACT.Tanh, scale=0.5)\
                    .then_inc(evacuated[jb[0]], 1)

            def square(h):
                act.wait_ge(pv_done, h + 1)
                act.wait_ge(sq_sum_done, h + 1)
                nc.scalar.activation(squares[:, :], ps_o[:, :], ACT.Square).then_inc(squares_done, 1)

            def y_hi_of(h, hd, before):
                act.wait_ge(y_done, h + 1)
                if before is not None:
                    wait_job(act, before)
                nc.scalar.activation(y_hi[:, hd, :], y_raw[:, :], ACT.Copy).then_inc(y_hi_done, 1)

            def back(i):
                jb = [job(J_LOOP_A, JOBS_PAIR, i, j) for j in range(4)]
                silu_head(q_sb, jb[0], i * 2 + 1)
                pair_unit(i, 5)
                square(i * 2)
                silu_head(k_sb, jb[1], i * 2 + 1)
                pair_unit(i, 6)
                tanh_gate(jb[2], at(0, 2, i, 0) if not isinstance(i, int) or i else None)
                pair_unit(i, 7)
                y_hi_of(i * 2, 0, at(J_LOOP_A, JOBS_PAIR, i, -1))
                tanh_gate(jb[3], i * 2 + 1)
                pair_unit(i, 8)
                square(i * 2 + 1)
                y_hi_of(i * 2 + 1, 1, None)

            act.wait_ge(in_lo_done, 2 * KC)
            silu_v(one_job(J_FRONT0), 0, None)
            silu_v(one_job(J_FRONT0 + 1), 1, None)
            pair_unit(0, 1)
            pair_unit(0, 2)
            silu_head(q_sb, one_job(J_FRONT0 + 2), None)
            pair_unit(0, 3)
            act.wait_ge(tables_in, 32)
            nc.scalar.activation(table_hi[:, :, :], table[:, :, :], ACT.Copy).then_inc(table_hi_done, 1)
            silu_head(k_sb, one_job(J_FRONT0 + 3), None)
            pair_unit(0, 4)
            for k in range(KC):
                act.wait_ge(ctx_in[k], 16)
                nc.scalar.activation(ctx_hi[:, k, :], ctx_raw[:, k, :], ACT.Copy).then_inc(in_hi_done, 1)
            for n, dst in enumerate((cos_t, sin_t)):
                s, _, m = one_job(J_TABLES + n)
                wait_job(act, m)
                nc.scalar.activation(dst[:, :], proj[s][:, :], ACT.Copy).then_inc(evacuated[s], 1)
            with act.Fori(0, PAIRS - 1) as i:
                back(i)
                jb = [job(J_LOOP_A, JOBS_PAIR, i, j) for j in range(JOBS_PAIR)]
                silu_v(jb[4], 0, i * 2 + 2)
                silu_v(jb[5], 1, None)
                pair_unit(i, 9)
                pair_unit(i, 10)
                silu_head(q_sb, jb[6], i * 2 + 2)
                pair_unit(i, 11)
                silu_head(k_sb, jb[7], None)
                pair_unit(i, 12)
                wait_job(act, jb[11][2])
                pair_unit(i, 13)
                pair_unit(i, 14)
            back(PAIRS - 1)
            act.dma_start(x_res[:, :, :], x_rows).then_inc(res_in, 16)

            def sqrt_var(n, cols):
                act.wait_ge(var_done, n + 1)
                nc.scalar.activation(std[:, cols], var_e[:, cols], ACT.Sqrt).then_inc(std_done, 1)

            sqrt_var(0, slice(0, BATCH))
            wait_job(act, J_END_A - 1)
            pair_unit(PAIRS - 1, 9)
            pair_unit(PAIRS - 1, 10)

            def norm_group(ln, g):
                sqrt_var(2 * ln + g + 1, slice(4 * g, 4 * g + 4))
                act.wait_ge(shift_done, 2 * ln + g + 1)
                for c in range(4 * g, 4 * g + 4):
                    nc.scalar.activation(acc[:, c, :], acc[:, c, :], ACT.Identity, scale=rstd[:, c:c + 1],
                                         bias=shift[:, c:c + 1]).then_inc(normed, 1)

            def turned_hi(tensor, c2, done):
                for c in range(2):
                    tok = slice((2 * c2 + c) * P, (2 * c2 + c + 1) * P)
                    last = nc.scalar.activation(xt_hi[:, :, tok], turned_view(tensor, c), ACT.Copy)
                last.then_inc(done, 1)

            def early_hi(jobs):
                for c2 in range(2):
                    wait_job(act, jobs + c2)
                    turned_hi(proj[(jobs + c2) % 2], c2, xt_hi_done)

            def late_hi(ln):
                for n, tensor in enumerate((ps_s, ps_o)):
                    act.wait_ge(late_turned, 2 * ln + n + 1)
                    turned_hi(tensor, 2 + n, late_hi_done)

            def copy_vt_first(f, jb, free):
                act.wait_ge(first_half, f + 1)
                if free is not None:
                    act.wait_ge(vt_turned, free)
                nc.scalar.activation(vt[:, half(0)], proj[jb[0]][:, half(0)], ACT.Copy)

            def copy_vt_second(jb):
                wait_job(act, jb[2])
                nc.scalar.activation(vt[:, half(1)], proj[jb[0]][:, half(1)], ACT.Copy).then_inc(evacuated[jb[0]], 1)

            def copy_v(i):
                act.wait_ge(vt_turned, i + 1)
                nc.scalar.activation(vx[:, :, :], bank_view(ps_o, P), ACT.Copy).then_inc(v_ready, 1)

            def swap_first(f, jb, free):
                act.wait_ge(first_half, f + 1)
                if free is not None:
                    act.wait_ge(sin_done, free)
                swap(jb, half(0))

            def swap_second(jb):
                wait_job(act, jb[2])
                swap(jb, half(1))

            def swap(jb, tok):
                nc.scalar.activation(swapped[0:64, tok], proj[jb[0]][64:128, tok], ACT.Copy)
                nc.scalar.activation(swapped[64:128, tok], proj[jb[0]][0:64, tok], ACT.Copy).then_inc(swap_done, 1)

            def exps(h):
                act.wait_ge(neg_max_done, h + 1)
                for b in range(BATCH):
                    last = nc.scalar.activation(pb[:, b, :], pb[:, b, :], ACT.Exp, bias=neg_max[:, b:b + 1],
                                                scale=SM_SCALE, accum_out=row_sum[:, b:b + 1])
                last.then_inc(exp_done, 1)

            def y_hi_cross(h, hd, before):
                act.wait_ge(pv_done, h + (HEADS + 1))
                if before is not None:
                    wait_job(act, before)
                nc.scalar.activation(y_hi[:, hd, :], ps_o[:, :], ACT.Copy).then_inc(y_hi_done, 1)

            def copy_pt(h, jb):
                wait_job(act, jb[2])
                act.wait_ge(pv_done, h + HEADS)
                nc.scalar.activation(pt[:, :, :], bank_view(proj[jb[0]], P), ACT.Copy)\
                    .then_inc(evacuated[jb[0]], 1)

            act.wait_ge(y_lo_done, HEADS)
            act.wait_ge(sq_sum_done, HEADS + 1)
            norm_group(0, 0)
            swap_first(0, one_job(J_K0), None)
            swap_second(one_job(J_K0))
            kv_unit(0, 0)
            early_hi(J_LN1)
            norm_group(0, 1)
            swap_first(1, one_job(J_Q0), 1)
            copy_vt_first(2, one_job(J_V0), None)
            late_hi(0)
            swap_second(one_job(J_Q0))
            copy_vt_second(one_job(J_V0))
            kv_unit(0, 1)
            kv_unit(0, 2)
            copy_v(0)
            swap_first(3, one_job(J_Q1), 2)
            exps(0)
            swap_second(one_job(J_Q1))
            kv_unit(0, 3)
            copy_pt(0, one_job(J_T0))
            swap_first(4, one_job(J_Q2), 3)
            exps(1)
            swap_second(one_job(J_Q2))
            kv_unit(0, 4)
            y_hi_cross(0, 0, None)
            copy_pt(1, one_job(J_T1))

            def heads_2_3(i, last):
                g = i * GROUP
                r = at(R_LOOP_B, ROPES_KV, i, 0)
                jb = [job(J_LOOP_B, JOBS_KV, i, j) for j in range(9)]
                q3, kn, t2, q0, o3, t3 = (jb[0], None, jb[1], None, jb[5], jb[6]) if last else \
                    (jb[0], jb[1], jb[2], jb[3], jb[7], jb[8])
                f = at(H_LOOP_B, HALVED_KV, i, 0)
                swap_first(f, q3, r)
                exps(g + 2)
                swap_second(q3)
                if not last:
                    kv_unit(i, 5)
                y_hi_cross(g + 1, 1, None)
                if not last:
                    swap_first(f + 1, kn, r + 1)
                    swap_second(kn)
                    kv_unit(i, 6)
                copy_pt(g + 2, t2)
                if not last:
                    swap_first(f + 2, q0, r + 2)
                exps(g + 3)
                if not last:
                    swap_second(q0)
                    kv_unit(i, 7)
                y_hi_cross(g + 2, 0, o3[2])
                if not last:
                    kv_unit(i, 8)
                    kv_unit(i, 9)
                copy_pt(g + 3, t3)

            with act.Fori(0, KV_HEADS - 1) as i:
                heads_2_3(i, False)
                g = i * GROUP
                r = at(R_LOOP_B, ROPES_KV, i, 3)
                jb = [job(J_LOOP_B, JOBS_KV, i, j) for j in range(JOBS_KV)]
                f = at(H_LOOP_B, HALVED_KV, i, 3)
                swap_first(f, jb[9], r)
                exps(g + 4)
                swap_second(jb[9])
                kv_unit(i, 10)
                y_hi_cross(g + 3, 1, None)
                copy_vt_first(f + 1, jb[10], i + 1)
                copy_vt_second(jb[10])
                kv_unit(i, 11)
                copy_pt(g + 4, jb[11])
                copy_v(i + 1)
                swap_first(f + 2, jb[12], r + 1)
                exps(g + 5)
                swap_second(jb[12])
                kv_unit(i, 12)
                y_hi_cross(g + 4, 0, jb[16][2])
                kv_unit(i, 13)
                kv_unit(i, 14)
                copy_pt(g + 5, jb[17])
            heads_2_3(KV_HEADS - 1, True)
            y_hi_cross(HEADS - 1, 1, None)

            def ffn_unit(i, j, which):
                n = UF_LOOP + j
                s = n % RING_F
                act.wait_ge(rawf_in[s], i * 16 + 16 * (n // RING_F + 1))
                nc.scalar.activation(raw[:, s, :], raw[:, s, :].bitcast(INT32), ACT.Copy,
                                     scale=scales[:, which:which + 1]).then_inc(w_ffn_done, 1)
                act.wait_ge(w_ffn_done, i * UNITS_F + (n + 1))
                nc.scalar.activation(w_hi[:, s, :], raw[:, s, :], ACT.Copy).then_inc(w_hi_done, 1)

            def silu_gate(jb, free):
                wait_job(act, jb[2])
                if free is not None:
                    wait_out_of_slot(act, free)
                nc.scalar.activation(g_act[:, :], proj[jb[0]][:, :], ACT.Silu).then_inc(evacuated[jb[0]], 1)

            def mid_hi(jb, before):
                wait_out_of_slot(act, jb)
                wait_job(act, before)
                nc.scalar.activation(y_hi[:, 0, :], mid[:, :], ACT.Copy).then_inc(y_hi_done, 1)

            act.wait_ge(small_in, 32)
            norm_group(1, 0)
            wait_job(act, J_LN2 - 1)
            ffn_unit(0, -2, 0)
            early_hi(J_LN2)
            ffn_unit(0, -1, 1)
            norm_group(1, 1)
            late_hi(1)
            ffn_unit(0, 0, 0)
            silu_gate(one_job(J_F0), None)
            ffn_unit(0, 1, 1)
            mid_hi(one_job(J_F0 + 1), J_LN2 - 1)
            ffn_unit(0, 2, 2)

            def chunk(i, last):
                jb = [job(J_LOOP_F, JOBS_F, i, j) for j in range(-3, JOBS_F)]
                up_before, gate_job, up_job, down_last = job(J_LOOP_F, JOBS_F, i, -1 - 2), jb[3], jb[6], jb[8]
                if isinstance(i, int) and i == 0:
                    up_before = one_job(J_F0 + 1)
                silu_gate(gate_job, up_before)
                ffn_unit(i, 3, 2 if last else 0)
                wait_job(act, up_job[2])
                if not last:
                    ffn_unit(i, 4, 1)
                mid_hi(up_job, down_last[2])
                if not last:
                    ffn_unit(i, 5, 2)

            chunk(0, False)
            with act.Fori(1, HCHUNKS - 2) as i:
                chunk(i, False)
            chunk(HCHUNKS - 2, True)
            norm_group(2, 0)
            norm_group(2, 1)

        @block.vector
        def _(dve):
            steps = [0]

            def link(ins):
                steps[0] += 1
                ins.then_inc(dve_step, 1)
                dve.wait_ge(dve_step, steps[0])

            for h in range(2):
                for k in range(KC):
                    dve.wait_ge(in_hi_done, h * KC + k + 1)
                    nc.vector.tensor_tensor(xt_lo[:, k, half(h)], x_raw[:, k, half(h)],
                                            xt_hi[:, k, half(h)].bitcast(FP32), ALU.subtract).then_inc(in_lo_done, 1)
            dve.wait_ge(pos_in, 16)
            link(nc.vector.tensor_scalar(pos_wrap[:, :], pos_i[:, :], 0.0, float(POSITIONS), ALU.is_lt, ALU.mult))
            link(nc.vector.tensor_tensor(pos_f[:, :], pos_i[:, :], pos_wrap[:, :], ALU.add))
            link(nc.vector.tensor_scalar(pos_f[:, :], pos_f[:, :], 0.0, float(POSITIONS - 1), ALU.max, ALU.min))
            dve.wait_ge(tables_in, 32)
            for c in range(4):
                nc.vector.tensor_scalar(onehot[:, c, :], pos_f[:, :], iota[:, c:c + 1], None, ALU.is_equal)\
                    .then_inc(onehot_done, 1)
            dve.wait_ge(table_hi_done, 1)
            nc.vector.tensor_tensor(table_lo[:, :, :], table[:, :, :], table_hi[:, :, :].bitcast(FP32), ALU.subtract)\
                .then_inc(table_lo_done, 1)
            for k in range(KC):
                dve.wait_ge(in_hi_done, 2 * KC + k + 1)
                nc.vector.tensor_tensor(ctx_lo[:, k, :], ctx_raw[:, k, :], ctx_hi[:, k, :].bitcast(FP32), ALU.subtract)\
                    .then_inc(in_lo_done, 1)
            dve.wait_ge(in_lo_done, 3 * KC)
            nc.vector.memset(acc[:, :, :], 0.0).then_inc(acc_zeroed, 1)
            dve.wait_ge(mask_in, 16)
            link(nc.vector.tensor_scalar(mask_tmp[:, :, :], mask_i[:, :, :], 0.0, MASKED, ALU.is_equal, ALU.mult))
            link(nc.vector.tensor_scalar(cap[:, :, :], mask_i[:, :, :], 0.0, UNMASKED, ALU.not_equal, ALU.mult))
            link(nc.vector.tensor_tensor(cap[:, :, :], cap[:, :, :], mask_tmp[:, :, :], ALU.add))
            dve.wait_ge(acc_zeroed, 1)
            wait_job(dve, J_TABLES + 1)
            dve.wait_ge(decay_in, 16)
            dve.wait_ge(small_in, 32)

            def decayed(h, free):
                dve.wait_ge(scores_done, h + 1)
                if free is not None:
                    dve.wait_ge(pv_done, free)
                nc.vector.tensor_tensor(probs[:, :, :], bank_view(ps_s, P),
                                        decay_sb[:, bass.ds(h, 1), :].broadcast_to([P, BATCH, P]),
                                        ALU.mult).then_inc(probs_done, 1)

            def finish_gate(jb):
                wait_out_of_slot(dve, jb)
                nc.vector.tensor_scalar(gate[:, :], gate[:, :], 0.5, 0.5, ALU.mult, ALU.add).then_inc(gate_done, 1)

            def gated(h, free):
                dve.wait_ge(squares_done, h + 1)
                dve.wait_ge(gate_done, h + 1)
                if free is not None:
                    dve.wait_ge(y_lo_done, free)
                nc.vector.scalar_tensor_tensor(out=y_raw[:, :], in0=ps_o[:, :], scalar=nw[:, bass.ds(h, 1)],
                                               in1=gate[:, :], op0=ALU.mult, op1=ALU.mult).then_inc(y_done, 1)

            def y_lo_of(h, hd):
                dve.wait_ge(y_hi_done, h + 1)
                nc.vector.tensor_tensor(y_lo[:, hd, :], y_raw[:, :], y_hi[:, hd, :].bitcast(FP32), ALU.subtract)\
                    .then_inc(y_lo_done, 1)

            def add_out(c, jb):
                wait_job(dve, jb[2])
                nc.vector.tensor_tensor(acc[:, 2 * c:2 * c + 2, :], acc[:, 2 * c:2 * c + 2, :],
                                        bank_view(proj[jb[0]], DIM), ALU.add).then_inc(evacuated[jb[0]], 1)

            def back(i):
                free = None if isinstance(i, int) and i == 0 else i * 2
                decayed(i * 2, free)
                finish_gate(job(J_LOOP_A, JOBS_PAIR, i, 2))
                decayed(i * 2 + 1, i * 2 + 1)
                gated(i * 2, free)
                y_lo_of(i * 2, 0)
                finish_gate(job(J_LOOP_A, JOBS_PAIR, i, 3))
                gated(i * 2 + 1, i * 2 + 1)
                y_lo_of(i * 2 + 1, 1)

            back(0)
            for c in range(4):
                add_out(c, one_job(J_LOOP_A + 8 + c))
            with dve.Fori(1, PAIRS - 1) as i:
                back(i)
                for c in range(4):
                    add_out(c, job(J_LOOP_A, JOBS_PAIR, i, 8 + c))
            back(PAIRS - 1)

            def rsqrt(n, cols):
                dve.wait_ge(std_done, n + 1)
                link(nc.vector.reciprocal(rstd[:, cols], std[:, cols]))
                link(nc.vector.tensor_tensor(newton[:, cols], rstd[:, cols], rstd[:, cols], ALU.mult))
                link(nc.vector.tensor_tensor(newton[:, cols], newton[:, cols], var_e[:, cols], ALU.mult))
                link(nc.vector.tensor_scalar(newton[:, cols], newton[:, cols], -0.5, 1.5, ALU.mult, ALU.add))
                link(nc.vector.tensor_tensor(rstd[:, cols], rstd[:, cols], newton[:, cols], ALU.mult))

            def ln_variance(g, jobs):
                for jb in jobs:
                    wait_out_of_slot(dve, jb)
                for c in range(4 * g, 4 * g + 4):
                    last = nc.vector.bn_stats(stats[:, c, :], acc[:, c, :])
                link(last)
                for c in range(4 * g, 4 * g + 4):
                    last = nc.vector.bn_aggr(mean_var[:, c, :], stats[:, c, :])
                link(last)
                nc.vector.tensor_scalar(var_e[:, 4 * g:4 * g + 4], mean_var[:, 4 * g:4 * g + 4, 1], LN_EPS, None,
                                        ALU.add).then_inc(var_done, 1)

            def ln_shift(ln, g):
                cols = slice(4 * g, 4 * g + 4)
                rsqrt(2 * ln + g + 1, cols)
                nc.vector.scalar_tensor_tensor(out=shift[:, cols], in0=mean_var[:, cols, 0], scalar=-1.0,
                                               in1=rstd[:, cols], op0=ALU.mult, op1=ALU.mult).then_inc(shift_done, 1)

            def turned_lo(tensor, c2, done):
                for c in range(2):
                    tok = slice((2 * c2 + c) * P, (2 * c2 + c + 1) * P)
                    last = nc.vector.tensor_tensor(xt_lo[:, :, tok], turned_view(tensor, c),
                                                   xt_hi[:, :, tok].bitcast(FP32), ALU.subtract)
                last.then_inc(done, 1)

            def early_lo(ln, jobs):
                for c2 in range(2):
                    dve.wait_ge(xt_hi_done, 2 * ln + c2 + 1)
                    turned_lo(proj[(jobs + c2) % 2], c2, evacuated[(jobs + c2) % 2])

            def late_lo(ln):
                for n, tensor in enumerate((ps_s, ps_o)):
                    dve.wait_ge(late_hi_done, 2 * ln + n + 1)
                    turned_lo(tensor, 2 + n, late_taken)

            def residual(g, jobs):
                for jb in jobs:
                    wait_out_of_slot(dve, jb)
                for c in range(4 * g, 4 * g + 4):
                    last = nc.vector.scalar_tensor_tensor(out=acc[:, c, :], in0=acc[:, c, :], scalar=rstd[:, c:c + 1],
                                                          in1=x_res[:, c, :], op0=ALU.mult, op1=ALU.add)
                link(last)

            outs = [one_job(J_END_A - 4 + c) for c in range(4)]
            add_out(0, outs[0])
            add_out(1, outs[1])
            dve.wait_ge(ms_done, 1)
            nc.vector.tensor_scalar(var_e[:, :], ps_o[:, 0:BATCH], 1.0 / (HEADS * P), RMS_EPS, ALU.mult, ALU.add)\
                .then_inc(var_done, 1)
            add_out(2, outs[2])
            rsqrt(0, slice(0, BATCH))
            dve.wait_ge(res_in, 16)
            residual(0, outs[0:2])
            ln_variance(0, [])
            add_out(3, outs[3])
            ln_shift(0, 0)

            def rope_part(r, jb, h):
                dve.wait_ge(swap_done, r * 2 + (h + 1))
                if h == 0 and not (isinstance(r, int) and r == 0):
                    dve.wait_ge(rope_done, r)
                ins = nc.vector.tensor_tensor(cosed[:, half(h)], proj[jb[0]][:, half(h)], cos_t[:, half(h)], ALU.mult)
                if h == 1:
                    ins.then_inc(evacuated[jb[0]], 1)
                ins = nc.vector.tensor_tensor(rot[:, half(h)], swapped[:, half(h)], sin_t[:, half(h)], ALU.mult)
                if h == 1:
                    ins.then_inc(sin_done, 1)

            def rope_sum(r, dst, free):
                dve.wait_ge(sin_done, r + 1)
                dve.wait_ge(scores_done, free)
                nc.vector.tensor_tensor(dst[:, :], cosed[:, :], rot[:, :], ALU.add).then_inc(rope_done, 1)

            def cap_and_max(h, t_before):
                dve.wait_ge(scores_done, h + (HEADS + 1))
                if t_before is not None:
                    wait_job(dve, t_before)
                nc.vector.tensor_tensor(pb[:, :, :], bank_view(ps_s, P), cap[:, :, :], ALU.min).then_inc(masked, 1)
                dve.wait_ge(masked, h + 1)
                nc.vector.tensor_reduce(row_max[:, :], pb[:, :, :], AX.X, ALU.max).then_inc(max_done, 1)
                dve.wait_ge(max_done, h + 1)
                nc.vector.tensor_scalar(neg_max[:, :], row_max[:, :], -SM_SCALE, None, ALU.mult)\
                    .then_inc(neg_max_done, 1)

            def normalise(h):
                dve.wait_ge(exp_done, h + 1)
                nc.vector.reciprocal(row_inv[:, :], row_sum[:, :]).then_inc(inv_done, 1)
                dve.wait_ge(inv_done, h + 1)
                nc.vector.tensor_tensor(pb[:, :, :], pb[:, :, :],
                                        row_inv[:, :].unsqueeze(2).broadcast_to([P, BATCH, P]),
                                        ALU.mult).then_inc(soft_done, 1)

            def y_lo_cross(h, hd):
                dve.wait_ge(y_hi_done, h + (HEADS + 1))
                nc.vector.tensor_tensor(y_lo[:, hd, :], ps_o[:, :], y_hi[:, hd, :].bitcast(FP32), ALU.subtract)\
                    .then_inc(y_lo_done, 1)

            dve.wait_ge(pv_done, HEADS)
            dve.wait_ge(y_done, HEADS)
            residual(1, outs[2:4])
            ln_variance(1, [])
            rope_part(0, one_job(J_K0), 0)
            rope_part(0, one_job(J_K0), 1)
            early_lo(0, J_LN1)
            rope_sum(0, kr, HEADS)
            ln_shift(0, 1)
            rope_part(1, one_job(J_Q0), 0)
            late_lo(0)
            rope_part(1, one_job(J_Q0), 1)
            rope_sum(1, qr, HEADS)
            dve.wait_ge(normed, BATCH)
            cap_and_max(0, None)
            rope_part(2, one_job(J_Q1), 0)
            normalise(0)
            rope_part(2, one_job(J_Q1), 1)
            rope_sum(2, qr, HEADS + 1)
            cap_and_max(1, J_T0)
            rope_part(3, one_job(J_Q2), 0)
            normalise(1)
            rope_part(3, one_job(J_Q2), 1)
            rope_sum(3, qr, HEADS + 2)
            y_lo_cross(0, 0)

            def heads_2_3(i, last):
                g = i * GROUP
                r = at(R_LOOP_B, ROPES_KV, i, 0)
                jb = [job(J_LOOP_B, JOBS_KV, i, j) for j in range(-1, 9)]
                t1, q3, kn, t2, q0, outs = (jb[0], jb[1], None, jb[2], None, jb[3:7]) if last else \
                    (jb[0], jb[1], jb[2], jb[3], jb[4], jb[5:9])
                cap_and_max(g + 2, t1[2])
                rope_part(r, q3, 0)
                normalise(g + 2)
                rope_part(r, q3, 1)
                rope_sum(r, qr, g + (HEADS + 3))
                y_lo_cross(g + 1, 1)
                if not last:
                    rope_part(r + 1, kn, 0)
                    rope_part(r + 1, kn, 1)
                cap_and_max(g + 3, t2[2])
                if not last:
                    rope_sum(r + 1, kr, g + (HEADS + 4))
                    rope_part(r + 2, q0, 0)
                normalise(g + 3)
                if not last:
                    rope_part(r + 2, q0, 1)
                    rope_sum(r + 2, qr, g + (HEADS + 4))
                for c in range(4):
                    add_out(c, outs[c])
                y_lo_cross(g + 2, 0)

            with dve.Fori(0, KV_HEADS - 1) as i:
                heads_2_3(i, False)
                g = i * GROUP
                r = at(R_LOOP_B, ROPES_KV, i, 3)
                jb = [job(J_LOOP_B, JOBS_KV, i, j) for j in range(JOBS_KV)]
                cap_and_max(g + 4, jb[8][2])
                rope_part(r, jb[9], 0)
                normalise(g + 4)
                rope_part(r, jb[9], 1)
                rope_sum(r, qr, g + (HEADS + 5))
                y_lo_cross(g + 3, 1)
                cap_and_max(g + 5, jb[11][2])
                rope_part(r + 1, jb[12], 0)
                normalise(g + 5)
                rope_part(r + 1, jb[12], 1)
                rope_sum(r + 1, qr, g + (HEADS + 6))
                for c in range(4):
                    add_out(c, jb[13 + c])
                y_lo_cross(g + 4, 0)
            heads_2_3(KV_HEADS - 1, True)
            y_lo_cross(HEADS - 1, 1)

            def last_outs(outs, ln):
                add_out(0, outs[0])
                add_out(1, outs[1])
                ln_variance(0, outs[0:2])
                add_out(2, outs[2])
                ln_shift(ln, 0)
                add_out(3, outs[3])
                ln_variance(1, outs[2:4])

            last_outs([one_job(J_TAIL_B + c) for c in range(4)], 1)
            early_lo(1, J_LN2)
            ln_shift(1, 1)
            late_lo(1)
            dve.wait_ge(normed, 2 * BATCH)

            def gate_up(c, gate_job, up_job):
                wait_out_of_slot(dve, gate_job)
                wait_job(dve, up_job[2])
                dve.wait_ge(y_lo_done, c + 2 * HEADS)
                nc.vector.tensor_tensor(mid[:, :], proj[up_job[0]][:, :], g_act[:, :], ALU.mult)\
                    .then_inc(evacuated[up_job[0]], 1)

            def mid_lo(c):
                dve.wait_ge(y_hi_done, c + (2 * HEADS + 1))
                nc.vector.tensor_tensor(y_lo[:, 0, :], mid[:, :], y_hi[:, 0, :].bitcast(FP32), ALU.subtract)\
                    .then_inc(y_lo_done, 1)

            gate_up(0, one_job(J_F0), one_job(J_F0 + 1))
            mid_lo(0)
            with dve.Fori(0, HCHUNKS - 1) as i:
                jb = [job(J_LOOP_F, JOBS_F, i, j) for j in range(JOBS_F)]
                add_out(0, jb[1])
                add_out(1, jb[2])
                gate_up(i + 1, jb[0], jb[3])
                add_out(2, jb[4])
                add_out(3, jb[5])
                mid_lo(i + 1)
            last_outs([one_job(J_TAIL_F + c) for c in range(4)], 2)
            ln_shift(2, 1)

        @block.tensor
        def _(pe):
            def split_product(ps, stationary, moving, k, count):
                (s_hi, s_lo), (m_hi, m_lo) = stationary, moving
                nc.tensor.matmul(ps, s_hi, m_hi, start=(k == 0), stop=False)
                nc.tensor.matmul(ps, s_hi, m_lo, start=False, stop=False)
                return nc.tensor.matmul(ps, s_lo, m_hi, start=False, stop=(k == count - 1))

            def begin(jb, unit):
                if not (isinstance(jb[1], int) and jb[1] == 0):
                    pe.wait_ge(evacuated[jb[0]], jb[1])
                if unit is not None:
                    pe.wait_ge(w_lo_done, unit + 1)

            def channels_half(jb, slot, x_hi, x_lo, h):
                for k in range(KC):
                    cols = slice(k * P, (k + 1) * P)
                    last = split_product(proj[jb[0]][:, half(h)], (w_hi[:, slot, cols], w_lo[:, slot, cols]),
                                         (x_hi[:, k, half(h)], x_lo[:, k, half(h)]), k, KC)
                return last

            def channels(jb, unit, slot, x_hi, x_lo, halved=False):
                begin(jb, unit)
                last = channels_half(jb, slot, x_hi, x_lo, 0)
                if halved:
                    last.then_inc(first_half, 1)
                channels_half(jb, slot, x_hi, x_lo, 1).then_inc(jobs_done, 1)

            def values(jb, unit, slots, part):
                begin(jb, unit)
                for b in range(4):
                    tok = slice((4 * part + b) * P, (4 * part + b + 1) * P)
                    for k in range(KC):
                        cols = slice(k % 2 * 2 * P, (k % 2 + 1) * 2 * P)
                        s = slots[k // 2]
                        last = split_product(proj[jb[0]][:, b * 2 * P:(b + 1) * 2 * P],
                                             (xt_hi[:, k, tok], xt_lo[:, k, tok]),
                                             (w_hi[:, s, cols], w_lo[:, s, cols]), k, KC)
                last.then_inc(jobs_done, 1)

            def output(jb, c, unit, slots, heads_ready):
                begin(jb, unit)
                if heads_ready is not None:
                    pe.wait_ge(y_lo_done, heads_ready)
                for b in range(2):
                    tok = slice((2 * c + b) * P, (2 * c + b + 1) * P)
                    for hd, s in enumerate(slots):
                        last = split_product(proj[jb[0]][:, b * DIM:(b + 1) * DIM],
                                             (y_hi[:, hd, tok], y_lo[:, hd, tok]),
                                             (w_hi[:, s, :], w_lo[:, s, :]), hd, len(slots))
                last.then_inc(jobs_done, 1)

            def slot_a(j):
                return (U_LOOP_A + j) % RING

            def front(unit, jobs, slots, in_lo=None):
                values(jobs[0], unit + 1, slots[0:2], 0)
                if in_lo is not None:
                    pe.wait_ge(in_lo_done, in_lo)
                values(jobs[1], None, slots[0:2], 1)
                channels(jobs[2], unit + 2, slots[2], xt_hi, xt_lo)
                channels(jobs[3], unit + 3, slots[3], xt_hi, xt_lo)

            def scores(h, q_job, k_job, free):
                wait_out_of_slot(pe, q_job)
                wait_out_of_slot(pe, k_job)
                if free is not None:
                    pe.wait_ge(probs_done, free)
                for b in range(BATCH):
                    tok = slice(b * P, (b + 1) * P)
                    last = nc.tensor.matmul(ps_s[:, tok], k_sb[:, tok], q_sb[:, tok], start=True, stop=True)
                last.then_inc(scores_done, 1)

            def times_v(h, hd, free):
                pe.wait_ge(probs_done, h + 1)
                if free is not None:
                    pe.wait_ge(y_done, free)
                for b in range(BATCH):
                    last = nc.tensor.matmul(ps_o[:, b * P:(b + 1) * P], v_sb[:, b, hd * P:(hd + 1) * P],
                                            probs[:, b, :], start=True, stop=True)
                last.then_inc(pv_done, 1)

            def back(i, first):
                jb = [job(J_LOOP_A, JOBS_PAIR, i, j) for j in range(4)]
                u = at(U_LOOP_A, UNITS_PAIR, i, 0)
                v_a, v_b, q_a, k_a = [one_job(J_FRONT0 + j) for j in range(4)] if first else \
                    [job(J_LOOP_A, JOBS_PAIR, i, j) for j in (-8, -7, -6, -5)]
                scores(i * 2, q_a, k_a, None if first else i * 2)
                channels(jb[0], u, slot_a(0), xt_hi, xt_lo)
                wait_out_of_slot(pe, v_a)
                wait_out_of_slot(pe, v_b)
                times_v(i * 2, 0, None if first else i * 2)
                channels(jb[1], u + 1, slot_a(1), xt_hi, xt_lo)
                channels(jb[2], u + 2, slot_a(2), xt_hi, xt_lo)
                scores(i * 2 + 1, jb[0], jb[1], i * 2 + 1)
                channels(jb[3], u + 3, slot_a(3), xt_hi, xt_lo)
                times_v(i * 2 + 1, 1, i * 2 + 1)

            def next_front_and_out(i):
                jb = [job(J_LOOP_A, JOBS_PAIR, i, j) for j in range(JOBS_PAIR)]
                u = at(U_LOOP_A, UNITS_PAIR, i, 0)
                front(u + 4, jb[4:8], [slot_a(j) for j in range(4, 8)])
                for c in range(4):
                    output(jb[8 + c], c, u + 9, [slot_a(8), slot_a(9)], i * 2 + 2)

            pe.wait_ge(in_lo_done, KC)
            front(U_FRONT0, [one_job(J_FRONT0 + j) for j in range(4)], [0, 1, 2, 3], 2 * KC)
            pe.wait_ge(table_lo_done, 1)
            pe.wait_ge(onehot_done, 4)
            for t in range(2):
                jb = one_job(J_TABLES + t)
                begin(jb, None)
                for h in range(2):
                    for c in range(4):
                        cols = slice(t * P, (t + 1) * P)
                        nc.tensor.matmul(proj[jb[0]][:, half(h)], table_hi[:, c, cols], onehot[:, c, half(h)],
                                         start=(c == 0), stop=False)
                        last = nc.tensor.matmul(proj[jb[0]][:, half(h)], table_lo[:, c, cols],
                                                onehot[:, c, half(h)], start=False, stop=(c == 3))
                last.then_inc(jobs_done, 1)
            back(0, True)
            next_front_and_out(0)
            with pe.Fori(1, PAIRS - 1) as i:
                back(i, False)
                next_front_and_out(i)
            back(PAIRS - 1, False)
            for c in range(2):
                output(one_job(J_END_A - 4 + c), c, U_B - 1, [slot_a(4), slot_a(5)], HEADS)
            pe.wait_ge(sq_sum_done, HEADS + 1)
            pe.wait_ge(y_done, HEADS)
            for b in range(BATCH):
                last = nc.tensor.matmul(ps_o[:, b:b + 1], sq_sum[:, b * P:(b + 1) * P], ones, start=True, stop=True)
            last.then_inc(ms_done, 1)
            for c in range(2, 4):
                output(one_job(J_END_A - 4 + c), c, None, [slot_a(4), slot_a(5)], None)

            def turn(tensor, c2, ln, done):
                pe.wait_ge(normed, BATCH * ln + 2 * c2 + 2)
                for c in range(2):
                    for k in range(KC):
                        last = nc.tensor.transpose(turned_view(tensor, c)[:, k, :],
                                                   acc[:, 2 * c2 + c, k * P:(k + 1) * P], ident)
                last.then_inc(done, 1)

            def turn_early(ln, jobs):
                for c2 in range(2):
                    begin(one_job(jobs + c2), None)
                    turn(proj[(jobs + c2) % 2], c2, ln, jobs_done)

            def turn_late(ln):
                for n, tensor in enumerate((ps_s, ps_o)):
                    turn(tensor, 2 + n, ln, late_turned)

            def first_halves(jobs, units, slots, early_jobs, halved):
                for jb, u, s in zip(jobs, units, slots):
                    for n in range(2):
                        wait_out_of_slot(pe, one_job(early_jobs + n))
                    begin(jb, u)
                    last = channels_half(jb, s, xt_hi, xt_lo, 0)
                    if halved:
                        last.then_inc(first_half, 1)

            def second_halves(jobs, slots, ln):
                pe.wait_ge(late_taken, 2 * ln + 2)
                for jb, s in zip(jobs, slots):
                    channels_half(jb, s, xt_hi, xt_lo, 1).then_inc(jobs_done, 1)

            def cross_scores(h, r_q):
                pe.wait_ge(rope_done, r_q + 1)
                if not (isinstance(h, int) and h == 0):
                    pe.wait_ge(masked, h)
                for b in range(BATCH):
                    tok = slice(b * P, (b + 1) * P)
                    last = nc.tensor.matmul(ps_s[:, tok], qr[:, tok], kr[:, tok], start=True, stop=True)
                last.then_inc(scores_done, 1)

            def turn_probs(h, jb):
                begin(jb, None)
                pe.wait_ge(soft_done, h + 1)
                for b in range(BATCH):
                    last = nc.tensor.transpose(proj[jb[0]][:, b * P:(b + 1) * P], pb[:, b, :], ident)
                last.then_inc(jobs_done, 1)

            def times_vx(h, t_job, free):
                wait_out_of_slot(pe, t_job)
                pe.wait_ge(y_lo_done, free)
                for b in range(BATCH):
                    last = nc.tensor.matmul(ps_o[:, b * P:(b + 1) * P], vx[:, b, :], pt[:, b, :],
                                            start=True, stop=True)
                last.then_inc(pv_done, 1)

            def turn_v(i, jb):
                wait_out_of_slot(pe, jb)
                pe.wait_ge(y_lo_done, i * GROUP + HEADS)
                for b in range(BATCH):
                    last = nc.tensor.transpose(ps_o[:, b * P:(b + 1) * P], vt[:, b * P:(b + 1) * P], ident)
                last.then_inc(vt_turned, 1)

            pe.wait_ge(in_lo_done, 3 * KC)
            channels(one_job(J_K0), U_B, U_B % RING, ctx_hi, ctx_lo, True)
            turn_early(0, J_LN1)
            first_halves([one_job(J_Q0)], [U_B + 1], [(U_B + 1) % RING], J_LN1, True)
            begin(one_job(J_V0), U_B + 2)
            channels_half(one_job(J_V0), (U_B + 2) % RING, ctx_hi, ctx_lo, 0).then_inc(first_half, 1)
            pe.wait_ge(var_done, 1)
            turn_late(0)
            second_halves([one_job(J_Q0)], [(U_B + 1) % RING], 0)
            channels_half(one_job(J_V0), (U_B + 2) % RING, ctx_hi, ctx_lo, 1).then_inc(jobs_done, 1)
            turn_v(0, one_job(J_V0))
            cross_scores(0, 1)
            channels(one_job(J_Q1), U_B + 3, (U_B + 3) % RING, xt_hi, xt_lo, True)
            turn_probs(0, one_job(J_T0))
            cross_scores(1, 2)
            channels(one_job(J_Q2), U_B + 4, (U_B + 4) % RING, xt_hi, xt_lo, True)
            pe.wait_ge(v_ready, 1)
            times_vx(0, one_job(J_T0), HEADS)
            turn_probs(1, one_job(J_T1))

            def slot_b(j):
                return (U_LOOP_B + j) % RING

            def heads_2_3(i, last):
                g = i * GROUP
                r = at(R_LOOP_B, ROPES_KV, i, 0)
                u = at(U_LOOP_B, UNITS_KV, i, 0)
                jb = [job(J_LOOP_B, JOBS_KV, i, j) for j in range(-1, 9)]
                t1, q3, kn, t2, q0, outs, t3 = (jb[0], jb[1], None, jb[2], None, jb[3:7], jb[7]) if last else \
                    (jb[0], jb[1], jb[2], jb[3], jb[4], jb[5:9], jb[9])
                o = 1 if last else 3
                cross_scores(g + 2, r - 1)
                channels(q3, u, slot_b(0), xt_hi, xt_lo, True)
                times_vx(g + 1, t1, g + (HEADS + 1))
                if not last:
                    channels(kn, u + 1, slot_b(1), ctx_hi, ctx_lo, True)
                turn_probs(g + 2, t2)
                cross_scores(g + 3, r)
                if not last:
                    channels(q0, u + 2, slot_b(2), xt_hi, xt_lo, True)
                output(outs[0], 0, u + (o + 1), [slot_b(o), slot_b(o + 1)], g + (HEADS + 2))
                times_vx(g + 2, t2, g + (HEADS + 2))
                for c in range(1, 4):
                    output(outs[c], c, None, [slot_b(o), slot_b(o + 1)], None)
                turn_probs(g + 3, t3)

            with pe.Fori(0, KV_HEADS - 1) as i:
                heads_2_3(i, False)
                g = i * GROUP
                r = at(R_LOOP_B, ROPES_KV, i, 0)
                u = at(U_LOOP_B, UNITS_KV, i, 0)
                jb = [job(J_LOOP_B, JOBS_KV, i, j) for j in range(JOBS_KV)]
                cross_scores(g + 4, r + 2)
                channels(jb[9], u + 5, slot_b(5), xt_hi, xt_lo, True)
                times_vx(g + 3, jb[8], g + (HEADS + 3))
                channels(jb[10], u + 6, slot_b(6), ctx_hi, ctx_lo, True)
                turn_probs(g + 4, jb[11])
                turn_v(i + 1, jb[10])
                cross_scores(g + 5, r + 3)
                channels(jb[12], u + 7, slot_b(7), xt_hi, xt_lo, True)
                output(jb[13], 0, u + 9, [slot_b(8), slot_b(9)], g + (HEADS + 4))
                pe.wait_ge(v_ready, i + 2)
                times_vx(g + 4, jb[11], g + (HEADS + 4))
                for c in range(1, 4):
                    output(jb[13 + c], c, None, [slot_b(8), slot_b(9)], None)
                turn_probs(g + 5, jb[17])
            heads_2_3(KV_HEADS - 1, True)
            times_vx(HEADS - 1, one_job(J_TAIL_B - 1), 2 * HEADS - 1)
            for c in range(4):
                output(one_job(J_TAIL_B + c), c, U_F - 1, [slot_b(3), slot_b(4)], 2 * HEADS)

            turn_early(1, J_LN2)
            gate_up = [one_job(J_F0), one_job(J_F0 + 1)]
            first_halves(gate_up, [U_F, U_F + 1], [0, 1], J_LN2, False)
            turn_late(1)
            second_halves(gate_up, [0, 1], 1)

            def slot_f(j):
                return (UF_LOOP + j) % RING_F

            with pe.Fori(0, HCHUNKS - 1) as i:
                jb = [job(J_LOOP_F, JOBS_F, i, j) for j in range(JOBS_F)]
                u = at(U_F + UF_LOOP, UNITS_F, i, 0)
                channels(jb[0], u, slot_f(0), xt_hi, xt_lo)
                output(jb[1], 0, u + 2, [slot_f(2)], i + (2 * HEADS + 1))
                output(jb[2], 1, None, [slot_f(2)], None)
                channels(jb[3], None, slot_f(1), xt_hi, xt_lo)
                output(jb[4], 2, None, [slot_f(2)], None)
                output(jb[5], 3, None, [slot_f(2)], None)
            for c in range(4):
                output(one_job(J_TAIL_F + c), c, U_F + UF_TOTAL - 1, [(UF_TOTAL - 1) % RING_F],
                       2 * HEADS + HCHUNKS)


def _decay_table():
    layer, layers = 1, 32
    base = 1.0 / 2.0 ** (8.0 / HEADS)
    slope = base ** (np.arange(HEADS, dtype=np.float32) + 1.0) * (1.0 - layer / (layers - 1 + 1e-05) + 1e-05)
    diff = np.arange(P)[None, :] - np.arange(P)[:, None]
    table = np.exp(-slope.astype(np.float64)[None, :, None] * np.maximum(diff, 0)[:, None, :])
    return (table * (diff >= 0)[:, None, :]).astype(np.float32)


def _rope_table():
    inv = (1.0 / ROPE_THETA ** (np.arange(0, P, 2, dtype=np.float32) / np.float32(P))).astype(np.float32)
    freqs = np.arange(POSITIONS, dtype=np.float32)[:, None] * inv[None, :]
    cos, sin = np.cos(freqs), np.sin(freqs)
    table = np.concatenate([cos, cos, -sin, sin], axis=1).astype(np.float32)
    return np.ascontiguousarray(table.reshape(4, P, 2 * P).transpose(1, 0, 2))


def _consts():
    iota = np.arange(POSITIONS, dtype=np.float32).reshape(4, P).T
    return np.concatenate([np.eye(P, dtype=np.float32), iota, np.ones((P, 1), np.float32)], axis=1)


def _in_rows(w):
    return w.reshape(KC, P, -1).transpose(1, 0, 2)


def _weight_stream(qkv_w, gate_w, out_w, wq, wk, wv, wo):
    qkv = qkv_w.reshape(HEADS, 3, P, DIM)

    def head(w):
        return _in_rows(w).reshape(P, DIM)

    units = []

    def front(i):
        v = _in_rows(qkv[2 * i:2 * i + 2, 2].reshape(2 * P, DIM).T)
        units.extend([v[:, 0:2].reshape(P, DIM), v[:, 2:4].reshape(P, DIM), head(qkv[2 * i, 0].T), head(qkv[2 * i, 1].T)])

    def back(i):
        units.extend([head(qkv[2 * i + 1, 0].T), head(qkv[2 * i + 1, 1].T)])
        units.extend(head(gate_w[h * P:(h + 1) * P].T) for h in (2 * i, 2 * i + 1))

    def out(i):
        units.extend(out_w[:, h * P:(h + 1) * P].T for h in (2 * i, 2 * i + 1))

    front(0)
    for i in range(PAIRS):
        back(i)
        if i + 1 < PAIRS:
            front(i + 1)
        out(i)

    def of(w, h):
        return head(w[:, h * P:(h + 1) * P])

    def rows(h):
        return [wo[n * P:(n + 1) * P] for n in (h, h + 1)]

    units += [of(wk, 0), of(wq, 0), of(wv, 0), of(wq, 1), of(wq, 2)]
    for i in range(KV_HEADS):
        g, more = GROUP * i, i + 1 < KV_HEADS
        units += [of(wq, g + 3)] + ([of(wk, i + 1), of(wq, g + 4)] if more else []) + rows(g)
        units += [of(wq, g + 5), of(wv, i + 1), of(wq, g + 6)] if more else []
        units += rows(g + 2)
    return np.stack(units)


def _ffn_stream(w_gate, w_up, w_down):
    pad = HCHUNKS * P - HIDDEN
    gate, up = (np.pad(w, ((0, pad), (0, 0))) for w in (w_gate, w_up))
    down = np.pad(w_down, ((0, 0), (0, pad)))
    units = []

    def cols(w, c):
        return _in_rows(w[c * P:(c + 1) * P].T).reshape(P, DIM)

    for c in range(HCHUNKS):
        units += [cols(gate, c), cols(up, c)]
        if c:
            units.append(down[:, (c - 1) * P:c * P].T)
    units.append(down[:, -P:].T)
    return np.stack(units)


def kernel(**inputs):
    import concourse.bacc as bacc
    from concourse.bass_utils import run_bass_kernel_spmd

    a = {k: np.asarray(v) for k, v in inputs.items()}
    x, ctx = a["x"], a["ctx_4096"]
    arrays = {
        "x_t": _in_rows(x.reshape(TOK, DIM).T),
        "x_rows": x.transpose(1, 0, 2),
        "ctx_t": _in_rows(ctx.reshape(TOK, DIM).T),
        "pos": a["pos_BxS2"].reshape(TOK),
        "mask": a["mask_BxSxS2_ik0"].transpose(1, 0, 2),
        "weights": _weight_stream(a["L0_attn_qkv_w"], a["L0_attn_gate_w"], a["L0_attn_out_w"], a["L0_xattn_Wq"],
                                  a["L0_xattn_Wk"], a["L0_xattn_Wv"], a["L0_xattn_Wo"]),
        "ffn_weights": _ffn_stream(a["L0_ffn_w_gate"], a["L0_ffn_w_up"], a["L0_ffn_w_down"]),
        "ffn_scales": np.tile(np.stack([a["L0_ffn_scale_gate"], a["L0_ffn_scale_up"], a["L0_ffn_scale_down"]])
                              .reshape(1, 3), (P, 1)),
        "norm_w": a["L0_attn_norm_w"].reshape(HEADS, P).T,
        "decay": _decay_table(),
        "rope_table": _rope_table(),
        "consts": _consts(),
    }
    arrays = {k: np.ascontiguousarray(v) for k, v in arrays.items()}
    nc = bacc.Bacc("TRN2", target_bir_lowering=False, num_devices=1)
    args = [nc.dram_tensor(k, v.shape, mybir.dt.from_np(v.dtype), kind="ExternalInput").ap()
            for k, v in arrays.items()]
    out = nc.dram_tensor("out", [BATCH, SEQ, DIM], FP32, kind="ExternalOutput").ap()
    build(nc, *args, out)
    r = run_bass_kernel_spmd(nc, [arrays], core_ids=[0])
    return r.results[0]["out"]
```

```python
import numpy as np

import concourse.bass as bass
from concourse import mybir

FP32 = mybir.dt.float32
FP32R = mybir.dt.float32r
INT32 = mybir.dt.int32
ALU = mybir.AluOpType
ACT = mybir.ActivationFunctionType
AX = mybir.AxisListType

P = 128
BATCH, SEQ, DIM = 8, 128, 512
TOK = BATCH * SEQ
KC = DIM // P
HEADS = 32
PAIRS = HEADS // 2
KV_HEADS = 8
GROUP = HEADS // KV_HEADS
HIDDEN = 1376
HCHUNKS = -(-HIDDEN // P)
POSITIONS = 512
ROPE_THETA = 10000.0
LN_EPS = 1e-5
RMS_EPS = 1e-5
SM_SCALE = float(1.0 / np.sqrt(np.float32(P)))
MASKED = float(-1e9 * np.sqrt(np.float32(P)))
UNMASKED = 3.0e38
HALF = TOK // 2
X_PARTS = (slice(0, 2 * P), slice(2 * P, HALF), slice(HALF, TOK))
RING = 5
RING_F = 3
EXACT = 2048.0


UNITS_PAIR, JOBS_PAIR = 10, 12
U_FRONT0, U_LOOP_A = 0, 4
J_FRONT0 = 0
J_TABLES = J_FRONT0 + 4
J_LOOP_A = J_TABLES + 2
J_OUTS_A = J_LOOP_A + JOBS_PAIR * (PAIRS - 1) + 4
U_B = U_LOOP_A + UNITS_PAIR * (PAIRS - 1) + 6
J_K0 = J_OUTS_A + 4
J_V0, J_Q0, J_Q1, J_T0, J_Q2, J_T1 = (J_K0 + n for n in range(1, 7))
J_LOOP_B = J_T1 + 1
UNITS_KV, JOBS_KV = 10, 18
U_LOOP_B = U_B + 5
ROPES_KV, R_LOOP_B = 5, 4
HALVED_KV, H_LOOP_B = 6, 5
J_LAST_B = J_LOOP_B + JOBS_KV * (KV_HEADS - 1)
J_TAIL_B = J_LAST_B + 7
U_F = U_LOOP_B + UNITS_KV * (KV_HEADS - 1) + 5
J_F0 = J_TAIL_B + 4
J_LOOP_F = J_F0 + 2
UNITS_F, JOBS_F = 3, 4
J_TAIL_F = J_LOOP_F + JOBS_F * (HCHUNKS - 2)
J_OUTS_F = J_TAIL_F + 2
HALVED_JOBS = H_LOOP_B + HALVED_KV * (KV_HEADS - 1) + 1 + 1
UF_LOOP = 2
UF_TOTAL = UF_LOOP + UNITS_F * (HCHUNKS - 1) + 1
SCAN = UF_TOTAL * DIM // PAIRS


def at(base, per, i, j):
    return i * per + (base + j)


def job(base, per, i, j):
    return (base + j) % 2, i * (per // 2) + (base + j) // 2, at(base, per, i, j)


def build(nc, x_t, x_rows, ctx_t, pos, mask, weights, ffn_weights, ffn_scan, ffn_scales, norm_w, decay, rope_table,
          consts, out):
    place_at = [(nc.sbuf_base + 31) // 32 * 32]

    def sb(name, shape, dtype=FP32, offset=None):
        size = 4 * int(np.prod(shape[1:]))
        if offset is None:
            offset = place_at[0]
            place_at[0] += (size + 31) // 32 * 32
            offsets[name] = offset
        return nc.alloc_sbuf_tensor_at(name, shape, dtype, offset=offset)

    offsets = {}
    xt_hi = sb("xt_hi", [P, KC, TOK], FP32R)
    xt_lo = sb("xt_lo", [P, KC, TOK], FP32R)
    ctx_hi = sb("ctx_hi", [P, KC, TOK], FP32R)
    ctx_lo = sb("ctx_lo", [P, KC, TOK], FP32R)
    acc = sb("acc", [P, BATCH, DIM])
    raw = sb("raw", [P, RING, DIM])
    w_hi = sb("w_hi", [P, RING, DIM], FP32R)
    w_lo = sb("w_lo", [P, RING, DIM], FP32R)
    q_sb = sb("q_sb", [P, TOK])
    k_sb = sb("k_sb", [P, TOK])
    v_sb = sb("v_sb", [P, BATCH, 2 * P])
    gate = sb("gate", [P, TOK])
    probs = sb("probs", [P, BATCH, P])
    y_raw = sb("y_raw", [P, TOK])
    squares = sb("squares", [P, TOK])
    sq_sum = sb("sq_sum", [P, TOK])
    y_hi = sb("y_hi", [P, 2, TOK], FP32R)
    y_lo = sb("y_lo", [P, 2, TOK], FP32R)
    decay_sb = sb("decay_sb", [P, HEADS, P])
    cos_t = sb("cos_t", [P, TOK])
    sin_t = sb("sin_t", [P, TOK])
    cap = sb("cap", [P, BATCH, P])
    nw = sb("nw", [P, HEADS])
    scales = sb("scales", [P, 3])
    cst = sb("cst", [P, P + 5])
    stats = sb("stats", [P, BATCH, 6])
    mean_var = sb("mean_var", [P, BATCH, 2])
    var_e = sb("var_e", [P, BATCH])
    std = sb("std", [P, BATCH])
    rms_inv = sb("rms_inv", [P, BATCH])
    shift = sb("shift", [P, BATCH])
    table_lo = sb("table_lo", [P, 4, 2 * P], FP32R)
    rstd = sb("rstd", [P, BATCH])
    newton = sb("newton", [P, BATCH])
    cosed = sb("cosed", [P, TOK])
    row_max = sb("row_max", [P, BATCH])
    neg_max = sb("neg_max", [P, BATCH])
    row_sum = sb("row_sum", [P, BATCH])
    row_inv = sb("row_inv", [P, BATCH])
    scan = sb("scan", [P, SCAN], INT32)
    extremes = sb("extremes", [P, 2, PAIRS])
    widest = sb("widest", [P, 3])
    wide = sb("wide", [P, 1])
    wide_parts = sb("wide_parts", [1, 1], INT32)
    assert place_at[0] <= nc.sbuf_usable_end
    ident, iota, ones = cst[:, 0:P], cst[:, P:P + 4], cst[:, P + 4:P + 5]
    x_raw = sb("x_raw", [P, KC, TOK], offset=offsets["q_sb"])
    ctx_raw = sb("ctx_raw", [P, KC, TOK], offset=offsets["acc"])
    onehot = sb("onehot", [P, 4, TOK], FP32R, offset=offsets["y_hi"])
    pos_i = sb("pos_i", [P, TOK], INT32, offset=offsets["gate"])
    pos_wrap = sb("pos_wrap", [P, TOK], offset=offsets["y_raw"])
    pos_f = sb("pos_f", [P, TOK], offset=offsets["squares"])
    table = sb("table", [P, 4, 2 * P], offset=offsets["cosed"])
    table_hi = sb("table_hi", [P, 4, 2 * P], FP32R, offset=offsets["probs"])
    mask_i = sb("mask_i", [P, BATCH, P], INT32, offset=offsets["cap"])
    mask_tmp = sb("mask_tmp", [P, BATCH, P], offset=offsets["gate"])
    x_res = sb("x_res", [P, BATCH, DIM], offset=offsets["xt_lo"])
    qr = sb("qr", [P, TOK], offset=offsets["q_sb"])
    pb = sb("pb", [P, BATCH, P], offset=offsets["k_sb"])
    rot = sb("rot", [P, TOK], offset=offsets["v_sb"])
    pt = sb("pt", [P, BATCH, P], offset=offsets["v_sb"] + 4 * TOK)
    kr = sb("kr", [P, TOK], offset=offsets["gate"])
    vx = sb("vx", [P, BATCH, P], offset=offsets["probs"])
    swapped = sb("swapped", [P, TOK], offset=offsets["y_raw"])
    vt = sb("vt", [P, TOK], offset=offsets["squares"])
    g_act = sb("g_act", [P, TOK], offset=offsets["q_sb"])
    mid = sb("mid", [P, TOK], offset=offsets["k_sb"])

    proj = [nc.alloc_psum_tensor(f"proj{s}", [P, TOK], FP32) for s in range(2)]
    ps_s = nc.alloc_psum_tensor("ps_s", [P, TOK], FP32)
    ps_o = nc.alloc_psum_tensor("ps_o", [P, TOK], FP32)

    sem = nc.alloc_semaphore
    tables_in = sem("tables_in")
    pos_in = sem("pos_in")
    table_hi_done = sem("table_hi_done")
    table_lo_done = sem("table_lo_done")
    mask_in = sem("mask_in")
    x_in = [sem(f"x_in{n}") for n in range(len(X_PARTS) * KC)]
    ctx_in = [sem(f"ctx_in{k}") for k in range(KC)]
    small_in = sem("small_in")
    decay_in = sem("decay_in")
    res_in = [sem(f"res_in{n}") for n in range(BATCH // 2)]
    raw_in = [sem(f"raw_in{s}") for s in range(RING)]
    rawf_in = [sem(f"rawf_in{s}") for s in range(RING_F)]
    stored = sem("stored")
    w_hi_done = sem("w_hi_done")
    w_lo_done = sem("w_lo_done")
    w_float_done = sem("w_float_done")
    scan_in = sem("scan_in")
    scanned = sem("scanned")
    wide_done = sem("wide_done")
    wide_known = sem("wide_known")
    sums_done = sem("sums_done")
    onehot_done = sem("onehot_done")
    in_hi_done = sem("in_hi_done")
    in_lo_done = sem("in_lo_done")
    acc_zeroed = sem("acc_zeroed")
    jobs_done = sem("jobs_done")
    evacuated = [sem(f"evacuated{s}") for s in range(2)]
    scores_done = sem("scores_done")
    probs_done = sem("probs_done")
    pv_done = sem("pv_done")
    gate_done = sem("gate_done")
    squares_done = sem("squares_done")
    sq_sum_done = sem("sq_sum_done")
    y_done = sem("y_done")
    y_hi_done = sem("y_hi_done")
    y_lo_done = sem("y_lo_done")
    ms_done = sem("ms_done")
    var_done = sem("var_done")
    std_done = sem("std_done")
    rms_done = sem("rms_done")
    acc_scaled = sem("acc_scaled")
    residual_added = sem("residual_added")
    shift_done = sem("shift_done")
    normed_dve = sem("normed_dve")
    normed_act = sem("normed_act")
    first_half = sem("first_half")
    turned = sem("turned")
    turned_hi_done = sem("turned_hi_done")
    turned_taken = sem("turned_taken")
    early_pv_done = sem("early_pv_done")
    early_y_done = sem("early_y_done")
    early_y_hi_done = sem("early_y_hi_done")
    early_y_lo_done = sem("early_y_lo_done")
    swap_done = sem("swap_done")
    sin_done = sem("sin_done")
    rope_done = sem("rope_done")
    masked = sem("masked")
    max_done = sem("max_done")
    neg_max_done = sem("neg_max_done")
    exp_done = sem("exp_done")
    inv_done = sem("inv_done")
    soft_done = sem("soft_done")
    vt_turned = sem("vt_turned")
    v_ready = sem("v_ready")
    dve_step = sem("dve_step")

    def bank_view(tensor, n):
        return tensor[:, :].rearrange("p (b n) -> p b n", n=n)

    def wait_job(eng, n):
        eng.wait_ge(jobs_done, n + 1)

    def wait_out_of_slot(eng, j):
        eng.wait_ge(evacuated[j[0]], j[1] + 1)

    def wait_all_out(eng, n):
        for s in range(2):
            eng.wait_ge(evacuated[s], (n + 1 - s) // 2)

    def one_job(n):
        return n % 2, n // 2, n

    def turned_view(tensor, c):
        return tensor[:, c * DIM:(c + 1) * DIM].rearrange("p (k t) -> p k t", k=KC)

    def half(h):
        return slice(h * HALF, (h + 1) * HALF)

    def four(h):
        return slice(4 * h, 4 * h + 4)

    def wait_normed(eng, ln, c2):
        eng.wait_ge((normed_dve, normed_act)[c2 % 2], 4 * ln + c2 // 2 * 2 + 2)

    with nc.Block() as block:

        @block.sync
        def _(sp):
            def load_unit(unit, slot, lo_before):
                if lo_before is not None:
                    sp.wait_ge(w_lo_done, lo_before)
                sp.dma_start(raw[:, slot, :], weights[unit, :, :].squeeze(0)).then_inc(raw_in[slot], 16)

            def load_x(n):
                for k in range(KC):
                    sp.dma_start(x_raw[:, k, X_PARTS[n]], x_t[:, k, X_PARTS[n]]).then_inc(x_in[n * KC + k], 16)

            for n in range(2):
                load_unit(slice(n, n + 1), n, None)
            for n in range(len(X_PARTS)):
                load_x(n)
            for n in range(2, RING):
                load_unit(slice(n, n + 1), n, None)
            sp.dma_start(pos_i[:, :], pos.partition_broadcast(P)).then_inc(pos_in, 16)
            sp.dma_start(cst[:, :], consts).then_inc(tables_in, 16)
            sp.dma_start(table[:, :, :], rope_table).then_inc(tables_in, 16)
            for n in range(RING, 2 * RING):
                load_unit(slice(n, n + 1), n % RING, n + 1 - RING)
            sp.dma_start(decay_sb[:, :, :], decay).then_inc(decay_in, 16)
            sp.dma_start(nw[:, :], norm_w).then_inc(small_in, 16)
            sp.dma_start(scales[:, :], ffn_scales).then_inc(small_in, 16)
            sp.dma_start(mask_i[:, :, :], mask).then_inc(mask_in, 16)
            for k in range(KC):
                sp.dma_start(ctx_raw[:, k, :], ctx_t[:, k, :]).then_inc(ctx_in[k], 16)
            def load_units(first, end):
                with sp.Fori(first // RING, end // RING) as r:
                    for s in range(RING):
                        load_unit(bass.ds(r * RING + s, 1), s, r * RING + (s + 1 - RING))

            load_units(2 * RING, U_B + RING)
            wait_job(sp, J_OUTS_A - 1)
            for n in range(BATCH // 2):
                pair_of = slice(2 * n, 2 * n + 2)
                sp.dma_start(x_res[:, pair_of, :], x_rows[:, pair_of, :]).then_inc(res_in[n], 16)
            load_units(U_B + RING, U_F)
            ffn_i = raw[:, :, :].bitcast(INT32)
            sp.wait_ge(w_lo_done, U_F)
            for m in range(RING_F):
                sp.dma_start(ffn_i[:, m, :], ffn_weights[m, :, :]).then_inc(rawf_in[m], 16)
            with sp.Fori(1, UF_TOTAL // RING_F) as r:
                for s in range(RING_F):
                    sp.wait_ge(w_lo_done, r * RING_F + (U_F - RING_F + s + 1))
                    sp.dma_start(ffn_i[:, s, :], ffn_weights[bass.ds(r * RING_F + s, 1), :, :].squeeze(0))\
                        .then_inc(rawf_in[s], 16)
            for c in range(BATCH):
                wait_normed(sp, 2, c // 2)
                sp.dma_start(out[c, :, :], acc[:, c, :]).then_inc(stored, 16)
            sp.wait_ge(stored, 16 * BATCH)

        @block.gpsimd
        def _(pool):
            def lo_of_unit(n, s):
                pool.wait_ge(w_hi_done, n + 1)
                nc.gpsimd.tensor_tensor(w_lo[:, s, :], raw[:, s, :], w_hi[:, s, :].bitcast(FP32),
                                        ALU.subtract).then_inc(w_lo_done, 1)

            def add_squares(h):
                pool.wait_ge(squares_done, h + 1)
                pool.wait_ge(sq_sum_done, h + 1)
                nc.gpsimd.tensor_tensor(sq_sum[:, :], sq_sum[:, :], squares[:, :], ALU.add)\
                    .then_inc(sq_sum_done, 1)

            nc.gpsimd.memset(sq_sum[:, :], 0.0).then_inc(sq_sum_done, 1)
            for n in range(U_LOOP_A + RING):
                lo_of_unit(n, n % RING)

            def pair(i, last):
                def lo(j):
                    lo_of_unit(at(U_LOOP_A + RING + j, UNITS_PAIR, i, 0), (U_LOOP_A + RING + j) % RING)
                lo(0)
                add_squares(i * 2)
                for j in range(1, 4):
                    lo(j)
                add_squares(i * 2 + 1)
                if last:
                    for n in range(4):
                        pool.wait_ge(acc_scaled, n + 1)
                        pool.wait_ge(res_in[2 + n // 2], 16)
                        nc.gpsimd.tensor_tensor(acc[:, 4 + n, :], acc[:, 4 + n, :], x_res[:, 4 + n, :], ALU.add)\
                            .then_inc(residual_added, 1)
                for j in range(4, 6 if last else UNITS_PAIR):
                    lo(j)

            with pool.Fori(0, PAIRS - 1) as i:
                pair(i, False)
            pair(PAIRS - 1, True)
            with pool.Fori(U_LOOP_B // RING, U_F // RING) as r:
                for s in range(RING):
                    lo_of_unit(r * RING + s, s)

            with pool.Fori(0, UF_TOTAL // RING_F) as r:
                for s in range(RING_F):
                    lo_of_unit(r * RING_F + (U_F + s), s)

        @block.scalar
        def _(act):
            def hi_of_unit(n, loads):
                s = n[0]
                act.wait_ge(raw_in[s], loads * 16)
                nc.scalar.activation(w_hi[:, s, :], raw[:, s, :], ACT.Copy).then_inc(w_hi_done, 1)

            def pair_unit(i, j):
                n = U_LOOP_A + j
                hi_of_unit((n % RING,), i * (UNITS_PAIR // RING) + (n // RING + 1))

            def kv_unit(i, j):
                n = U_LOOP_B + j
                hi_of_unit((n % RING,), i * (UNITS_KV // RING) + (n // RING + 1))

            def hi_of_x(n):
                for k in range(KC):
                    act.wait_ge(x_in[n * KC + k], 16)
                    nc.scalar.activation(xt_hi[:, k, X_PARTS[n]], x_raw[:, k, X_PARTS[n]], ACT.Copy)\
                        .then_inc(in_hi_done, 1)

            for n in range(2):
                hi_of_unit((n,), 1)
            for n in range(len(X_PARTS)):
                hi_of_x(n)
            for n in range(2, RING):
                hi_of_unit((n,), 1)

            def silu_v(jb, half, free):
                wait_job(act, jb[2])
                if free is not None:
                    act.wait_ge(pv_done, free)
                nc.scalar.activation(v_sb[:, 4 * half:4 * half + 4, :], bank_view(proj[jb[0]], 2 * P), ACT.Silu)\
                    .then_inc(evacuated[jb[0]], 1)

            def silu_head(dst, jb, free):
                wait_job(act, jb[2])
                if free is not None:
                    act.wait_ge(scores_done, free)
                nc.scalar.activation(dst[:, :], proj[jb[0]][:, :], ACT.Silu).then_inc(evacuated[jb[0]], 1)

            def tanh_gate(jb, free):
                wait_job(act, jb[2])
                if free is not None:
                    act.wait_ge(y_done, free)
                nc.scalar.activation(gate[:, :], proj[jb[0]][:, :], ACT.Tanh, scale=0.5)\
                    .then_inc(evacuated[jb[0]], 1)

            def square(h):
                act.wait_ge(pv_done, h + 1)
                act.wait_ge(sq_sum_done, h + 1)
                nc.scalar.activation(squares[:, :], ps_o[:, :], ACT.Square).then_inc(squares_done, 1)

            def y_hi_of(h, hd, before):
                act.wait_ge(y_done, h + 1)
                if before is not None:
                    wait_job(act, before)
                nc.scalar.activation(y_hi[:, hd, :], y_raw[:, :], ACT.Copy).then_inc(y_hi_done, 1)

            def back(i, last=False):
                jb = [job(J_LOOP_A, JOBS_PAIR, i, j) for j in range(4)]
                if not (isinstance(i, int) and i == 0):
                    act.wait_ge(scanned, i * 2)
                act.dma_start(scan[:, :], ffn_scan[bass.ds(i, 1), :, :].squeeze(0)).then_inc(scan_in, 16)
                silu_head(q_sb, jb[0], i * 2 + 1)
                pair_unit(i, 5)
                square(i * 2)
                silu_head(k_sb, jb[1], i * 2 + 1)
                pair_unit(i, 6)
                tanh_gate(jb[2], None if isinstance(i, int) and i == 0 else i * 2)
                pair_unit(i, 7)
                y_hi_of(i * 2, 0, at(J_LOOP_A, JOBS_PAIR, i, -1))
                tanh_gate(jb[3], i * 2 + 1)
                pair_unit(i, 8)
                if not last:
                    square(i * 2 + 1)
                    y_hi_of(i * 2 + 1, 1, None)
                    return
                act.wait_ge(sq_sum_done, HEADS)
                act.wait_ge(early_y_done, 1)
                nc.scalar.activation(y_hi[:, 1, half(0)], y_raw[:, half(0)], ACT.Copy).then_inc(early_y_hi_done, 1)
                nc.scalar.activation(squares[:, half(0)], ps_o[:, half(0)], ACT.Square)
                act.wait_ge(y_done, HEADS)
                nc.scalar.activation(y_hi[:, 1, half(1)], y_raw[:, half(1)], ACT.Copy).then_inc(y_hi_done, 1)
                nc.scalar.activation(squares[:, half(1)], ps_o[:, half(1)], ACT.Square).then_inc(squares_done, 1)

            act.wait_ge(tables_in, 32)
            nc.scalar.activation(table_hi[:, :, :], table[:, :, :], ACT.Copy).then_inc(table_hi_done, 1)
            act.wait_ge(in_lo_done, len(X_PARTS) * KC)
            silu_v(one_job(J_FRONT0), 0, None)
            silu_v(one_job(J_FRONT0 + 1), 1, None)
            pair_unit(0, 1)
            pair_unit(0, 2)
            silu_head(q_sb, one_job(J_FRONT0 + 2), None)
            pair_unit(0, 3)
            silu_head(k_sb, one_job(J_FRONT0 + 3), None)
            pair_unit(0, 4)
            for n, dst in enumerate((cos_t, sin_t)):
                s, _, m = one_job(J_TABLES + n)
                wait_job(act, m)
                nc.scalar.activation(dst[:, :], proj[s][:, :], ACT.Copy).then_inc(evacuated[s], 1)
            for k in range(KC):
                act.wait_ge(ctx_in[k], 16)
                nc.scalar.activation(ctx_hi[:, k, :], ctx_raw[:, k, :], ACT.Copy).then_inc(in_hi_done, 1)

            def pair(i):
                back(i)
                jb = [job(J_LOOP_A, JOBS_PAIR, i, j) for j in range(JOBS_PAIR)]
                silu_v(jb[4], 0, i * 2 + 2)
                silu_v(jb[5], 1, None)
                pair_unit(i, 9)
                pair_unit(i, 10)
                silu_head(q_sb, jb[6], i * 2 + 2)
                pair_unit(i, 11)
                silu_head(k_sb, jb[7], None)
                pair_unit(i, 12)
                wait_job(act, jb[11][2])
                pair_unit(i, 13)
                pair_unit(i, 14)

            pair(0)
            with act.Fori(1, PAIRS - 1) as i:
                pair(i)
            back(PAIRS - 1, True)

            def sqrt_var(n, cols):
                act.wait_ge(var_done, n + 1)
                nc.scalar.activation(std[:, cols], var_e[:, cols], ACT.Sqrt).then_inc(std_done, 1)

            sqrt_var(0, slice(0, BATCH))
            wait_all_out(act, J_OUTS_A)
            act.wait_ge(rms_done, 1)
            for c in range(4, BATCH):
                nc.scalar.activation(acc[:, c, :], acc[:, c, :], ACT.Copy, scale=rms_inv[:, c:c + 1])\
                    .then_inc(acc_scaled, 1)
            wait_job(act, J_K0 - 1)
            pair_unit(PAIRS - 1, 9)
            pair_unit(PAIRS - 1, 10)

            def normalise_batches(n, cols, batches):
                sqrt_var(n + 1, cols)
                act.wait_ge(shift_done, n + 1)
                for c in batches:
                    nc.scalar.activation(acc[:, c, :], acc[:, c, :], ACT.Identity, scale=rstd[:, c:c + 1],
                                         bias=shift[:, c:c + 1]).then_inc(normed_act, 1)

            def turned_hi(ln, c2):
                act.wait_ge(turned, 4 * ln + c2 + 1)
                for c in range(2):
                    tok = slice((2 * c2 + c) * P, (2 * c2 + c + 1) * P)
                    last = nc.scalar.activation(xt_hi[:, :, tok], turned_view((ps_s, ps_o)[c2 % 2], c), ACT.Copy)
                last.then_inc(turned_hi_done, 1)

            def copy_vt_first(f, jb, free):
                act.wait_ge(first_half, f + 1)
                if free is not None:
                    act.wait_ge(vt_turned, free)
                nc.scalar.activation(vt[:, half(0)], proj[jb[0]][:, half(0)], ACT.Copy)

            def copy_vt_second(jb):
                wait_job(act, jb[2])
                nc.scalar.activation(vt[:, half(1)], proj[jb[0]][:, half(1)], ACT.Copy).then_inc(evacuated[jb[0]], 1)

            def copy_v(i):
                act.wait_ge(vt_turned, i + 1)
                nc.scalar.activation(vx[:, :, :], bank_view(ps_o, P), ACT.Copy).then_inc(v_ready, 1)

            def swap_first(f, jb, free):
                act.wait_ge(first_half, f + 1)
                if free is not None:
                    act.wait_ge(sin_done, free)
                swap(jb, half(0))

            def swap_second(jb):
                wait_job(act, jb[2])
                swap(jb, half(1))

            def swap(jb, tok):
                nc.scalar.activation(swapped[0:64, tok], proj[jb[0]][64:128, tok], ACT.Copy)
                nc.scalar.activation(swapped[64:128, tok], proj[jb[0]][0:64, tok], ACT.Copy).then_inc(swap_done, 1)

            def exps(h):
                act.wait_ge(neg_max_done, h + 1)
                for b in range(BATCH):
                    last = nc.scalar.activation(pb[:, b, :], pb[:, b, :], ACT.Exp, bias=neg_max[:, b:b + 1],
                                                scale=SM_SCALE, accum_out=row_sum[:, b:b + 1])
                last.then_inc(exp_done, 1)

            def y_hi_cross(h, hd, before):
                act.wait_ge(pv_done, h + (HEADS + 1))
                if before is not None:
                    wait_job(act, before)
                nc.scalar.activation(y_hi[:, hd, :], ps_o[:, :], ACT.Copy).then_inc(y_hi_done, 1)

            def copy_pt(h, jb):
                wait_job(act, jb[2])
                act.wait_ge(pv_done, h + HEADS)
                nc.scalar.activation(pt[:, :, :], bank_view(proj[jb[0]], P), ACT.Copy)\
                    .then_inc(evacuated[jb[0]], 1)

            act.wait_ge(y_lo_done, HEADS)
            act.wait_ge(sq_sum_done, HEADS + 1)
            normalise_batches(0, four(0), (2, 3))
            swap_first(0, one_job(J_K0), None)
            swap_second(one_job(J_K0))
            turned_hi(0, 0)
            turned_hi(0, 1)
            normalise_batches(1, four(1), (6, 7))
            copy_vt_first(1, one_job(J_V0), None)
            copy_vt_second(one_job(J_V0))
            kv_unit(0, 0)
            kv_unit(0, 1)
            turned_hi(0, 2)
            turned_hi(0, 3)
            swap_first(2, one_job(J_Q0), 1)
            swap_second(one_job(J_Q0))
            kv_unit(0, 2)
            copy_v(0)
            act.preload_act_table(ACT.Exp)
            swap_first(3, one_job(J_Q1), 2)
            exps(0)
            swap_second(one_job(J_Q1))
            kv_unit(0, 3)
            copy_pt(0, one_job(J_T0))
            exps(1)
            swap_first(4, one_job(J_Q2), 3)
            swap_second(one_job(J_Q2))
            kv_unit(0, 4)
            y_hi_cross(0, 0, None)
            copy_pt(1, one_job(J_T1))

            def heads_2_3(i, last):
                g = i * GROUP
                r = at(R_LOOP_B, ROPES_KV, i, 0)
                jb = [job(J_LOOP_B, JOBS_KV, i, j) for j in range(9)]
                q3, kn, t2, q0, o3, t3 = (jb[0], None, jb[1], None, jb[6], jb[5]) if last else \
                    (jb[0], jb[1], jb[2], jb[3], jb[7], jb[8])
                f = at(H_LOOP_B, HALVED_KV, i, 0)
                swap_first(f, q3, r)
                exps(g + 2)
                swap_second(q3)
                if not last:
                    kv_unit(i, 5)
                y_hi_cross(g + 1, 1, None)
                if not last:
                    swap_first(f + 1, kn, r + 1)
                    swap_second(kn)
                    kv_unit(i, 6)
                copy_pt(g + 2, t2)
                if not last:
                    swap_first(f + 2, q0, r + 2)
                exps(g + 3)
                if not last:
                    swap_second(q0)
                    kv_unit(i, 7)
                if last:
                    copy_pt(g + 3, t3)
                y_hi_cross(g + 2, 0, o3[2])
                if not last:
                    kv_unit(i, 8)
                    kv_unit(i, 9)
                    copy_pt(g + 3, t3)

            with act.Fori(0, KV_HEADS - 1) as i:
                heads_2_3(i, False)
                g = i * GROUP
                r = at(R_LOOP_B, ROPES_KV, i, 3)
                jb = [job(J_LOOP_B, JOBS_KV, i, j) for j in range(JOBS_KV)]
                f = at(H_LOOP_B, HALVED_KV, i, 3)
                swap_first(f, jb[9], r)
                exps(g + 4)
                swap_second(jb[9])
                kv_unit(i, 10)
                y_hi_cross(g + 3, 1, None)
                copy_vt_first(f + 1, jb[10], i + 1)
                copy_vt_second(jb[10])
                kv_unit(i, 11)
                copy_pt(g + 4, jb[11])
                copy_v(i + 1)
                swap_first(f + 2, jb[12], r + 1)
                exps(g + 5)
                swap_second(jb[12])
                kv_unit(i, 12)
                y_hi_cross(g + 4, 0, jb[16][2])
                kv_unit(i, 13)
                kv_unit(i, 14)
                copy_pt(g + 5, jb[17])
            heads_2_3(KV_HEADS - 1, True)
            act.wait_ge(early_pv_done, 2)
            nc.scalar.activation(y_hi[:, 1, half(0)], ps_s[:, half(0)], ACT.Copy).then_inc(early_y_hi_done, 1)
            act.wait_ge(pv_done, 2 * HEADS)
            nc.scalar.activation(y_hi[:, 1, half(1)], ps_s[:, half(1)], ACT.Copy).then_inc(y_hi_done, 1)

            def ffn_floats(i, j):
                n = UF_LOOP + j
                s = n % RING_F
                act.wait_ge(rawf_in[s], i * 16 + 16 * (n // RING_F + 1))
                nc.scalar.activation(raw[:, s, :], raw[:, s, :].bitcast(INT32), ACT.Copy).then_inc(w_float_done, 1)

            def ffn_hi(i, j):
                n = UF_LOOP + j
                s = n % RING_F
                act.wait_ge(w_float_done, i * UNITS_F + (n + 1))
                nc.scalar.activation(w_hi[:, s, :], raw[:, s, :], ACT.Copy).then_inc(w_hi_done, 1)

            def ffn_unit(i, j):
                ffn_floats(i, j)
                ffn_hi(i, j)

            def silu_gate(jb, free):
                wait_job(act, jb[2])
                if free is not None:
                    wait_out_of_slot(act, free)
                nc.scalar.activation(g_act[:, :], proj[jb[0]][:, :], ACT.Silu, scale=scales[:, 0:1])\
                    .then_inc(evacuated[jb[0]], 1)

            def mid_hi(jb):
                wait_out_of_slot(act, jb)
                nc.scalar.activation(y_hi[:, 0, :], mid[:, :], ACT.Copy).then_inc(y_hi_done, 1)

            wait_job(act, J_TAIL_B - 1)
            act.wait_ge(small_in, 32)
            ffn_unit(0, -2)
            ffn_unit(0, -1)
            normalise_batches(2, four(0), (2, 3))
            turned_hi(1, 0)
            turned_hi(1, 1)
            normalise_batches(3, four(1), (6, 7))
            turned_hi(1, 2)
            turned_hi(1, 3)
            ffn_unit(0, 0)
            silu_gate(one_job(J_F0), None)
            ffn_unit(0, 1)
            mid_hi(one_job(J_F0 + 1))
            ffn_unit(0, 2)

            def chunk(i):
                jb = [job(J_LOOP_F, JOBS_F, i, j) for j in range(-2, JOBS_F)]
                up_before, gate_job, up_job, down_last = jb[0], jb[2], jb[4], jb[5]
                if isinstance(i, int) and i == 0:
                    up_before = one_job(J_F0 + 1)
                silu_gate(gate_job, up_before)
                ffn_unit(i, 3)
                wait_job(act, up_job[2])
                ffn_unit(i, 4)
                ffn_floats(i, 5)
                wait_job(act, down_last[2])
                ffn_hi(i, 5)
                mid_hi(up_job)

            chunk(0)
            with act.Fori(1, HCHUNKS - 2) as i:
                chunk(i)
            silu_gate(one_job(J_TAIL_F), job(J_LOOP_F, JOBS_F, HCHUNKS - 2, -2))
            ffn_unit(HCHUNKS - 2, 3)
            act.wait_ge(early_y_done, 2)
            nc.scalar.activation(y_hi[:, 1, half(0)], mid[:, half(0)], ACT.Copy).then_inc(early_y_hi_done, 1)
            wait_out_of_slot(act, one_job(J_TAIL_F + 1))
            nc.scalar.activation(y_hi[:, 1, half(1)], mid[:, half(1)], ACT.Copy).then_inc(y_hi_done, 1)
            normalise_batches(4, four(0), (2, 3))
            normalise_batches(5, four(1), (6, 7))

        @block.vector
        def _(dve):
            steps = [0]

            def link(ins):
                steps[0] += 1
                ins.then_inc(dve_step, 1)
                dve.wait_ge(dve_step, steps[0])

            for n, part in enumerate(X_PARTS):
                for k in range(KC):
                    dve.wait_ge(in_hi_done, n * KC + k + 1)
                    nc.vector.tensor_tensor(xt_lo[:, k, part], x_raw[:, k, part], xt_hi[:, k, part].bitcast(FP32),
                                            ALU.subtract).then_inc(in_lo_done, 1)
            dve.wait_ge(pos_in, 16)
            link(nc.vector.tensor_scalar(pos_wrap[:, :], pos_i[:, :], 0.0, float(POSITIONS), ALU.is_lt, ALU.mult))
            link(nc.vector.tensor_tensor(pos_f[:, :], pos_i[:, :], pos_wrap[:, :], ALU.add))
            link(nc.vector.tensor_scalar(pos_f[:, :], pos_f[:, :], 0.0, float(POSITIONS - 1), ALU.max, ALU.min))
            dve.wait_ge(tables_in, 32)
            for c in range(4):
                nc.vector.tensor_scalar(onehot[:, c, :], pos_f[:, :], iota[:, c:c + 1], None, ALU.is_equal)\
                    .then_inc(onehot_done, 1)
            dve.wait_ge(table_hi_done, 1)
            nc.vector.tensor_tensor(table_lo[:, :, :], table[:, :, :], table_hi[:, :, :].bitcast(FP32), ALU.subtract)\
                .then_inc(table_lo_done, 1)
            dve.wait_ge(mask_in, 16)
            link(nc.vector.tensor_scalar(mask_tmp[:, :, :], mask_i[:, :, :], 0.0, MASKED, ALU.is_equal, ALU.mult))
            link(nc.vector.tensor_scalar(cap[:, :, :], mask_i[:, :, :], 0.0, UNMASKED, ALU.not_equal, ALU.mult))
            link(nc.vector.tensor_tensor(cap[:, :, :], cap[:, :, :], mask_tmp[:, :, :], ALU.add))
            wait_job(dve, J_TABLES + 1)
            dve.wait_ge(decay_in, 16)
            dve.wait_ge(small_in, 32)

            def decayed(h, free):
                dve.wait_ge(scores_done, h + 1)
                if free is not None:
                    dve.wait_ge(pv_done, free)
                nc.vector.tensor_tensor(probs[:, :, :], bank_view(ps_s, P),
                                        decay_sb[:, bass.ds(h, 1), :].broadcast_to([P, BATCH, P]),
                                        ALU.mult).then_inc(probs_done, 1)

            def finish_gate(jb):
                wait_out_of_slot(dve, jb)
                nc.vector.tensor_scalar(gate[:, :], gate[:, :], 0.5, 0.5, ALU.mult, ALU.add).then_inc(gate_done, 1)

            def gated(h, free):
                dve.wait_ge(squares_done, h + 1)
                dve.wait_ge(gate_done, h + 1)
                if free is not None:
                    dve.wait_ge(y_lo_done, free)
                nc.vector.scalar_tensor_tensor(out=y_raw[:, :], in0=ps_o[:, :], scalar=nw[:, bass.ds(h, 1)],
                                               in1=gate[:, :], op0=ALU.mult, op1=ALU.mult).then_inc(y_done, 1)

            def y_lo_of(h, hd):
                dve.wait_ge(y_hi_done, h + 1)
                nc.vector.tensor_tensor(y_lo[:, hd, :], y_raw[:, :], y_hi[:, hd, :].bitcast(FP32), ALU.subtract)\
                    .then_inc(y_lo_done, 1)

            def add_out(c, jb):
                wait_job(dve, jb[2])
                nc.vector.tensor_tensor(acc[:, 2 * c:2 * c + 2, :], acc[:, 2 * c:2 * c + 2, :],
                                        bank_view(proj[jb[0]], DIM), ALU.add).then_inc(evacuated[jb[0]], 1)

            def back(i, last=False):
                free = None if isinstance(i, int) and i == 0 else i * 2
                decayed(i * 2, free)
                dve.wait_ge(scan_in, i * 16 + 16)
                for n, op in enumerate((ALU.max, ALU.min)):
                    nc.vector.tensor_reduce(extremes[:, n, bass.ds(i, 1)], scan[:, :], AX.X, op).then_inc(scanned, 1)
                finish_gate(job(J_LOOP_A, JOBS_PAIR, i, 2))
                decayed(i * 2 + 1, i * 2 + 1)
                gated(i * 2, free)
                y_lo_of(i * 2, 0)
                finish_gate(job(J_LOOP_A, JOBS_PAIR, i, 3))
                if not last:
                    gated(i * 2 + 1, i * 2 + 1)
                    y_lo_of(i * 2 + 1, 1)
                    return
                dve.wait_ge(gate_done, HEADS)
                dve.wait_ge(y_lo_done, HEADS - 1)
                for h, there, done in ((0, early_pv_done, early_y_done), (1, pv_done, y_done)):
                    dve.wait_ge(there, HEADS if h else 1)
                    nc.vector.scalar_tensor_tensor(out=y_raw[:, half(h)], in0=ps_o[:, half(h)],
                                                   scalar=nw[:, HEADS - 1:HEADS], in1=gate[:, half(h)],
                                                   op0=ALU.mult, op1=ALU.mult).then_inc(done, 1)
                for h, there, done in ((0, early_y_hi_done, early_y_lo_done), (1, y_hi_done, y_lo_done)):
                    dve.wait_ge(there, HEADS if h else 1)
                    nc.vector.tensor_tensor(y_lo[:, 1, half(h)], y_raw[:, half(h)],
                                            y_hi[:, 1, half(h)].bitcast(FP32), ALU.subtract).then_inc(done, 1)

            back(0)
            for k in range(KC):
                dve.wait_ge(in_hi_done, len(X_PARTS) * KC + k + 1)
                nc.vector.tensor_tensor(ctx_lo[:, k, :], ctx_raw[:, k, :], ctx_hi[:, k, :].bitcast(FP32), ALU.subtract)\
                    .then_inc(in_lo_done, 1)
            dve.wait_ge(in_lo_done, (len(X_PARTS) + 1) * KC)
            nc.vector.memset(acc[:, :, :], 0.0).then_inc(acc_zeroed, 1)
            dve.wait_ge(acc_zeroed, 1)
            for c in range(4):
                add_out(c, one_job(J_LOOP_A + 8 + c))
            with dve.Fori(1, PAIRS - 1) as i:
                back(i)
                for c in range(4):
                    add_out(c, job(J_LOOP_A, JOBS_PAIR, i, 8 + c))
            back(PAIRS - 1, True)

            def rsqrt(dst, cols, n):
                dve.wait_ge(std_done, n + 1)
                link(nc.vector.reciprocal(dst[:, cols], std[:, cols]))
                link(nc.vector.tensor_tensor(newton[:, cols], dst[:, cols], dst[:, cols], ALU.mult))
                link(nc.vector.tensor_tensor(newton[:, cols], newton[:, cols], var_e[:, cols], ALU.mult))
                link(nc.vector.tensor_scalar(newton[:, cols], newton[:, cols], -0.5, 1.5, ALU.mult, ALU.add))
                return nc.vector.tensor_tensor(dst[:, cols], dst[:, cols], newton[:, cols], ALU.mult)

            def ln_stats(batches, jb=None):
                if jb is not None:
                    wait_out_of_slot(dve, jb)
                for c in batches:
                    last = nc.vector.bn_stats(stats[:, c, :], acc[:, c, :])
                link(last)

            def normalise_batches(n, mine, cols):
                for c in range(cols.start, cols.stop):
                    last = nc.vector.bn_aggr(mean_var[:, c, :], stats[:, c, :])
                link(last)
                nc.vector.tensor_scalar(var_e[:, cols], mean_var[:, cols, 1], LN_EPS, None, ALU.add)\
                    .then_inc(var_done, 1)
                link(rsqrt(rstd, cols, n + 1))
                nc.vector.scalar_tensor_tensor(out=shift[:, cols], in0=mean_var[:, cols, 0], scalar=-1.0,
                                               in1=rstd[:, cols], op0=ALU.mult, op1=ALU.mult).then_inc(shift_done, 1)
                for c in mine:
                    nc.vector.tensor_scalar(acc[:, c, :], acc[:, c, :], mean_var[:, c, 0:1], rstd[:, c:c + 1],
                                            ALU.subtract, ALU.mult).then_inc(normed_dve, 1)

            def turned_lo(ln, c2):
                dve.wait_ge(turned_hi_done, 4 * ln + c2 + 1)
                for c in range(2):
                    tok = slice((2 * c2 + c) * P, (2 * c2 + c + 1) * P)
                    last = nc.vector.tensor_tensor(xt_lo[:, :, tok], turned_view((ps_s, ps_o)[c2 % 2], c),
                                                   xt_hi[:, :, tok].bitcast(FP32), ALU.subtract)
                last.then_inc(turned_taken, 1)

            def residual(c2, jb):
                wait_out_of_slot(dve, jb)
                dve.wait_ge(res_in[c2], 16)
                for c in (2 * c2, 2 * c2 + 1):
                    last = nc.vector.scalar_tensor_tensor(out=acc[:, c, :], in0=acc[:, c, :],
                                                          scalar=rms_inv[:, c:c + 1], in1=x_res[:, c, :],
                                                          op0=ALU.mult, op1=ALU.add)
                link(last)

            def add_scaled(c2, jb):
                wait_job(dve, jb[2])
                dve.wait_ge(residual_added, 2 * c2 - 2)
                for n in range(2):
                    c = 2 * c2 + n
                    last = nc.vector.scalar_tensor_tensor(out=acc[:, c, :],
                                                          in0=proj[jb[0]][:, n * DIM:(n + 1) * DIM],
                                                          scalar=rms_inv[:, c:c + 1], in1=acc[:, c, :],
                                                          op0=ALU.mult, op1=ALU.add)
                last.then_inc(evacuated[jb[0]], 1)

            dve.wait_ge(scanned, 2 * PAIRS)
            nc.vector.tensor_reduce(widest[:, 0:1], extremes[:, 0, :], AX.X, ALU.max)
            link(nc.vector.tensor_reduce(widest[:, 1:2], extremes[:, 1, :], AX.X, ALU.min))
            link(nc.vector.scalar_tensor_tensor(out=widest[:, 2:3], in0=widest[:, 1:2], scalar=-1.0,
                                                in1=widest[:, 0:1], op0=ALU.mult, op1=ALU.max))
            nc.vector.tensor_scalar(wide[:, :], widest[:, 2:3], EXACT, None, ALU.is_gt).then_inc(wide_done, 1)
            outs = [one_job(J_OUTS_A + c) for c in range(4)]
            add_out(0, outs[0])
            dve.wait_ge(ms_done, 1)
            nc.vector.tensor_scalar(var_e[:, :], ps_o[:, 0:BATCH], 1.0 / (HEADS * P), RMS_EPS, ALU.mult, ALU.add)\
                .then_inc(var_done, 1)
            nc.vector.tensor_copy(wide_parts[:, :], ps_o[0:1, BATCH:BATCH + 1]).then_inc(wide_known, 1)
            rsqrt(rms_inv, slice(0, BATCH), 0).then_inc(rms_done, 1)
            dve.wait_ge(rms_done, 1)
            add_out(1, outs[1])
            residual(0, outs[0])
            ln_stats((0, 1))
            residual(1, outs[1])
            add_scaled(2, outs[2])
            ln_stats((2, 3))
            normalise_batches(0, (0, 1), four(0))
            add_scaled(3, outs[3])
            ln_stats((4, 5), outs[2])
            ln_stats((6, 7), outs[3])
            normalise_batches(1, (4, 5), four(1))

            def rope_part(r, jb, h):
                dve.wait_ge(swap_done, r * 2 + (h + 1))
                if h == 0 and not (isinstance(r, int) and r == 0):
                    dve.wait_ge(rope_done, r)
                ins = nc.vector.tensor_tensor(cosed[:, half(h)], proj[jb[0]][:, half(h)], cos_t[:, half(h)], ALU.mult)
                if h == 1:
                    ins.then_inc(evacuated[jb[0]], 1)
                ins = nc.vector.tensor_tensor(rot[:, half(h)], swapped[:, half(h)], sin_t[:, half(h)], ALU.mult)
                if h == 1:
                    ins.then_inc(sin_done, 1)

            def rope_sum(r, dst, free):
                dve.wait_ge(sin_done, r + 1)
                dve.wait_ge(scores_done, free)
                nc.vector.tensor_tensor(dst[:, :], cosed[:, :], rot[:, :], ALU.add).then_inc(rope_done, 1)

            def cap_and_max(h, t_before):
                dve.wait_ge(scores_done, h + (HEADS + 1))
                if t_before is not None:
                    wait_job(dve, t_before)
                nc.vector.tensor_tensor(pb[:, :, :], bank_view(ps_s, P), cap[:, :, :], ALU.min).then_inc(masked, 1)
                dve.wait_ge(masked, h + 1)
                nc.vector.tensor_reduce(row_max[:, :], pb[:, :, :], AX.X, ALU.max).then_inc(max_done, 1)
                dve.wait_ge(max_done, h + 1)
                nc.vector.tensor_scalar(neg_max[:, :], row_max[:, :], -SM_SCALE, None, ALU.mult)\
                    .then_inc(neg_max_done, 1)

            def normalise(h):
                dve.wait_ge(exp_done, h + 1)
                nc.vector.reciprocal(row_inv[:, :], row_sum[:, :]).then_inc(inv_done, 1)
                dve.wait_ge(inv_done, h + 1)
                nc.vector.tensor_tensor(pb[:, :, :], pb[:, :, :],
                                        row_inv[:, :].unsqueeze(2).broadcast_to([P, BATCH, P]),
                                        ALU.mult).then_inc(soft_done, 1)

            def y_lo_cross(h, hd):
                dve.wait_ge(y_hi_done, h + (HEADS + 1))
                nc.vector.tensor_tensor(y_lo[:, hd, :], ps_o[:, :], y_hi[:, hd, :].bitcast(FP32), ALU.subtract)\
                    .then_inc(y_lo_done, 1)

            dve.wait_ge(pv_done, HEADS)
            dve.wait_ge(y_done, HEADS)
            turned_lo(0, 0)
            turned_lo(0, 1)
            rope_part(0, one_job(J_K0), 0)
            rope_part(0, one_job(J_K0), 1)
            turned_lo(0, 2)
            turned_lo(0, 3)
            rope_sum(0, kr, HEADS)
            rope_part(1, one_job(J_Q0), 0)
            rope_part(1, one_job(J_Q0), 1)
            rope_sum(1, qr, HEADS)
            cap_and_max(0, None)
            rope_part(2, one_job(J_Q1), 0)
            normalise(0)
            rope_part(2, one_job(J_Q1), 1)
            rope_sum(2, qr, HEADS + 1)
            cap_and_max(1, J_T0)
            normalise(1)
            rope_part(3, one_job(J_Q2), 0)
            rope_part(3, one_job(J_Q2), 1)
            rope_sum(3, qr, HEADS + 2)
            y_lo_cross(0, 0)

            def heads_2_3(i, last):
                g = i * GROUP
                r = at(R_LOOP_B, ROPES_KV, i, 0)
                jb = [job(J_LOOP_B, JOBS_KV, i, j) for j in range(-1, 9)]
                t1, q3, kn, t2, q0, outs = (jb[0], jb[1], None, jb[2], None, jb[3:6] + jb[7:8]) if last else \
                    (jb[0], jb[1], jb[2], jb[3], jb[4], jb[5:9])
                cap_and_max(g + 2, t1[2])
                rope_part(r, q3, 0)
                normalise(g + 2)
                rope_part(r, q3, 1)
                rope_sum(r, qr, g + (HEADS + 3))
                y_lo_cross(g + 1, 1)
                if not last:
                    rope_part(r + 1, kn, 0)
                    rope_part(r + 1, kn, 1)
                cap_and_max(g + 3, t2[2])
                if not last:
                    rope_sum(r + 1, kr, g + (HEADS + 4))
                    rope_part(r + 2, q0, 0)
                else:
                    add_out(0, outs[0])
                normalise(g + 3)
                if not last:
                    rope_part(r + 2, q0, 1)
                    rope_sum(r + 2, qr, g + (HEADS + 4))
                for c in range(1 if last else 0, 4):
                    add_out(c, outs[c])
                y_lo_cross(g + 2, 0)

            with dve.Fori(0, KV_HEADS - 1) as i:
                heads_2_3(i, False)
                g = i * GROUP
                r = at(R_LOOP_B, ROPES_KV, i, 3)
                jb = [job(J_LOOP_B, JOBS_KV, i, j) for j in range(JOBS_KV)]
                cap_and_max(g + 4, jb[8][2])
                rope_part(r, jb[9], 0)
                normalise(g + 4)
                rope_part(r, jb[9], 1)
                rope_sum(r, qr, g + (HEADS + 5))
                y_lo_cross(g + 3, 1)
                cap_and_max(g + 5, jb[11][2])
                rope_part(r + 1, jb[12], 0)
                normalise(g + 5)
                rope_part(r + 1, jb[12], 1)
                rope_sum(r + 1, qr, g + (HEADS + 6))
                for c in range(4):
                    add_out(c, jb[13 + c])
                y_lo_cross(g + 4, 0)
            heads_2_3(KV_HEADS - 1, True)
            for h, there, done in ((0, early_y_hi_done, early_y_lo_done), (1, y_hi_done, y_lo_done)):
                dve.wait_ge(there, 2 * HEADS if h else 2)
                nc.vector.tensor_tensor(y_lo[:, 1, half(h)], ps_s[:, half(h)], y_hi[:, 1, half(h)].bitcast(FP32),
                                        ALU.subtract).then_inc(done, 1)
            outs = [one_job(J_TAIL_B + c) for c in range(4)]
            for c in range(4):
                add_out(c, outs[c])
                if c < 2:
                    ln_stats((2 * c, 2 * c + 1), outs[c])
                if c == 1:
                    normalise_batches(2, (0, 1), four(0))
            turned_lo(1, 0)
            turned_lo(1, 1)
            ln_stats((4, 5), outs[2])
            ln_stats((6, 7), outs[3])
            normalise_batches(3, (4, 5), four(1))
            turned_lo(1, 2)
            turned_lo(1, 3)
            dve.wait_ge(normed_act, 4 * 2)

            def scaled_by(n, dst, product, other, op):
                return nc.vector.scalar_tensor_tensor(out=dst, in0=product, scalar=scales[:, n:n + 1], in1=other,
                                                      op0=ALU.mult, op1=op)

            def add_product(c, product):
                sums = acc[:, 2 * c:2 * c + 2, :]
                return scaled_by(2, sums, bank_view(product, DIM), sums, ALU.add)

            def add_down(c, jb):
                wait_job(dve, jb[2])
                add_product(c, proj[jb[0]]).then_inc(evacuated[jb[0]], 1)

            def gate_up(c, gate_job, up_job):
                wait_out_of_slot(dve, gate_job)
                wait_job(dve, up_job[2])
                dve.wait_ge(y_lo_done, c + 2 * HEADS)
                scaled_by(1, mid[:, :], proj[up_job[0]][:, :], g_act[:, :], ALU.mult)\
                    .then_inc(evacuated[up_job[0]], 1)

            def mid_lo(c):
                dve.wait_ge(y_hi_done, c + (2 * HEADS + 1))
                nc.vector.tensor_tensor(y_lo[:, 0, :], mid[:, :], y_hi[:, 0, :].bitcast(FP32), ALU.subtract)\
                    .then_inc(y_lo_done, 1)

            gate_up(0, one_job(J_F0), one_job(J_F0 + 1))
            mid_lo(0)
            with dve.Fori(0, HCHUNKS - 2) as i:
                jb = [job(J_LOOP_F, JOBS_F, i, j) for j in range(JOBS_F)]
                add_down(2, jb[1])
                gate_up(i + 1, jb[0], jb[2])
                add_down(3, jb[3])
                mid_lo(i + 1)
            gate_job, up_job = one_job(J_TAIL_F), one_job(J_TAIL_F + 1)
            wait_out_of_slot(dve, gate_job)
            dve.wait_ge(y_lo_done, 2 * HEADS + HCHUNKS - 1)
            dve.wait_ge(first_half, HALVED_JOBS)
            scaled_by(1, mid[:, half(0)], proj[up_job[0]][:, half(0)], g_act[:, half(0)], ALU.mult)\
                .then_inc(early_y_done, 1)
            dve.wait_ge(early_y_hi_done, 3)
            nc.vector.tensor_tensor(y_lo[:, 1, half(0)], mid[:, half(0)], y_hi[:, 1, half(0)].bitcast(FP32),
                                    ALU.subtract).then_inc(early_y_lo_done, 1)
            wait_job(dve, up_job[2])
            scaled_by(1, mid[:, half(1)], proj[up_job[0]][:, half(1)], g_act[:, half(1)], ALU.mult)\
                .then_inc(evacuated[up_job[0]], 1)
            dve.wait_ge(y_hi_done, 2 * HEADS + HCHUNKS)
            nc.vector.tensor_tensor(y_lo[:, 1, half(1)], mid[:, half(1)], y_hi[:, 1, half(1)].bitcast(FP32),
                                    ALU.subtract).then_inc(y_lo_done, 1)
            outs = [one_job(J_OUTS_F + n) for n in range(3)]

            def add_last(n, c):
                wait_job(dve, outs[n][2])
                scaled_by(2, acc[:, c, :], proj[outs[n][0]][:, 0:DIM], acc[:, c, :], ALU.add)\
                    .then_inc(evacuated[outs[n][0]], 1)

            dve.wait_ge(sums_done, 1)
            link(add_product(0, ps_s))
            ln_stats((0, 1))
            dve.wait_ge(sums_done, 2)
            link(add_product(1, ps_o))
            add_down(2, outs[0])
            ln_stats((2, 3))
            normalise_batches(4, (0, 1), four(0))
            add_last(1, 6)
            add_last(2, 7)
            ln_stats((4, 5), outs[0])
            ln_stats((6,), outs[1])
            ln_stats((7,), outs[2])
            normalise_batches(5, (4, 5), four(1))

        @block.tensor
        def _(pe):
            def split_product(ps, stationary, moving, k, count, lo_of=(True, True)):
                (s_hi, s_lo), (m_hi, m_lo) = stationary, moving
                passes = [(s_hi, m_hi)] + ([(s_hi, m_lo)] if lo_of[1] else []) + ([(s_lo, m_hi)] if lo_of[0] else [])
                for n, (left, right) in enumerate(passes):
                    last = nc.tensor.matmul(ps, left, right, start=(k == 0 and n == 0),
                                            stop=(k == count - 1 and n == len(passes) - 1))
                return last

            def begin(jb, unit):
                if not (isinstance(jb[1], int) and jb[1] == 0):
                    pe.wait_ge(evacuated[jb[0]], jb[1])
                if unit is not None:
                    pe.wait_ge(w_lo_done, unit + 1)

            def channels_part(jb, slot, x_hi, x_lo, tok, w_has_lo=True):
                for k in range(KC):
                    cols = slice(k * P, (k + 1) * P)
                    last = split_product(proj[jb[0]][:, tok], (w_hi[:, slot, cols], w_lo[:, slot, cols]),
                                         (x_hi[:, k, tok], x_lo[:, k, tok]), k, KC, (w_has_lo, True))
                return last

            def channels_half(jb, slot, x_hi, x_lo, h, w_has_lo=True):
                return channels_part(jb, slot, x_hi, x_lo, half(h), w_has_lo)

            def channels(jb, unit, slot, x_hi, x_lo, halved=False, w_has_lo=True):
                begin(jb, unit)
                last = channels_half(jb, slot, x_hi, x_lo, 0, w_has_lo)
                if halved:
                    last.then_inc(first_half, 1)
                channels_half(jb, slot, x_hi, x_lo, 1, w_has_lo).then_inc(jobs_done, 1)

            def values(jb, unit, slots, part, first=False):
                begin(jb, unit)
                for b in range(4):
                    if first and b in ((0, 2), (0,))[part]:
                        pe.wait_ge(in_lo_done, (2 * part + b // 2 + 1) * KC)
                    tok = slice((4 * part + b) * P, (4 * part + b + 1) * P)
                    for k in range(KC):
                        cols = slice(k % 2 * 2 * P, (k % 2 + 1) * 2 * P)
                        s = slots[k // 2]
                        last = split_product(proj[jb[0]][:, b * 2 * P:(b + 1) * 2 * P],
                                             (xt_hi[:, k, tok], xt_lo[:, k, tok]),
                                             (w_hi[:, s, cols], w_lo[:, s, cols]), k, KC)
                last.then_inc(jobs_done, 1)

            def output_batch(ps, batch, slots, before, count, w_has_lo=True):
                tok = slice(batch * P, (batch + 1) * P)
                for hd, s in enumerate(slots):
                    last = split_product(ps, (y_hi[:, hd, tok], y_lo[:, hd, tok]), (w_hi[:, s, :], w_lo[:, s, :]),
                                         before + hd, count, (True, w_has_lo))
                return last

            def output(jb, c, unit, slots, heads_ready, early=None, batches=None, w_has_lo=True):
                begin(jb, unit)
                if heads_ready is not None:
                    pe.wait_ge(y_lo_done, heads_ready)
                if early is not None:
                    pe.wait_ge(early_y_lo_done, early)
                for b, batch in enumerate(batches or (2 * c, 2 * c + 1)):
                    last = output_batch(proj[jb[0]][:, b * DIM:(b + 1) * DIM], batch, slots, 0, len(slots), w_has_lo)
                last.then_inc(jobs_done, 1)

            def slot_a(j):
                return (U_LOOP_A + j) % RING

            def front(unit, jobs, slots, first=False):
                values(jobs[0], unit + 1, slots[0:2], 0, first)
                values(jobs[1], None, slots[0:2], 1, first)
                channels(jobs[2], unit + 2, slots[2], xt_hi, xt_lo)
                channels(jobs[3], unit + 3, slots[3], xt_hi, xt_lo)

            def scores(h, q_job, k_job, free):
                wait_out_of_slot(pe, q_job)
                wait_out_of_slot(pe, k_job)
                if free is not None:
                    pe.wait_ge(probs_done, free)
                for b in range(BATCH):
                    tok = slice(b * P, (b + 1) * P)
                    last = nc.tensor.matmul(ps_s[:, tok], k_sb[:, tok], q_sb[:, tok], start=True, stop=True)
                last.then_inc(scores_done, 1)

            def times_v(h, hd, free, early=False):
                pe.wait_ge(probs_done, h + 1)
                if free is not None:
                    pe.wait_ge(y_done, free)
                for b in range(BATCH):
                    last = nc.tensor.matmul(ps_o[:, b * P:(b + 1) * P], v_sb[:, b, hd * P:(hd + 1) * P],
                                            probs[:, b, :], start=True, stop=True)
                    if early and b == 3:
                        last.then_inc(early_pv_done, 1)
                last.then_inc(pv_done, 1)

            def back(i, first, last=False):
                jb = [job(J_LOOP_A, JOBS_PAIR, i, j) for j in range(4)]
                u = at(U_LOOP_A, UNITS_PAIR, i, 0)
                v_a, v_b, q_a, k_a = [one_job(J_FRONT0 + j) for j in range(4)] if first else \
                    [job(J_LOOP_A, JOBS_PAIR, i, j) for j in (-8, -7, -6, -5)]
                scores(i * 2, q_a, k_a, None if first else i * 2)
                channels(jb[0], u, slot_a(0), xt_hi, xt_lo)
                wait_out_of_slot(pe, v_a)
                wait_out_of_slot(pe, v_b)
                times_v(i * 2, 0, None if first else i * 2)
                channels(jb[1], u + 1, slot_a(1), xt_hi, xt_lo)
                channels(jb[2], u + 2, slot_a(2), xt_hi, xt_lo)
                scores(i * 2 + 1, jb[0], jb[1], i * 2 + 1)
                channels(jb[3], u + 3, slot_a(3), xt_hi, xt_lo)
                times_v(i * 2 + 1, 1, i * 2 + 1, last)

            def next_front_and_out(i):
                jb = [job(J_LOOP_A, JOBS_PAIR, i, j) for j in range(JOBS_PAIR)]
                u = at(U_LOOP_A, UNITS_PAIR, i, 0)
                front(u + 4, jb[4:8], [slot_a(j) for j in range(4, 8)])
                for c in range(4):
                    output(jb[8 + c], c, u + 9, [slot_a(8), slot_a(9)], i * 2 + 2)

            front(U_FRONT0, [one_job(J_FRONT0 + j) for j in range(4)], [0, 1, 2, 3], True)
            pe.wait_ge(table_lo_done, 1)
            pe.wait_ge(onehot_done, 4)
            for t in range(2):
                jb = one_job(J_TABLES + t)
                begin(jb, None)
                for h in range(2):
                    for c in range(4):
                        cols = slice(t * P, (t + 1) * P)
                        nc.tensor.matmul(proj[jb[0]][:, half(h)], table_hi[:, c, cols], onehot[:, c, half(h)],
                                         start=(c == 0), stop=False)
                        last = nc.tensor.matmul(proj[jb[0]][:, half(h)], table_lo[:, c, cols],
                                                onehot[:, c, half(h)], start=False, stop=(c == 3))
                last.then_inc(jobs_done, 1)
            back(0, True)
            next_front_and_out(0)
            with pe.Fori(1, PAIRS - 1) as i:
                back(i, False)
                next_front_and_out(i)
            back(PAIRS - 1, False, True)
            out_slots = [slot_a(4), slot_a(5)]
            output(one_job(J_OUTS_A), 0, U_B - 1, out_slots, HEADS - 1, early=1)
            pe.wait_ge(sq_sum_done, HEADS + 1)
            pe.wait_ge(y_done, HEADS)
            for b in range(BATCH):
                nc.tensor.matmul(ps_o[:, b:b + 1], sq_sum[:, b * P:(b + 1) * P], ones, start=True, stop=True)
            pe.wait_ge(wide_done, 1)
            nc.tensor.matmul(ps_o[0:1, BATCH:BATCH + 1], wide[:, :], ones, start=True, stop=True).then_inc(ms_done, 1)
            output(one_job(J_OUTS_A + 1), 1, None, out_slots, None)
            output(one_job(J_OUTS_A + 2), 2, None, out_slots, HEADS)
            output(one_job(J_OUTS_A + 3), 3, None, out_slots, None)

            def turn(ln, c2):
                wait_normed(pe, ln, c2)
                if c2 >= 2:
                    pe.wait_ge(turned_taken, 4 * ln + c2 - 1)
                for c in range(2):
                    for k in range(KC):
                        last = nc.tensor.transpose(turned_view((ps_s, ps_o)[c2 % 2], c)[:, k, :],
                                                   acc[:, 2 * c2 + c, k * P:(k + 1) * P], ident)
                last.then_inc(turned, 1)

            def cross_scores(h, r_q):
                pe.wait_ge(rope_done, r_q + 1)
                if not (isinstance(h, int) and h == 0):
                    pe.wait_ge(masked, h)
                for b in range(BATCH):
                    tok = slice(b * P, (b + 1) * P)
                    last = nc.tensor.matmul(ps_s[:, tok], qr[:, tok], kr[:, tok], start=True, stop=True)
                last.then_inc(scores_done, 1)

            def turn_probs(h, jb):
                begin(jb, None)
                pe.wait_ge(soft_done, h + 1)
                for b in range(BATCH):
                    last = nc.tensor.transpose(proj[jb[0]][:, b * P:(b + 1) * P], pb[:, b, :], ident)
                last.then_inc(jobs_done, 1)

            def times_vx(h, t_job, free):
                wait_out_of_slot(pe, t_job)
                pe.wait_ge(y_lo_done, free)
                for b in range(BATCH):
                    last = nc.tensor.matmul(ps_o[:, b * P:(b + 1) * P], vx[:, b, :], pt[:, b, :],
                                            start=True, stop=True)
                last.then_inc(pv_done, 1)

            def turn_v(i, jb):
                wait_out_of_slot(pe, jb)
                pe.wait_ge(y_lo_done, i * GROUP + HEADS)
                for b in range(BATCH):
                    last = nc.tensor.transpose(ps_o[:, b * P:(b + 1) * P], vt[:, b * P:(b + 1) * P], ident)
                last.then_inc(vt_turned, 1)

            pe.wait_ge(in_lo_done, (len(X_PARTS) + 1) * KC)
            channels(one_job(J_K0), U_B, U_B % RING, ctx_hi, ctx_lo, True)
            pe.wait_ge(rms_done, 1)
            turn(0, 0)
            turn(0, 1)
            channels(one_job(J_V0), U_B + 1, (U_B + 1) % RING, ctx_hi, ctx_lo, True)
            turn(0, 2)
            turn(0, 3)
            begin(one_job(J_Q0), U_B + 2)
            pe.wait_ge(turned_taken, 2)
            channels_half(one_job(J_Q0), (U_B + 2) % RING, xt_hi, xt_lo, 0).then_inc(first_half, 1)
            pe.wait_ge(turned_taken, 4)
            channels_half(one_job(J_Q0), (U_B + 2) % RING, xt_hi, xt_lo, 1).then_inc(jobs_done, 1)
            turn_v(0, one_job(J_V0))
            cross_scores(0, 1)
            channels(one_job(J_Q1), U_B + 3, (U_B + 3) % RING, xt_hi, xt_lo, True)
            turn_probs(0, one_job(J_T0))
            cross_scores(1, 2)
            channels(one_job(J_Q2), U_B + 4, (U_B + 4) % RING, xt_hi, xt_lo, True)
            pe.wait_ge(v_ready, 1)
            times_vx(0, one_job(J_T0), HEADS)
            turn_probs(1, one_job(J_T1))

            def slot_b(j):
                return (U_LOOP_B + j) % RING

            def heads_2_3(i, last):
                g = i * GROUP
                r = at(R_LOOP_B, ROPES_KV, i, 0)
                u = at(U_LOOP_B, UNITS_KV, i, 0)
                jb = [job(J_LOOP_B, JOBS_KV, i, j) for j in range(-1, 9)]
                t1, q3, kn, t2, q0, outs, t3 = (jb[0], jb[1], None, jb[2], None, jb[3:6] + jb[7:8], jb[6]) \
                    if last else \
                    (jb[0], jb[1], jb[2], jb[3], jb[4], jb[5:9], jb[9])
                o = 1 if last else 3
                cross_scores(g + 2, r - 1)
                channels(q3, u, slot_b(0), xt_hi, xt_lo, True)
                times_vx(g + 1, t1, g + (HEADS + 1))
                if not last:
                    channels(kn, u + 1, slot_b(1), ctx_hi, ctx_lo, True)
                turn_probs(g + 2, t2)
                cross_scores(g + 3, r)
                if not last:
                    channels(q0, u + 2, slot_b(2), xt_hi, xt_lo, True)
                output(outs[0], 0, u + (o + 1), [slot_b(o), slot_b(o + 1)], g + (HEADS + 2))
                times_vx(g + 2, t2, g + (HEADS + 2))
                for c in range(1, 4):
                    if last and c == 3:
                        turn_probs(g + 3, t3)
                    output(outs[c], c, None, [slot_b(o), slot_b(o + 1)], None)
                if not last:
                    turn_probs(g + 3, t3)

            with pe.Fori(0, KV_HEADS - 1) as i:
                heads_2_3(i, False)
                g = i * GROUP
                r = at(R_LOOP_B, ROPES_KV, i, 0)
                u = at(U_LOOP_B, UNITS_KV, i, 0)
                jb = [job(J_LOOP_B, JOBS_KV, i, j) for j in range(JOBS_KV)]
                cross_scores(g + 4, r + 2)
                channels(jb[9], u + 5, slot_b(5), xt_hi, xt_lo, True)
                times_vx(g + 3, jb[8], g + (HEADS + 3))
                channels(jb[10], u + 6, slot_b(6), ctx_hi, ctx_lo, True)
                turn_probs(g + 4, jb[11])
                turn_v(i + 1, jb[10])
                cross_scores(g + 5, r + 3)
                channels(jb[12], u + 7, slot_b(7), xt_hi, xt_lo, True)
                output(jb[13], 0, u + 9, [slot_b(8), slot_b(9)], g + (HEADS + 4))
                pe.wait_ge(v_ready, i + 2)
                times_vx(g + 4, jb[11], g + (HEADS + 4))
                for c in range(1, 4):
                    output(jb[13 + c], c, None, [slot_b(8), slot_b(9)], None)
                turn_probs(g + 5, jb[17])
            heads_2_3(KV_HEADS - 1, True)
            wait_out_of_slot(pe, one_job(J_TAIL_B - 2))
            pe.wait_ge(masked, HEADS)
            for b in range(BATCH):
                last = nc.tensor.matmul(ps_s[:, b * P:(b + 1) * P], vx[:, b, :], pt[:, b, :], start=True, stop=True)
                if b == 3:
                    last.then_inc(early_pv_done, 1)
            last.then_inc(pv_done, 1)
            for c in range(4):
                output(one_job(J_TAIL_B + c), c, U_F - 1, [slot_b(3), slot_b(4)],
                       2 * HEADS - 1 if c < 2 else 2 * HEADS, early=2)

            turn(1, 0)
            turn(1, 1)

            def slot_f(j):
                return (UF_LOOP + j) % RING_F

            def feed_forward(w_has_lo):
                gate_up = [one_job(J_F0), one_job(J_F0 + 1)]
                for c2 in range(4):
                    if c2 == 2:
                        turn(1, 2)
                        turn(1, 3)
                    pe.wait_ge(turned_taken, 4 + c2 + 1)
                    for n in range(2):
                        if c2 == 0:
                            begin(gate_up[n], U_F + n)
                        last = channels_part(gate_up[n], n, xt_hi, xt_lo, slice(2 * c2 * P, (2 * c2 + 2) * P), w_has_lo)
                        if c2 == 3:
                            last.then_inc(jobs_done, 1)

                def sum_down(c2, slots, before):
                    for b in range(2):
                        last = output_batch((ps_s, ps_o)[c2][:, b * DIM:(b + 1) * DIM], 2 * c2 + b, slots, before,
                                            HCHUNKS, w_has_lo)
                    return last

                def chunk(i, before):
                    jb = [job(J_LOOP_F, JOBS_F, i, j) for j in range(JOBS_F)]
                    u = at(U_F + UF_LOOP, UNITS_F, i, 0)
                    channels(jb[0], u, slot_f(0), xt_hi, xt_lo, w_has_lo=w_has_lo)
                    pe.wait_ge(w_lo_done, u + 3)
                    pe.wait_ge(y_lo_done, i + (2 * HEADS + 1))
                    sum_down(0, [slot_f(2)], before)
                    output(jb[1], 2, None, [slot_f(2)], None, w_has_lo=w_has_lo)
                    channels(jb[2], None, slot_f(1), xt_hi, xt_lo, w_has_lo=w_has_lo)
                    sum_down(1, [slot_f(2)], before)
                    output(jb[3], 3, None, [slot_f(2)], None, w_has_lo=w_has_lo)

                chunk(0, 0)
                with pe.Fori(1, HCHUNKS - 2) as i:
                    chunk(i, 1)
                u = U_F + UF_TOTAL
                channels(one_job(J_TAIL_F), u - 4, (UF_TOTAL - 4) % RING_F, xt_hi, xt_lo, w_has_lo=w_has_lo)
                channels(one_job(J_TAIL_F + 1), u - 3, (UF_TOTAL - 3) % RING_F, xt_hi, xt_lo, True, w_has_lo)
                down_slots = [(UF_TOTAL - 2) % RING_F, (UF_TOTAL - 1) % RING_F]
                pe.wait_ge(w_lo_done, u)
                pe.wait_ge(y_lo_done, 2 * HEADS + HCHUNKS - 1)
                pe.wait_ge(early_y_lo_done, 3)
                for c2 in range(2):
                    sum_down(c2, down_slots, HCHUNKS - 2).then_inc(sums_done, 1)
                for n, batches in enumerate(((4, 5), (6,), (7,))):
                    output(one_job(J_OUTS_F + n), None, None, down_slots, 2 * HEADS + HCHUNKS, batches=batches,
                           w_has_lo=w_has_lo)

            pe.wait_ge(wide_known, 1)
            wide_count = pe.value_load(wide_parts[0:1, 0:1])
            with pe.If(wide_count == 0):
                feed_forward(False)
            with pe.If(wide_count != 0):
                feed_forward(True)


def _decay_table():
    layer, layers = 1, 32
    base = 1.0 / 2.0 ** (8.0 / HEADS)
    slope = base ** (np.arange(HEADS, dtype=np.float32) + 1.0) * (1.0 - layer / (layers - 1 + 1e-05) + 1e-05)
    diff = np.arange(P)[None, :] - np.arange(P)[:, None]
    table = np.exp(-slope.astype(np.float64)[None, :, None] * np.maximum(diff, 0)[:, None, :])
    return (table * (diff >= 0)[:, None, :]).astype(np.float32)


def _rope_table():
    inv = (1.0 / ROPE_THETA ** (np.arange(0, P, 2, dtype=np.float32) / np.float32(P))).astype(np.float32)
    freqs = np.arange(POSITIONS, dtype=np.float32)[:, None] * inv[None, :]
    cos, sin = np.cos(freqs), np.sin(freqs)
    table = np.concatenate([cos, cos, -sin, sin], axis=1).astype(np.float32)
    return np.ascontiguousarray(table.reshape(4, P, 2 * P).transpose(1, 0, 2))


def _consts():
    iota = np.arange(POSITIONS, dtype=np.float32).reshape(4, P).T
    return np.concatenate([np.eye(P, dtype=np.float32), iota, np.ones((P, 1), np.float32)], axis=1)


def _in_rows(w):
    return w.reshape(KC, P, -1).transpose(1, 0, 2)


def _weight_stream(qkv_w, gate_w, out_w, wq, wk, wv, wo):
    qkv = qkv_w.reshape(HEADS, 3, P, DIM)

    def head(w):
        return _in_rows(w).reshape(P, DIM)

    units = []

    def front(i):
        v = _in_rows(qkv[2 * i:2 * i + 2, 2].reshape(2 * P, DIM).T)
        units.extend([v[:, 0:2].reshape(P, DIM), v[:, 2:4].reshape(P, DIM)])
        units.extend([head(qkv[2 * i, 0].T), head(qkv[2 * i, 1].T)])

    def back(i):
        units.extend([head(qkv[2 * i + 1, 0].T), head(qkv[2 * i + 1, 1].T)])
        units.extend(head(gate_w[h * P:(h + 1) * P].T) for h in (2 * i, 2 * i + 1))

    def out(i):
        units.extend(out_w[:, h * P:(h + 1) * P].T for h in (2 * i, 2 * i + 1))

    front(0)
    for i in range(PAIRS):
        back(i)
        if i + 1 < PAIRS:
            front(i + 1)
        out(i)

    def of(w, h):
        return head(w[:, h * P:(h + 1) * P])

    def rows(h):
        return [wo[n * P:(n + 1) * P] for n in (h, h + 1)]

    units += [of(wk, 0), of(wv, 0), of(wq, 0), of(wq, 1), of(wq, 2)]
    for i in range(KV_HEADS):
        g, more = GROUP * i, i + 1 < KV_HEADS
        units += [of(wq, g + 3)] + ([of(wk, i + 1), of(wq, g + 4)] if more else []) + rows(g)
        units += [of(wq, g + 5), of(wv, i + 1), of(wq, g + 6)] if more else []
        units += rows(g + 2)
    return np.stack(units)


def _ffn_stream(w_gate, w_up, w_down):
    pad = HCHUNKS * P - HIDDEN
    gate, up = (np.pad(w, ((0, pad), (0, 0))) for w in (w_gate, w_up))
    down = np.pad(w_down, ((0, 0), (0, pad)))
    units = []

    def cols(w, c):
        return _in_rows(w[c * P:(c + 1) * P].T).reshape(P, DIM)

    for c in range(HCHUNKS):
        units += [cols(gate, c), cols(up, c)]
        if c:
            units.append(down[:, (c - 1) * P:c * P].T)
    units.append(down[:, -P:].T)
    return np.stack(units)


def kernel(**inputs):
    import concourse.bacc as bacc
    from concourse.bass_utils import run_bass_kernel_spmd

    a = {k: np.asarray(v) for k, v in inputs.items()}
    x, ctx = a["x"], a["ctx_4096"]
    ffn = _ffn_stream(a["L0_ffn_w_gate"], a["L0_ffn_w_up"], a["L0_ffn_w_down"])
    arrays = {
        "x_t": _in_rows(x.reshape(TOK, DIM).T),
        "x_rows": x.transpose(1, 0, 2),
        "ctx_t": _in_rows(ctx.reshape(TOK, DIM).T),
        "pos": a["pos_BxS2"].reshape(TOK),
        "mask": a["mask_BxSxS2_ik0"].transpose(1, 0, 2),
        "weights": _weight_stream(a["L0_attn_qkv_w"], a["L0_attn_gate_w"], a["L0_attn_out_w"], a["L0_xattn_Wq"],
                                  a["L0_xattn_Wk"], a["L0_xattn_Wv"], a["L0_xattn_Wo"]),
        "ffn_weights": ffn,
        "ffn_scan": ffn.reshape(PAIRS, P, SCAN),
        "ffn_scales": np.tile(np.stack([a["L0_ffn_scale_gate"], a["L0_ffn_scale_up"], a["L0_ffn_scale_down"]])
                              .reshape(1, 3), (P, 1)),
        "norm_w": a["L0_attn_norm_w"].reshape(HEADS, P).T,
        "decay": _decay_table(),
        "rope_table": _rope_table(),
        "consts": _consts(),
    }
    arrays = {k: np.ascontiguousarray(v) for k, v in arrays.items()}
    nc = bacc.Bacc("TRN2", target_bir_lowering=False, num_devices=1)
    args = [nc.dram_tensor(k, v.shape, mybir.dt.from_np(v.dtype), kind="ExternalInput").ap()
            for k, v in arrays.items()]
    out = nc.dram_tensor("out", [BATCH, SEQ, DIM], FP32, kind="ExternalOutput").ap()
    build(nc, *args, out)
    r = run_bass_kernel_spmd(nc, [arrays], core_ids=[0])
    return r.results[0]["out"]
```
